# Optimizing a Trainium2 kernel written in Bass

```python
import numpy as np
import jax
import jax.numpy as jnp

def _softmax(x, axis=-1):
    return jax.nn.softmax(x, axis=axis)

def _gelu(x):
    return jax.nn.gelu(x, approximate=True)

def _silu(x):
    return jax.nn.silu(x)

def _sigmoid(x):
    return jax.nn.sigmoid(x)

def _layernorm(x, axis=-1, eps=1e-05):
    m = jnp.mean(x, axis=axis, keepdims=True)
    v = jnp.var(x, axis=axis, keepdims=True)
    return (x - m) / jnp.sqrt(v + eps)

def _scatter_add(tgt, idx, src, axis=0):
    return tgt.at[idx].add(src)

def _segment_sum(src, seg, n):
    return jax.ops.segment_sum(src, seg, n)
kernel_name = 'mk_gps_d1_gnn_r8_062d9b'

def setup_inputs(seed: int=0):
    np.random.seed(seed)
    _w = jnp.asarray

    def _rec_inputs():
        import jax
        import jax.numpy as jnp
        _gk = jax.random.key(seed)
        x = -0.0002928 + 1 * jax.random.normal(jax.random.fold_in(_gk, 1), (1250, 512), jnp.float32)
        _s = jax.random.randint(jax.random.fold_in(_gk, 2), (20000,), 0, 1250, jnp.int32)
        _d = jax.random.randint(jax.random.fold_in(_gk, 3), (20000,), 0, 1250, jnp.int32)
        _loop = jnp.arange(1250, dtype=jnp.int32)
        src = jnp.concatenate([_s, _d, _loop])
        dst = jnp.concatenate([_d, _s, _loop])
        _o = jnp.argsort(dst, stable=True)
        src = src[_o]
        dst = dst[_o]
        return (x, src, dst)
    x, src, dst = _rec_inputs()

    def _L0_gnn_setup():
        import jax, jax.numpy as jnp
        import numpy as np
        N, IN_DIM, OUT_DIM, H = (1024, 512, 512, 4)
        E = 16384
        HC = H * OUT_DIM
        key = jax.random.key(seed)
        ks = jax.random.split(key, 12)
        s = 1.0 / np.sqrt(IN_DIM)
        return {'x': jax.random.normal(ks[0], (N, IN_DIM), dtype=jnp.float32), 'edge_index': jax.random.randint(ks[1], (2, E), 0, N, dtype=jnp.int64), 'Wq': jax.random.normal(ks[2], (IN_DIM, HC), dtype=jnp.float32) * s, 'bq': jnp.zeros((HC,), dtype=jnp.float32), 'Wk': jax.random.normal(ks[3], (IN_DIM, HC), dtype=jnp.float32) * s, 'bk': jnp.zeros((HC,), dtype=jnp.float32), 'Wv': jax.random.normal(ks[4], (IN_DIM, HC), dtype=jnp.float32) * s, 'bv': jnp.zeros((HC,), dtype=jnp.float32), 'Wskip': jax.random.normal(ks[5], (IN_DIM, HC), dtype=jnp.float32) * s, 'bskip': jnp.zeros((HC,), dtype=jnp.float32), 'Wlin': jax.random.normal(ks[6], (HC, OUT_DIM), dtype=jnp.float32) / np.sqrt(HC), 'blin': jnp.zeros((OUT_DIM,), dtype=jnp.float32), 'gamma': jnp.ones((OUT_DIM,), dtype=jnp.float32), 'beta': jnp.zeros((OUT_DIM,), dtype=jnp.float32)}
    _L0_gnn_all = _L0_gnn_setup()
    _L0_gnn_in = {k: v for k, v in _L0_gnn_all.items() if k in ('Wq', 'bq', 'Wk', 'bk', 'Wv', 'bv', 'Wskip', 'bskip', 'Wlin', 'blin', 'gamma', 'beta')}
    del _L0_gnn_all

    def _L0_mix_setup():
        import jax, jax.numpy as jnp
        import numpy as np
        HEADS = 8
        DIM_HEAD = 64
        EPS = 1e-05

        def layer_norm(x, gamma):
            mu = jnp.mean(x, axis=-1, keepdims=True)
            var = jnp.var(x, axis=-1, keepdims=True)
            return (x - mu) * jax.lax.rsqrt(var + EPS) * gamma
        key = jax.random.key(seed)
        k1, k2, k3 = jax.random.split(key, 3)
        b, n, dim = (4, 2048, 512)
        hidden = HEADS * DIM_HEAD
        x = jax.random.normal(k1, (b, n, dim), dtype=jnp.float32)
        norm_gamma = jnp.ones((dim,), dtype=jnp.float32)
        w_qkv = jax.random.normal(k2, (hidden * 3, dim), dtype=jnp.float32) * dim ** (-0.5)
        w_out = jax.random.normal(k3, (dim, hidden), dtype=jnp.float32) * hidden ** (-0.5)
        out_gamma = jnp.ones((dim,), dtype=jnp.float32)
        return {'x': x, 'norm_gamma': norm_gamma, 'w_qkv': w_qkv, 'w_out': w_out, 'out_gamma': out_gamma}
    _L0_mix_all = _L0_mix_setup()
    _L0_mix_in = {k: v for k, v in _L0_mix_all.items() if k in ('norm_gamma', 'w_qkv', 'w_out', 'out_gamma')}
    del _L0_mix_all

    def _L0_ffn_setup():
        import jax, jax.numpy as jnp
        import numpy as np
        CAPACITY_FACTOR = 1.25
        TOP_K = 2

        def _moe(x, Wg, W1, b1, W2, b2):
            B, T, D = x.shape
            N = Wg.shape[1]
            K = TOP_K
            BT = B * T
            BTK = BT * K
            C = int(np.ceil(CAPACITY_FACTOR * BTK / N))
            x_flat = x.reshape(BT, D)
            probs = jax.nn.softmax(x_flat @ Wg, axis=-1)
            vals, idx = jax.lax.top_k(probs, K)
            vals = vals / jnp.clip(vals.sum(-1, keepdims=True), 1e-09)
            a = idx.reshape(BTK)
            oh = jax.nn.one_hot(a, N, dtype=jnp.int32)
            rank = jnp.cumsum(oh, axis=0) - oh
            pos = jnp.take_along_axis(rank, a[:, None], axis=1)[:, 0]
            keep = pos < C
            dest = jnp.where(keep, a * C + pos, N * C)
            token = jnp.arange(BTK) // K
            buf = jnp.zeros((N * C, D), x.dtype).at[dest].set(x_flat[token], mode='drop')
            buf = buf.reshape(N, C, D)
            h = jax.nn.relu(jnp.einsum('ncd,ndh->nch', buf, W1) + b1[:, None, :])
            o = (jnp.einsum('nch,nhd->ncd', h, W2) + b2[:, None, :]).reshape(N * C, D)
            gathered = o[jnp.minimum(dest, N * C - 1)]
            w = vals.reshape(BTK) * keep.astype(x.dtype)
            y_flat = jax.ops.segment_sum(gathered * w[:, None], token, num_segments=BT)
            contrib = jax.ops.segment_sum(w, token, num_segments=BT)
            y_flat = jnp.where(contrib[:, None] <= 1e-12, x_flat, y_flat)
            return y_flat.reshape(B, T, D)
        key = jax.random.key(seed)
        ks = jax.random.split(key, 4)
        B, T, D, H, N = (8, 1024, 512, 512, 32)
        x = jax.random.normal(ks[0], (B, T, D), jnp.float32)
        Wg = jax.random.normal(ks[1], (D, N), jnp.float32) * 0.02
        W1 = jax.random.normal(ks[2], (N, D, H), jnp.float32) * 0.02
        b1 = jnp.zeros((N, H), jnp.float32)
        W2 = jax.random.normal(ks[3], (N, H, D), jnp.float32) * 0.02
        b2 = jnp.zeros((N, D), jnp.float32)
        return {'x': x, 'Wg': Wg, 'W1': W1, 'b1': b1, 'W2': W2, 'b2': b2}
    _L0_ffn_all = _L0_ffn_setup()
    _L0_ffn_in = {k: v for k, v in _L0_ffn_all.items() if k in ('Wg', 'W1', 'b1', 'W2', 'b2')}
    del _L0_ffn_all
    return {'x': x, 'src': src, 'dst': dst, 'L0_gnn_Wq': _L0_gnn_in['Wq'], 'L0_gnn_bq': _L0_gnn_in['bq'], 'L0_gnn_Wk': _L0_gnn_in['Wk'], 'L0_gnn_bk': _L0_gnn_in['bk'], 'L0_gnn_Wv': _L0_gnn_in['Wv'], 'L0_gnn_bv': _L0_gnn_in['bv'], 'L0_gnn_Wskip': _L0_gnn_in['Wskip'], 'L0_gnn_bskip': _L0_gnn_in['bskip'], 'L0_gnn_Wlin': _L0_gnn_in['Wlin'], 'L0_gnn_blin': _L0_gnn_in['blin'], 'L0_gnn_gamma': _L0_gnn_in['gamma'], 'L0_gnn_beta': _L0_gnn_in['beta'], 'L0_mix_norm_gamma': _L0_mix_in['norm_gamma'], 'L0_mix_w_qkv': _L0_mix_in['w_qkv'], 'L0_mix_w_out': _L0_mix_in['w_out'], 'L0_mix_out_gamma': _L0_mix_in['out_gamma'], 'L0_ffn_Wg': _L0_ffn_in['Wg'], 'L0_ffn_W1': _L0_ffn_in['W1'], 'L0_ffn_b1': _L0_ffn_in['b1'], 'L0_ffn_W2': _L0_ffn_in['W2'], 'L0_ffn_b2': _L0_ffn_in['b2']}

def reference(x, src, dst, L0_gnn_Wq, L0_gnn_bq, L0_gnn_Wk, L0_gnn_bk, L0_gnn_Wv, L0_gnn_bv, L0_gnn_Wskip, L0_gnn_bskip, L0_gnn_Wlin, L0_gnn_blin, L0_gnn_gamma, L0_gnn_beta, L0_mix_norm_gamma, L0_mix_w_qkv, L0_mix_w_out, L0_mix_out_gamma, L0_ffn_Wg, L0_ffn_W1, L0_ffn_b1, L0_ffn_W2, L0_ffn_b2):
    import jax
    import jax.numpy as jnp

    def _L0_gnn_ref(x, edge_index, Wq, bq, Wk, bk, Wv, bv, Wskip, bskip, Wlin, blin, gamma, beta):
        import jax, jax.numpy as jnp
        import numpy as np
        N, IN_DIM, OUT_DIM, H = (1024, 512, 512, 4)
        E = 16384
        HC = H * OUT_DIM
        n = x.shape[0]
        src, dst = (edge_index[0], edge_index[1])
        q = (x @ Wq + bq).reshape(n, H, OUT_DIM)
        k = (x @ Wk + bk).reshape(n, H, OUT_DIM)
        v = (x @ Wv + bv).reshape(n, H, OUT_DIM)
        alpha = jnp.einsum('ehc,ehc->eh', q[dst], k[src]) / np.sqrt(OUT_DIM)
        amax = jax.ops.segment_max(alpha, dst, num_segments=n)
        ex = jnp.exp(alpha - amax[dst])
        denom = jax.ops.segment_sum(ex, dst, num_segments=n)
        attn = ex / denom[dst]
        msg = attn[:, :, None] * v[src]
        agg = jax.ops.segment_sum(msg, dst, num_segments=n).reshape(n, HC)
        x_attn = agg + x @ Wskip + bskip
        x_lin = x_attn @ Wlin + blin
        h = x_lin + x_attn[:, :OUT_DIM]
        mu = jnp.mean(h, axis=-1, keepdims=True)
        var = jnp.mean((h - mu) ** 2, axis=-1, keepdims=True)
        return gamma * (h - mu) / jnp.sqrt(var + 1e-05) + beta

    def _L0_mix_ref(x, norm_gamma, w_qkv, w_out, out_gamma):
        import jax, jax.numpy as jnp
        import numpy as np
        HEADS = 8
        DIM_HEAD = 64
        EPS = 1e-05

        def layer_norm(x, gamma):
            mu = jnp.mean(x, axis=-1, keepdims=True)
            var = jnp.var(x, axis=-1, keepdims=True)
            return (x - mu) * jax.lax.rsqrt(var + EPS) * gamma
        b, n, dim = x.shape
        h, d = (HEADS, DIM_HEAD)
        scale = d ** (-0.5)
        x = layer_norm(x, norm_gamma)
        qkv = jnp.einsum('bnc,fc->bnf', x, w_qkv)
        q, k, v = jnp.split(qkv, 3, axis=-1)
        to_bhnd = lambda t: t.reshape(b, n, h, d).transpose(0, 2, 1, 3)
        q, k, v = (to_bhnd(q), to_bhnd(k), to_bhnd(v))
        q = jax.nn.softmax(q, axis=-1) * scale
        k = jax.nn.softmax(k, axis=-2)
        context = jnp.einsum('bhnd,bhne->bhde', k, v)
        out = jnp.einsum('bhde,bhnd->bhne', context, q)
        out = out.transpose(0, 2, 1, 3).reshape(b, n, h * d)
        out = jnp.einsum('bnf,cf->bnc', out, w_out)
        return layer_norm(out, out_gamma)

    def _L0_ffn_ref(x, Wg, W1, b1, W2, b2):
        import jax, jax.numpy as jnp
        import numpy as np
        CAPACITY_FACTOR = 1.25
        TOP_K = 2

        def _moe(x, Wg, W1, b1, W2, b2):
            B, T, D = x.shape
            N = Wg.shape[1]
            K = TOP_K
            BT = B * T
            BTK = BT * K
            C = int(np.ceil(CAPACITY_FACTOR * BTK / N))
            x_flat = x.reshape(BT, D)
            probs = jax.nn.softmax(x_flat @ Wg, axis=-1)
            vals, idx = jax.lax.top_k(probs, K)
            vals = vals / jnp.clip(vals.sum(-1, keepdims=True), 1e-09)
            a = idx.reshape(BTK)
            oh = jax.nn.one_hot(a, N, dtype=jnp.int32)
            rank = jnp.cumsum(oh, axis=0) - oh
            pos = jnp.take_along_axis(rank, a[:, None], axis=1)[:, 0]
            keep = pos < C
            dest = jnp.where(keep, a * C + pos, N * C)
            token = jnp.arange(BTK) // K
            buf = jnp.zeros((N * C, D), x.dtype).at[dest].set(x_flat[token], mode='drop')
            buf = buf.reshape(N, C, D)
            h = jax.nn.relu(jnp.einsum('ncd,ndh->nch', buf, W1) + b1[:, None, :])
            o = (jnp.einsum('nch,nhd->ncd', h, W2) + b2[:, None, :]).reshape(N * C, D)
            gathered = o[jnp.minimum(dest, N * C - 1)]
            w = vals.reshape(BTK) * keep.astype(x.dtype)
            y_flat = jax.ops.segment_sum(gathered * w[:, None], token, num_segments=BT)
            contrib = jax.ops.segment_sum(w, token, num_segments=BT)
            y_flat = jnp.where(contrib[:, None] <= 1e-12, x_flat, y_flat)
            return y_flat.reshape(B, T, D)
        return _moe(x, Wg, W1, b1, W2, b2)
    edge_index = jnp.stack([src, dst])
    xn = _layernorm(x, axis=-1)
    x = x + _L0_gnn_ref(xn, edge_index, L0_gnn_Wq, L0_gnn_bq, L0_gnn_Wk, L0_gnn_bk, L0_gnn_Wv, L0_gnn_bv, L0_gnn_Wskip, L0_gnn_bskip, L0_gnn_Wlin, L0_gnn_blin, L0_gnn_gamma, L0_gnn_beta) + _L0_mix_ref(xn[None], L0_mix_norm_gamma, L0_mix_w_qkv, L0_mix_w_out, L0_mix_out_gamma)[0]
    x = x + _L0_ffn_ref(_layernorm(x, axis=-1)[None], L0_ffn_Wg, L0_ffn_W1, L0_ffn_b1, L0_ffn_W2, L0_ffn_b2)[0]
    return x

_drawn_inputs = setup_inputs


def setup_inputs(seed=0):
    import zlib

    import numpy as np

    out = dict(_drawn_inputs(seed))
    spreads = {'L0_gnn_bq': (0.0, 0.337),
     'L0_gnn_bk': (0.0, 0.8),
     'L0_gnn_bv': (0.0, 0.1),
     'L0_gnn_bskip': (0.0, 0.1),
     'L0_gnn_blin': (0.0, 0.1),
     'L0_gnn_gamma': (1.0, 0.2),
     'L0_gnn_beta': (0.0, 0.1),
     'L0_mix_norm_gamma': (1.0, 0.2),
     'L0_mix_out_gamma': (1.0, 0.2),
     'L0_ffn_b1': (0.0, 0.689),
     'L0_ffn_b2': (0.0, 0.1)}
    factors = {}
    for name, (base, spread) in spreads.items():
        noise = np.random.default_rng([zlib.crc32(name.encode()), seed]).standard_normal(out[name].shape)
        drawn = base * np.exp(spread * noise) if base else spread * noise
        out[name] = jnp.asarray(drawn.astype(out[name].dtype))
    for name, factor in factors.items():
        out[name] = (out[name] * factor).astype(out[name].dtype)
    return out
```

```python
from contextlib import ExitStack

import numpy as np

import concourse.bass as bass
from concourse import mybir

F32 = mybir.dt.float32
F32R = mybir.dt.float32r
F16 = mybir.dt.float16
BF16 = mybir.dt.bfloat16
I32 = mybir.dt.int32
U32 = mybir.dt.uint32
U16 = mybir.dt.uint16
ALU = mybir.AluOpType
ACT = mybir.ActivationFunctionType
AX = mybir.AxisListType

P = 128
N = 1250
TOK = 125
NT = N // TOK
D = 512
DC = D // P
HEADS = 4
BW = 418
NB = 3
NS = BW * NB
GRP = 2 * TOK
NG = N // GRP
EDGES = 41250
EB = 375
NEB = EDGES // EB
SUB = EB // TOK
EPS = 1e-5
FAR = 1.0e30
MIX_HEADS, MIX_DIM = 8, 64
EXPERTS = 32
CAP = 98
SLOTS = EXPERTS * CAP
TOPK = 2


class Buffers:

    used = []

    def __init__(self, nc, ctx):
        self.nc, self.ctx = nc, ctx

    def sb(self, name, shape, dt=F32):
        return self.ctx.enter_context(self.nc.sbuf_tensor(name, shape, dt))

    def ps(self, name, shape, dt=F32):
        return self.ctx.enter_context(self.nc.psum_tensor(name, shape, dt))

    def sem(self, name):
        self.used.append(self.nc.alloc_semaphore(name))
        return self.used[-1]

    @classmethod
    def reset(cls, nc):
        nc.clear_and_free_semaphores(list(cls.used))
        cls.used.clear()
        nc.all_engine_barrier()


def chain(engine, sem):
    done = [0]

    def link(ins):
        done[0] += 1
        ins.then_inc(sem, 1)
        engine.wait_ge(sem, done[0])

    return link


def tile_parts(g):
    return range(4 * g, min(4 * g + 4, NT))


def node_stats(dve, link, source, stats, mean_var, root_in):
    for t in range(NT):
        ins = dve.bn_stats(stats[:, t, :], source[:, t, :])
    link(ins)
    for t in range(NT):
        ins = dve.bn_aggr(mean_var[:, t, :], stats[:, t, :])
    link(ins)
    return dve.tensor_scalar(root_in[:, :], mean_var[:, :, 1], EPS, None, ALU.add)


def inverse_root(dve, link, root_in, root, scratch, rstd):
    link(dve.reciprocal(rstd, root))
    link(dve.tensor_tensor(scratch, rstd, rstd, ALU.mult))
    link(dve.tensor_tensor(scratch, scratch, root_in, ALU.mult))
    link(dve.tensor_scalar(scratch, scratch, -0.5, 1.5, ALU.mult, ALU.add))
    link(dve.tensor_tensor(rstd, rstd, scratch, ALU.mult))


def stage_norm(nc, x, ident, xnT_hi, xnT_lo, xrow):
    with ExitStack() as ctx:
        b = Buffers(nc, ctx)
        stats = b.sb("n_stats", [TOK, NT, 6])
        mean_var = b.sb("n_mean_var", [TOK, NT, 2])
        root_in = b.sb("n_root_in", [TOK, NT])
        root = b.sb("n_root", [TOK, NT])
        scratch = b.sb("n_scratch", [TOK, NT])
        rstd = b.sb("n_rstd", [TOK, NT])
        bank = [b.ps(f"n_bank{i}", [P, 512]) for i in range(4)]
        x_loaded = b.sem("n_x_loaded")
        dve_step = b.sem("n_dve_step")
        ident_ready = b.sem("n_ident_ready")
        var_ready = b.sem("n_var_ready")
        root_ready = b.sem("n_root_ready")
        row_ready = b.sem("n_row_ready")
        turned = b.sem("n_turned")
        hi_ready = b.sem("n_hi_ready")
        lo_ready = b.sem("n_lo_ready")
        block = ctx.enter_context(nc.Block())
        units = [(g, c) for g in range(3) for c in range(DC)]

        @block.sync
        def _(sp):
            view = x.rearrange("(t p) c -> p t c", p=TOK)
            for t in range(NT):
                sp.dma_start(xrow[:, t, :], view[:, t, :]).then_inc(x_loaded, 16)

        @block.gpsimd
        def _(pool):
            pool.memset(ident[:, :], 0.0).then_inc(ident_ready, 1)
            pool.wait_ge(ident_ready, 1)
            pool.affine_select(out=ident[:, :], in_=ident[:, :], compare_op=ALU.not_equal, fill=1.0,
                               base=0, pattern=[[-1, P]], channel_multiplier=1).then_inc(ident_ready, 1)
            pool.memset(xnT_hi[:, :, N:NS].bitcast(F32), 0.0)
            pool.memset(xnT_lo[:, :, N:NS].bitcast(F32), 0.0)

        @block.vector
        def _(dve):
            link = chain(dve, dve_step)
            dve.wait_ge(x_loaded, 16 * NT)
            node_stats(dve, link, xrow, stats, mean_var, root_in).then_inc(var_ready, 1)
            dve.wait_ge(root_ready, 1)
            inverse_root(dve, link, root_in[:, :], root[:, :], scratch[:, :], rstd[:, :])
            for t in range(NT):
                dve.tensor_scalar(xrow[:, t, :], xrow[:, t, :], mean_var[:, t, 0:1], rstd[:, t:t + 1],
                                  ALU.subtract, ALU.mult).then_inc(row_ready, 1)
            for u, (g, c) in enumerate(units):
                n = TOK * len(tile_parts(g))
                cols = slice(500 * g, 500 * g + n)
                dve.wait_ge(hi_ready, u + 1)
                dve.tensor_tensor(xnT_lo[:, c, cols], bank[u % 4][:, 0:n], xnT_hi[:, c, cols].bitcast(F32),
                                  ALU.subtract).then_inc(lo_ready, 1)

        @block.scalar
        def _(act):
            act.wait_ge(var_ready, 1)
            act.activation(root[:, :], root_in[:, :], ACT.Sqrt).then_inc(root_ready, 1)
            for u, (g, c) in enumerate(units):
                n = TOK * len(tile_parts(g))
                act.wait_ge(turned, u + 1)
                act.activation(xnT_hi[:, c, 500 * g:500 * g + n], bank[u % 4][:, 0:n],
                               ACT.Copy).then_inc(hi_ready, 1)

        @block.tensor
        def _(pe):
            pe.wait_ge(ident_ready, 2)
            for u, (g, c) in enumerate(units):
                if u >= 4:
                    pe.wait_ge(lo_ready, u - 3)
                pe.wait_ge(row_ready, tile_parts(g)[-1] + 1)
                for i, t in enumerate(tile_parts(g)):
                    ins = pe.transpose(bank[u % 4][:, TOK * i:TOK * (i + 1)], xrow[:, t, P * c:P * (c + 1)],
                                       ident[0:TOK, 0:TOK])
                ins.then_inc(turned, 1)


def stage_count(nc, src, dst, ident, counts):
    with ExitStack() as ctx:
        b = Buffers(nc, ctx)
        edge_in = b.sb("c_edge_in", [NEB, 2, EB], I32)
        edge_row = b.sb("c_edge_row", [NEB, 2, EB])
        edge_col = b.sb("c_edge_col", [TOK, 2, SUB, NEB])
        reach = b.sb("c_reach", [NEB, 2])
        block_no = b.sb("c_block_no", [NT, NEB])
        tile_lo = b.sb("c_tile_lo", [NT, 2])
        over = b.sb("c_over", [NT, 2, NEB])
        at = b.sb("c_at", [NT, 2, NEB])
        span = b.sb("c_span", [NT, 2])
        span_int = b.sb("c_span_int", [NT, 2], I32)
        span_row = b.sb("c_span_row", [1, 2 * NT], I32)
        node_no = b.sb("c_node_no", [TOK, NS], F16)
        src_hot = b.sb("c_src_hot", [TOK, SUB, NS], BF16)
        dst_hot = b.sb("c_dst_hot", [TOK, SUB, TOK], BF16)
        zeros = b.sb("c_zeros", [TOK, 512], BF16)
        count_out = b.sb("c_count_out", [TOK, NS], U16)
        turn_bank = [b.ps(f"c_turn{i}", [P, 512]) for i in range(2)]
        reach_bank = b.ps("c_reach_bank", [P, 512])
        acc = b.ps("c_acc", [P, NB, 512])
        edges_loaded = b.sem("c_edges_loaded")
        iota_ready = b.sem("c_iota_ready")
        dve_step = b.sem("c_dve_step")
        rows_ready = b.sem("c_rows_ready")
        turned = b.sem("c_turned")
        cols_ready = b.sem("c_cols_ready")
        reach_ready = b.sem("c_reach_ready")
        reach_spread = b.sem("c_reach_spread")
        span_ready = b.sem("c_span_ready")
        span_loaded = b.sem("c_span_loaded")
        hot_ready = b.sem("c_hot_ready")
        hot_used = b.sem("c_hot_used")
        tile_counted = b.sem("c_tile_counted")
        tile_copied = b.sem("c_tile_copied")
        tile_stored = b.sem("c_tile_stored")
        block = ctx.enter_context(nc.Block())

        @block.sync
        def _(sp):
            sp.dma_start(edge_in[:, 0, :], src.rearrange("(r e) -> r e", e=EB)).then_inc(edges_loaded, 16)
            sp.dma_start(edge_in[:, 1, :], dst.rearrange("(r e) -> r e", e=EB)).then_inc(edges_loaded, 16)
            sp.wait_ge(span_ready, 1)
            sp.dma_start(span_row[0:1, :].rearrange("o (t k) -> o t k", k=2), span_int[:, :]).then_inc(span_loaded, 16)
            with sp.Fori(0, NT) as t:
                sp.wait_ge(tile_copied, t + 2)
                sp.dma_start(counts[bass.ds(t * TOK, TOK), :], count_out[:, :]).then_inc(tile_stored, 16)
            sp.wait_ge(tile_stored, 16 * (NT + 1))

        @block.gpsimd
        def _(pool):
            pool.iota(node_no[:, :], [[1, NS]], base=0, channel_multiplier=0,
                      allow_small_or_imprecise_dtypes=True).then_inc(iota_ready, 1)
            pool.iota(block_no[:, :], [[1, NEB]], base=0, channel_multiplier=0,
                      allow_small_or_imprecise_dtypes=True).then_inc(iota_ready, 1)
            pool.iota(tile_lo[:, :], [[TOK - 1, 2]], base=0, channel_multiplier=TOK,
                      allow_small_or_imprecise_dtypes=True).then_inc(iota_ready, 1)
            pool.memset(zeros[:, :], 0.0).then_inc(iota_ready, 1)

        @block.vector
        def _(dve):
            link = chain(dve, dve_step)
            dve.wait_ge(edges_loaded, 32)
            link(dve.tensor_copy(edge_row[:, :, :], edge_in[:, :, :]))
            dve.tensor_reduce(reach[:, 0:1], edge_row[:, 1, :], AX.X, ALU.min)
            link(dve.tensor_reduce(reach[:, 1:2], edge_row[:, 1, :], AX.X, ALU.max))
            dve.sem_inc(rows_ready, 1)
            for w in range(2):
                dve.wait_ge(turned, w + 1)
                dve.tensor_copy(edge_col[:, w, :, :], turn_bank[w][0:TOK, 0:SUB * NEB].rearrange(
                    "p (k r) -> p k r", k=SUB)).then_inc(cols_ready, 1)
            dve.wait_ge(reach_spread, 1)
            dve.wait_ge(iota_ready, 4)
            dve.tensor_scalar(over[:, 0, :], reach_bank[0:NT, 0:NEB], tile_lo[:, 1:2], None, ALU.is_le)
            link(dve.tensor_scalar(over[:, 1, :], reach_bank[0:NT, NEB:2 * NEB], tile_lo[:, 0:1], None, ALU.is_ge))
            link(dve.tensor_tensor(over[:, 0, :], over[:, 0, :], over[:, 1, :], ALU.mult))
            dve.scalar_tensor_tensor(at[:, 0, :], block_no[:, :], -float(NEB - 1), over[:, 0, :], ALU.add, ALU.mult)
            link(dve.scalar_tensor_tensor(at[:, 1, :], block_no[:, :], 1.0, over[:, 0, :], ALU.add, ALU.mult))
            dve.tensor_reduce(span[:, 0:1], at[:, 0, :], AX.X, ALU.min)
            link(dve.tensor_reduce(span[:, 1:2], at[:, 1, :], AX.X, ALU.max))
            link(dve.tensor_scalar(span[:, 0:1], span[:, 0:1], float(NEB - 1), None, ALU.add))
            link(dve.scalar_tensor_tensor(span[:, 1:2], span[:, 0:1], 1.0, span[:, 1:2], ALU.add, ALU.max))
            dve.tensor_copy(span_int[:, :], span[:, :]).then_inc(span_ready, 1)
            dve.wait_ge(cols_ready, 2)
            dve.wait_ge(span_loaded, 16)
            serial = dve.alloc_register("c_dve_serial")
            dve.reg_mov(serial, 1)
            dve.sem_inc(hot_used, SUB)
            dve.sem_inc(hot_ready, 1)
            with dve.Fori(0, NT) as t:
                first = dve.value_load(span_row[0:1, bass.ds(2 * t, 1)], min_val=0, max_val=NEB - 1)
                stop = dve.value_load(span_row[0:1, bass.ds(2 * t + 1, 1)], min_val=1, max_val=NEB)
                with dve.Fori(first, stop) as r:
                    for k in range(SUB):
                        dve.wait_ge(hot_used, serial)
                        dve.tensor_scalar(src_hot[:, k, :], node_no[:, :], edge_col[:, 0, k, bass.ds(r, 1)],
                                          None, ALU.is_equal)
                        dve.tensor_scalar(dst_hot[:, k, :], node_no[:, 0:TOK], edge_col[:, 1, k, bass.ds(r, 1)],
                                          None, ALU.is_equal).then_inc(hot_ready, 1)
                        dve.reg_add(serial, serial, 1)
                dve.wait_ge(hot_ready, serial)
                dve.tensor_scalar(edge_col[:, 1, :, :], edge_col[:, 1, :, :], -float(TOK), None,
                                  ALU.add).then_inc(cols_ready, 1)
                dve.wait_ge(cols_ready, t + 3)

        @block.scalar
        def _(act):
            act.sem_inc(tile_copied, 1)
            with act.Fori(0, NT) as t:
                act.wait_ge(tile_counted, t + 1)
                act.wait_ge(tile_stored, 16 * t + 16)
                act.activation(count_out[:, :].rearrange("p (b n) -> p b n", b=NB), acc[0:TOK, :, 0:BW],
                               ACT.Copy).then_inc(tile_copied, 1)

        @block.tensor
        def _(pe):
            pe.wait_ge(rows_ready, 1)
            for w in range(2):
                for k in range(SUB):
                    ins = pe.transpose(turn_bank[w][0:TOK, NEB * k:NEB * (k + 1)],
                                       edge_row[:, w, TOK * k:TOK * (k + 1)], ident[0:NEB, 0:NEB])
                ins.then_inc(turned, 1)
            for w in range(2):
                ins = pe.matmul(reach_bank[0:NT, NEB * w:NEB * (w + 1)],
                                reach[:, w:w + 1].to_broadcast([NEB, NT]), ident[0:NEB, 0:NEB],
                                start=True, stop=True)
            ins.then_inc(reach_spread, 1)
            pe.wait_ge(span_loaded, 16)
            pe.sem_inc(tile_stored, 16)
            serial = pe.alloc_register("c_pe_serial")
            pe.reg_mov(serial, 2)
            with pe.Fori(0, NT) as t:
                first = pe.value_load(span_row[0:1, bass.ds(2 * t, 1)], min_val=0, max_val=NEB - 1)
                stop = pe.value_load(span_row[0:1, bass.ds(2 * t + 1, 1)], min_val=1, max_val=NEB)
                pe.wait_ge(tile_copied, t + 1)
                for n in range(NB):
                    pe.matmul(acc[0:TOK, n, 0:BW], zeros[:, 0:TOK], zeros[:, 0:BW], start=True, stop=False)
                with pe.Fori(first, stop) as r:
                    for k in range(SUB):
                        pe.wait_ge(hot_ready, serial)
                        for n in range(NB):
                            ins = pe.matmul(acc[0:TOK, n, 0:BW], dst_hot[:, k, :], src_hot[:, k, BW * n:BW * (n + 1)],
                                            start=False, stop=False)
                        ins.then_inc(hot_used, 1)
                        pe.reg_add(serial, serial, 1)
                for n in range(NB):
                    ins = pe.matmul(acc[0:TOK, n, 0:BW], zeros[:, 0:TOK], zeros[:, 0:BW], start=False, stop=True)
                ins.then_inc(tile_counted, 1)


def stage_fold(nc, w_query, w_key, bias_rows, ident, xnT_hi, xnT_lo, fold_hi_dram, fold_lo_dram,
               fold_bias, row_shift, skip_bias):
    w_bq, w_bk, w_bskip = bias_rows
    HC = HEADS * DC
    with ExitStack() as ctx:
        b = Buffers(nc, ctx)
        raw = [b.sb(f"f_raw{w}", [P, DC, D]) for w in range(2)]
        turn_hi = [b.sb(f"f_turn_hi{w}", [P, DC, D], F32R) for w in range(2)]
        turn_lo = [b.sb(f"f_turn_lo{w}", [P, DC, D], F32R) for w in range(2)]
        fold_hi = b.sb("f_fold_hi", [P, DC, D], F32R)
        fold_lo = b.sb("f_fold_lo", [P, DC, D], F32R)
        bias_in = b.sb("f_bias_in", [3 * HC, P])
        bias_col = b.sb("f_bias_col", [P, 3, HC])
        bias_pair = b.sb("f_bias_pair", [P, 2, HC, 2], F32R)
        shift_col = b.sb("f_shift_col", [P, HEADS, DC])
        shift_pair = b.sb("f_shift_pair", [P, DC, HEADS, 2], F32R)
        bias_dot = b.sb("f_bias_dot", [P, HC])
        bias_dots = b.sb("f_bias_dots", [P, HEADS])
        ones = b.sb("f_ones", [P, TOK])
        shift_sum = b.sb("f_shift_sum", [TOK, NT, HEADS])
        bank = [b.ps(f"f_bank{i}", [P, 512]) for i in range(2)]
        fold_bank = [b.ps(f"f_fold{i}", [P, 512]) for i in range(2)]
        small = b.ps("f_small", [P, 512])
        shift_bank = b.ps("f_shift", [P, 512])
        bias_loaded = b.sem("f_bias_loaded")
        bias_turned = b.sem("f_bias_turned")
        pair_ready = b.sem("f_pair_ready")
        ones_ready = b.sem("f_ones_ready")
        dve_step = b.sem("f_dve_step")
        raw_loaded = [b.sem(f"f_raw_loaded{w}") for w in range(2)]
        turned = b.sem("f_turned")
        turn_hi_ready = b.sem("f_turn_hi_ready")
        turn_ready = b.sem("f_turn_ready")
        folded = b.sem("f_folded")
        fold_hi_ready = b.sem("f_fold_hi_ready")
        fold_ready = b.sem("f_fold_ready")
        small_done = b.sem("f_small_done")
        small_read = b.sem("f_small_read")
        stored = b.sem("f_stored")
        dots_ready = b.sem("f_dots_ready")
        shift_done = b.sem("f_shift_done")
        block = ctx.enter_context(nc.Block())
        PARTS = ((0, 0), (0, 1), (1, 0))

        @block.sync
        def _(sp):
            for i, rows in enumerate((w_bq, w_bk, w_bskip)):
                sp.dma_start(bias_in[HC * i:HC * (i + 1), :], rows.rearrange("(r p) -> r p", p=P)).then_inc(bias_loaded, 16)
            sp.sem_inc(stored, 32)
            with sp.Fori(0, HEADS) as h:
                for w, weights in enumerate((w_query, w_key)):
                    sp.wait_ge(turned, 8 * h + 1)
                    sp.dma_start(raw[w][:, :, :], weights.rearrange("(c p) n -> p c n", p=P)[:, :, bass.ds(h * D, D)]
                                 ).then_inc(raw_loaded[w], 16)
            sp.wait_ge(stored, 32 * (HEADS + 1))

        @block.gpsimd
        def _(pool):
            pool.memset(ones[:, :], 1.0).then_inc(ones_ready, 1)

        @block.scalar
        def _(act):
            with act.Fori(0, HEADS) as h:
                for u in range(8):
                    w, j = divmod(u, DC)
                    act.wait_ge(turned, 8 * h + u + 2)
                    act.activation(turn_hi[w][:, j, :], bank[u % 2][:, :],
                                   ACT.Copy).then_inc(turn_hi_ready, 1)
                act.wait_ge(stored, 32 * h + 32)
                for c in range(DC):
                    act.wait_ge(folded, 4 * h + c + 1)
                    act.activation(fold_hi[:, c, :], fold_bank[c % 2][:, :], ACT.Copy).then_inc(fold_hi_ready, 1)
                act.wait_ge(fold_ready, 4 * h + 5)
                for part, out in ((fold_hi, fold_hi_dram), (fold_lo, fold_lo_dram)):
                    act.dma_start(out[bass.ds(h * DC, DC), :, :].rearrange("c p n -> p c n"),
                                  part[:, :, :].bitcast(F32)
                                  ).then_inc(stored, 16)

        @block.vector
        def _(dve):
            link = chain(dve, dve_step)
            dve.wait_ge(bias_turned, 1)
            link(dve.tensor_copy(bias_col[:, :, :], small[:, 0:3 * HC].rearrange("p (i k) -> p i k", i=3)))
            dve.tensor_copy(skip_bias[:, :], bias_col[:, 2, :])
            link(dve.tensor_copy(bias_pair[:, :, :, 0], bias_col[:, 0:2, :]))
            dve.tensor_tensor(bias_pair[:, :, :, 1], bias_col[:, 0:2, :], bias_pair[:, :, :, 0].bitcast(F32),
                              ALU.subtract).then_inc(pair_ready, 1)
            link(dve.tensor_tensor(bias_dot[:, :], bias_col[:, 0, :], bias_col[:, 1, :], ALU.mult))
            link(dve.tensor_reduce(bias_dots[:, :], bias_dot[:, :].rearrange("p (h c) -> p h c", c=DC), AX.X, ALU.add))
            dve.sem_inc(dots_ready, 1)
            dve.sem_inc(turn_ready, 1)
            dve.sem_inc(fold_ready, 1)
            dve.sem_inc(small_read, 1)
            with dve.Fori(0, HEADS) as h:
                for u in range(8):
                    w, j = divmod(u, DC)
                    dve.wait_ge(turn_hi_ready, 8 * h + u + 1)
                    dve.tensor_tensor(turn_lo[w][:, j, :], bank[u % 2][:, :], turn_hi[w][:, j, :].bitcast(F32),
                                      ALU.subtract).then_inc(turn_ready, 1)
                dve.wait_ge(small_done, h + 1)
                dve.tensor_reduce(fold_bias[:, bass.ds(h, 1), :].rearrange("p o c -> p (o c)"),
                                  small[:, 64:64 + 2 * DC].rearrange("p (c k) -> p c k", k=2), AX.X, ALU.add)
                dve.tensor_reduce(shift_col[:, bass.ds(h, 1), :].rearrange("p o c -> p (o c)"),
                                  small[:, 128:128 + 2 * DC].rearrange("p (c k) -> p c k", k=2), AX.X, ALU.add
                                  ).then_inc(small_read, 1)
                for c in range(DC):
                    dve.wait_ge(fold_hi_ready, 4 * h + c + 1)
                    dve.tensor_tensor(fold_lo[:, c, :], fold_bank[c % 2][:, :], fold_hi[:, c, :].bitcast(F32),
                                      ALU.subtract).then_inc(fold_ready, 1)
            dve.wait_ge(small_read, HEADS + 1)
            link(dve.tensor_copy(shift_pair[:, :, :, 0], shift_col[:, :, :].rearrange("p h c -> p c h")))
            dve.tensor_tensor(shift_pair[:, :, :, 1], shift_col[:, :, :].rearrange("p h c -> p c h"),
                              shift_pair[:, :, :, 0].bitcast(F32), ALU.subtract).then_inc(pair_ready, 1)
            dve.wait_ge(shift_done, 1)
            link(dve.tensor_reduce(shift_sum[:, :, :], shift_bank[0:TOK, 0:2 * NT * HEADS].rearrange(
                "p (t h k) -> p t h k", t=NT, k=2), AX.X, ALU.add))
            link(dve.tensor_tensor(row_shift[:, :, :], shift_sum[:, :, :],
                                   small[0:TOK, 256:256 + HEADS].unsqueeze(1).to_broadcast([TOK, NT, HEADS]), ALU.add))

        @block.tensor
        def _(pe):
            pe.wait_ge(bias_loaded, 48)
            pe.transpose(small[:, 0:3 * HC], bias_in[:, :], ident[0:3 * HC, 0:3 * HC]).then_inc(bias_turned, 1)
            pe.wait_ge(pair_ready, 1)
            pe.sem_inc(turned, 1)
            with pe.Fori(0, HEADS) as h:
                for u in range(8):
                    w, j = divmod(u, DC)
                    if j == 0:
                        pe.wait_ge(raw_loaded[w], 16 * h + 16)
                    if u >= 2:
                        pe.wait_ge(turn_ready, 8 * h + u)
                    for c in range(DC):
                        ins = pe.transpose(bank[u % 2][:, P * c:P * (c + 1)], raw[w][:, c, P * j:P * (j + 1)], ident[:, :])
                    ins.then_inc(turned, 1)
                pe.wait_ge(turn_ready, 8 * h + 9)
                pe.wait_ge(small_read, h + 1)
                for to, w, vec in ((64, 1, 0), (128, 0, 1)):
                    for c in range(DC):
                        for j in range(DC):
                            for n, part in enumerate((turn_hi[w], turn_lo[w])):
                                ins = pe.matmul(small[:, to + 2 * c:to + 2 * c + 2], part[:, j, P * c:P * (c + 1)],
                                                bias_pair[:, vec, bass.ds(h * DC + j, 1), :].rearrange("p o k -> p (o k)"),
                                                start=(j == 0 and n == 0), stop=(j == DC - 1 and n == 1))
                ins.then_inc(small_done, 1)
                for c in range(DC):
                    if c >= 2:
                        pe.wait_ge(fold_ready, 4 * h + c)
                    for j in range(DC):
                        for n, (x, y) in enumerate(PARTS):
                            ins = pe.matmul(fold_bank[c % 2][:, :], (turn_hi, turn_lo)[x][0][:, j, P * c:P * (c + 1)],
                                            (turn_hi, turn_lo)[y][1][:, j, :], start=(j == 0 and n == 0),
                                            stop=(j == DC - 1 and n == 2))
                    ins.then_inc(folded, 1)
                pe.wait_ge(fold_ready, 4 * h + 5)
            pe.wait_ge(pair_ready, 2)
            for t in range(NT):
                for c in range(DC):
                    for n, part in enumerate((xnT_hi, xnT_lo)):
                        pe.matmul(shift_bank[0:TOK, 8 * t:8 * t + 8], part[:, c, TOK * t:TOK * (t + 1)],
                                  shift_pair[:, c, :, :].rearrange("p h k -> p (h k)"),
                                  start=(c == 0 and n == 0), stop=(c == DC - 1 and n == 1))
            pe.wait_ge(dots_ready, 1)
            pe.wait_ge(ones_ready, 1)
            pe.matmul(small[0:TOK, 256:256 + HEADS], ones[:, :], bias_dots[:, :], start=True, stop=True).then_inc(shift_done, 1)


class Steps:

    def __init__(self, engine, sem, base, total):
        self.engine, self.sem, self.base, self.total, self.n = engine, sem, base, total, 0

    def __call__(self, ins):
        self.n += 1
        ins.then_inc(self.sem, 1)
        self.engine.wait_ge(self.sem, self.base + self.n)

    def end(self):
        assert self.n == self.total


PARTS = ((0, 0), (0, 1), (1, 0))


def stage_attend(nc, xnT, counts, fold_dram, fold_bias, row_shift, skip_bias, ident,
                 w_value, b_value, w_skip, w_lin, b_lin, hidden):
    SCALE = float(D) ** -0.5
    HEAD_STEPS, GROUP_STEPS = 6, 12
    with ExitStack() as ctx:
        b = Buffers(nc, ctx)
        fold = [b.sb(f"a_fold_{k}", [P, DC, D], F32R) for k in ("hi", "lo")]
        skip_w = [b.sb(f"a_skip_w_{k}", [P, DC, D], F32R) for k in ("hi", "lo")]
        lin_w = [b.sb(f"a_lin_w_{k}", [P, DC, D], F32R) for k in ("hi", "lo")]
        shared = [b.sb(f"a_shared_{k}", [P, NT * GRP], F32R) for k in ("hi", "lo")]
        value_w = [s[:, 0:DC * D].rearrange("p (c n) -> p c n", c=DC) for s in shared]
        prob_t = [s[0:TOK, :].rearrange("p (s n) -> p s n", s=NT) for s in shared]
        raw = b.sb("a_raw", [P, DC, D])
        value = [b.sb(f"a_value_{k}", [TOK, NT, D], F32R) for k in ("hi", "lo")]
        value_sum = b.sb("a_value_sum", [TOK, 2, D])
        value_bias = b.sb("a_value_bias", [TOK, D])
        query_t = [b.sb(f"a_query_t_{k}", [P, DC, GRP], F32R) for k in ("hi", "lo")]
        attn_t = [b.sb(f"a_attn_t_{k}", [P, DC, GRP], F32R) for k in ("hi", "lo")]
        count = [b.sb(f"a_count{t}", [TOK, NS], U16) for t in range(2)]
        no_edge = b.sb("a_no_edge", [TOK, NS], BF16)
        score = [b.sb(f"a_score{t}", [TOK, NS]) for t in range(2)]
        fold_bias_now = b.sb("a_fold_bias_now", [P, DC])
        skip_bias_now = b.sb("a_skip_bias_now", [P, DC])
        top = b.sb("a_top", [TOK, 2])
        shift = b.sb("a_shift", [TOK, 2])
        den = b.sb("a_den", [TOK, 2])
        inv_den = b.sb("a_inv_den", [TOK, 2])
        hold = b.sb("a_hold", [TOK, 2, D])
        head0 = b.sb("a_head0", [P, P])
        bank_a = b.ps("a_bank_a", [P, NB, 512])
        bank_b = b.ps("a_bank_b", [P, NB, 512])
        bank_c = b.ps("a_bank_c", [P, 2, 512])

        fold_loaded = b.sem("a_fold_loaded")
        raw_loaded = b.sem("a_raw_loaded")
        value_bias_loaded = b.sem("a_value_bias_loaded")
        count_loaded = [b.sem(f"a_count_loaded{t}") for t in range(2)]
        hold_loaded = b.sem("a_hold_loaded")
        hidden_stored = b.sem("a_hidden_stored")
        lin_raw_ready = b.sem("a_lin_raw_ready")
        split_hi = b.sem("a_split_hi")
        split_done = b.sem("a_split_done")
        value_done = b.sem("a_value_done")
        value_summed = b.sem("a_value_summed")
        value_hi = b.sem("a_value_hi")
        value_ready = b.sem("a_value_ready")
        query_done = b.sem("a_query_done")
        query_hi = b.sem("a_query_hi")
        query_ready = b.sem("a_query_ready")
        scored = b.sem("a_scored")
        masked = b.sem("a_masked")
        shift_ready = b.sem("a_shift_ready")
        exp_done = b.sem("a_exp_done")
        weighted = b.sem("a_weighted")
        inv_ready = b.sem("a_inv_ready")
        prob_ready = b.sem("a_prob_ready")
        turned = b.sem("a_turned")
        prob_t_hi = b.sem("a_prob_t_hi")
        prob_t_ready = b.sem("a_prob_t_ready")
        attn_done = b.sem("a_attn_done")
        attn_hi = b.sem("a_attn_hi")
        attn_ready = b.sem("a_attn_ready")
        lin_done = b.sem("a_lin_done")
        added = b.sem("a_added")
        bias_ready = b.sem("a_bias_ready")
        dve_step = b.sem("a_dve_step")
        block = ctx.enter_context(nc.Block())

        def half(bank, c):
            return bank[:, c // 2, GRP * (c % 2):GRP * (c % 2 + 1)]

        def groups(engine, group, h):
            with engine.Fori(0, NG - 1) as g:
                group(h, g, False)
            group(h, NG - 1, True)


        @block.sync
        def _(sp):
            def group(h, g, last):
                nth = h * NG + (g + 1)
                for t in range(2):
                    sp.wait_ge(weighted, 2 * nth - 1 + t)
                    sp.dma_start(count[t][:, :], counts[bass.ds(g * GRP + t * TOK, TOK), :]).then_inc(count_loaded[t], 16)

            def weights(src, h):
                return src.rearrange("(c p) n -> p c n", p=P)[:, :, bass.ds(h * D, D)]

            with sp.Fori(0, HEADS) as h:
                sp.wait_ge(query_done, h * NG + 1)
                for k in range(2):
                    sp.dma_start(fold[k][:, :, :].bitcast(F32), fold_dram[k][bass.ds(h * DC, DC), :, :].rearrange(
                        "c p n -> p c n")).then_inc(fold_loaded, 16)
                sp.wait_ge(split_done, 3 * h + 1)
                sp.dma_start(raw[:, :, :], weights(w_value, h)).then_inc(raw_loaded, 16)
                sp.wait_ge(value_ready, NT * h + 1)
                sp.dma_start(value_bias[:, :], b_value[bass.ds(h * D, D)].unsqueeze(0).to_broadcast([TOK, D])
                             ).then_inc(value_bias_loaded, 16)
                sp.wait_ge(split_done, 3 * h + 2)
                sp.dma_start(raw[:, :, :], weights(w_skip, h)).then_inc(raw_loaded, 16)
                sp.wait_ge(split_done, 3 * h + 3)
                sp.dma_start(raw[:, :, :], w_lin.rearrange("(c p) n -> p c n", p=P)[:, bass.ds(h * DC, DC), :]
                             ).then_inc(raw_loaded, 16)
                groups(sp, group, h)

        @block.scalar
        def _(act):
            act.dma_start(hidden[:, :], b_lin.unsqueeze(0).to_broadcast([N, D])).then_inc(hidden_stored, 16)

            def rows(g):
                return hidden[bass.ds(g * GRP, GRP), :].rearrange("(t p) c -> p t c", p=TOK)

            def split(h, i, weight):
                act.wait_ge(raw_loaded, 16 * (3 * h + i + 1))
                if i == 2:
                    act.wait_ge(lin_raw_ready, h + 2)
                act.activation(weight[0], raw[:, :, :], ACT.Copy).then_inc(split_hi, 1)

            def query(h, bank, nth):
                act.wait_ge(query_done, nth + 1)
                for c in range(DC):
                    act.activation(query_t[0][:, c, :], half(bank, c), ACT.Identity,
                                   bias=fold_bias_now[:, c:c + 1]).then_inc(query_hi, 1)

            def group(h, g, last):
                nth = h * NG + (g + 1)
                act.wait_ge(hidden_stored, 16 * nth)
                act.dma_start(hold[:, :, :], rows(g)).then_inc(hold_loaded, 16)
                for t in range(2):
                    act.wait_ge(shift_ready, 2 * nth - 1 + t)
                    act.activation(score[t][:, :], score[t][:, :], ACT.Exp, bias=shift[:, t:t + 1],
                                   scale=SCALE).then_inc(exp_done, 1)
                    act.wait_ge(inv_ready, 2 * nth - 1 + t)
                    act.activation(score[t][:, :], score[t][:, :], ACT.Copy,
                                   scale=inv_den[:, t:t + 1]).then_inc(prob_ready, 1)
                if not last:
                    query(h, bank_a, nth + 1)
                for t, bank in ((0, bank_b), (1, bank_a)):
                    act.wait_ge(turned, 2 * nth - 1 + t)
                    cols = slice(TOK * t, TOK * (t + 1))
                    act.activation(prob_t[0][:, 0:8, cols].rearrange("p (b i) n -> p b i n", b=2),
                                   bank[0:TOK, 0:2, 0:500].rearrange("p b (i n) -> p b i n", n=TOK), ACT.Copy)
                    act.activation(prob_t[0][:, 8:10, cols],
                                   bank[0:TOK, 2, 0:250].rearrange("p (i n) -> p i n", n=TOK), ACT.Copy
                                   ).then_inc(prob_t_hi, 1)
                for c in range(DC):
                    act.wait_ge(attn_done, 2 * nth - 1 + c // 2)
                    act.activation(attn_t[0][:, c, :], half(bank_c, c), ACT.Identity,
                                   bias=skip_bias_now[:, c:c + 1]).then_inc(attn_hi, 1)
                act.wait_ge(added, 2 * nth + 1)
                act.dma_start(rows(g), hold[:, :, :]).then_inc(hidden_stored, 16)

            with act.Fori(0, HEADS) as h:
                act.wait_ge(lin_done, h * NG + 1)
                act.wait_ge(bias_ready, h + 1)
                split(h, 0, value_w)
                for s in range(NT):
                    act.wait_ge(value_summed, NT * h + s + 1)
                    act.activation(value[0][:, s, :], value_sum[:, s % 2, :], ACT.Copy).then_inc(value_hi, 1)
                    if s == 4:
                        split(h, 1, [w[:, :, :] for w in skip_w])
                    if s == 8:
                        split(h, 2, [w[:, :, :] for w in lin_w])
                query(h, bank_c, h * NG + 1)
                groups(act, group, h)
            act.wait_ge(hidden_stored, 16 * (HEADS * NG + 1))

        @block.vector
        def _(dve):
            def split(h, i, weight):
                dve.wait_ge(split_hi, 3 * h + i + 1)
                dve.tensor_tensor(weight[1], raw[:, :, :], weight[0].bitcast(F32), ALU.subtract).then_inc(split_done, 1)

            def query(h, bank, nth):
                for c in range(DC):
                    dve.wait_ge(query_hi, 4 * nth - 3 + (c | 1))
                    dve.scalar_tensor_tensor(query_t[1][:, c, :], half(bank, c), fold_bias_now[:, c:c + 1],
                                             query_t[0][:, c, :].bitcast(F32), ALU.add, ALU.subtract
                                             ).then_inc(query_ready, 1)

            def group(h, g, last):
                nth = h * NG + (g + 1)
                link = Steps(dve, dve_step, h * (HEAD_STEPS + NG * GROUP_STEPS) + HEAD_STEPS + g * GROUP_STEPS, GROUP_STEPS)
                banks = (bank_a, bank_b)

                def mask(t):
                    dve.wait_ge(count_loaded[t], 16 * nth)
                    link(dve.tensor_scalar(no_edge[:, :], count[t][:, :], 0.0, -FAR, ALU.is_equal, ALU.mult))

                def largest(t):
                    dve.wait_ge(scored, 2 * nth - 1 + t)
                    dve.scalar_tensor_tensor(score[t][:, :].rearrange("p (b n) -> p b n", b=NB),
                                             no_edge[:, :].rearrange("p (b n) -> p b n", b=NB),
                                             row_shift[:, bass.ds(g * 2 + t, 1), bass.ds(h, 1)].rearrange("p a o -> p (a o)"),
                                             banks[t][0:TOK, :, 0:BW], ALU.add, ALU.add).then_inc(masked, 1)
                    dve.wait_ge(masked, 2 * nth - 1 + t)
                    link(dve.tensor_reduce(top[:, t:t + 1], score[t][:, :], AX.X, ALU.max))
                    dve.tensor_scalar(shift[:, t:t + 1], top[:, t:t + 1], -SCALE, None, ALU.mult).then_inc(shift_ready, 1)

                def weigh(t):
                    dve.wait_ge(exp_done, 2 * nth - 1 + t)
                    dve.scalar_tensor_tensor(score[t][:, :], count[t][:, :], 1.0, score[t][:, :], ALU.mult, ALU.mult,
                                             accum_out=den[:, t:t + 1]).then_inc(weighted, 1)
                    dve.wait_ge(weighted, 2 * nth + 1 + t)
                    link(dve.tensor_scalar(den[:, t:t + 1], den[:, t:t + 1], 0.5, None, ALU.max))
                    dve.reciprocal(inv_den[:, t:t + 1], den[:, t:t + 1]).then_inc(inv_ready, 1)

                mask(0)
                largest(0)
                mask(1)
                weigh(0)
                largest(1)
                weigh(1)
                if not last:
                    query(h, bank_a, nth + 1)
                for t, bank in ((0, bank_b), (1, bank_a)):
                    dve.wait_ge(prob_t_hi, 2 * nth - 1 + t)
                    cols = slice(TOK * t, TOK * (t + 1))
                    four = [prob_t[k][:, 0:8, cols].rearrange("p (b i) n -> p b i n", b=2) for k in range(2)]
                    dve.tensor_tensor(four[1], bank[0:TOK, 0:2, 0:500].rearrange("p b (i n) -> p b i n", n=TOK),
                                      four[0].bitcast(F32), ALU.subtract)
                    dve.tensor_tensor(prob_t[1][:, 8:10, cols],
                                      bank[0:TOK, 2, 0:250].rearrange("p (i n) -> p i n", n=TOK),
                                      prob_t[0][:, 8:10, cols].bitcast(F32), ALU.subtract).then_inc(prob_t_ready, 1)
                for c in range(DC):
                    dve.wait_ge(attn_hi, 4 * nth - 3 + (c | 1))
                    dve.scalar_tensor_tensor(attn_t[1][:, c, :], half(bank_c, c), skip_bias_now[:, c:c + 1],
                                             attn_t[0][:, c, :].bitcast(F32), ALU.add, ALU.subtract
                                             ).then_inc(attn_ready, 1)
                dve.wait_ge(lin_done, nth + 1)
                dve.wait_ge(hold_loaded, 16 * nth)
                for t in range(2):
                    dve.tensor_tensor(hold[:, t, :], bank_b[0:TOK, t, :], hold[:, t, :], ALU.add).then_inc(added, 1)
                while link.n < GROUP_STEPS:
                    dve.sem_inc(dve_step, 1)
                    link.n += 1

            dve.tensor_copy(head0[:, :], ident[:, :]).then_inc(lin_raw_ready, 1)
            dve.wait_ge(lin_raw_ready, 1)
            dve.sem_inc(split_done, 1)
            dve.sem_inc(value_ready, 1)
            dve.sem_inc(weighted, 2)
            dve.sem_inc(attn_ready, 1)
            dve.sem_inc(added, 1)
            with dve.Fori(0, HEADS) as h:
                link = Steps(dve, dve_step, h * (HEAD_STEPS + NG * GROUP_STEPS), HEAD_STEPS)
                dve.wait_ge(added, 2 * NG * h + 1)
                dve.tensor_copy(fold_bias_now[:, :], fold_bias[:, bass.ds(h, 1), :].rearrange("p o c -> p (o c)"))
                dve.tensor_copy(skip_bias_now[:, :], skip_bias[:, bass.ds(h * DC, DC)]).then_inc(bias_ready, 1)
                dve.wait_ge(bias_ready, h + 1)
                split(h, 0, value_w)
                dve.wait_ge(value_bias_loaded, 16 * h + 16)
                for s in range(NT):
                    bank = ((bank_a, bank_b)[(s // 2) % 2])
                    dve.wait_ge(value_done, NT * h + s + 1)
                    dve.tensor_tensor(value_sum[:, s % 2, :], bank[0:TOK, s % 2, :], value_bias[:, :],
                                      ALU.add).then_inc(value_summed, 1)
                    if s == 8:
                        dve.wait_ge(raw_loaded, 16 * (3 * h + 3))
                        for c in range(DC):
                            ins = dve.tensor_tensor(raw[:, c, P * c:P * (c + 1)], raw[:, c, P * c:P * (c + 1)],
                                                    head0[:, :], ALU.add)
                        ins.then_inc(lin_raw_ready, 1)
                        dve.wait_ge(lin_raw_ready, h + 2)
                        link(dve.memset(head0[:, :], 0.0))
                    dve.wait_ge(value_hi, NT * h + s + 1)
                    dve.tensor_tensor(value[1][:, s, :], value_sum[:, s % 2, :], value[0][:, s, :].bitcast(F32),
                                      ALU.subtract).then_inc(value_ready, 1)
                    if s == 4:
                        split(h, 1, [w[:, :, :] for w in skip_w])
                    if s == 8:
                        split(h, 2, [w[:, :, :] for w in lin_w])
                query(h, bank_c, h * NG + 1)
                while link.n < HEAD_STEPS:
                    dve.sem_inc(dve_step, 1)
                    link.n += 1
                groups(dve, group, h)

        @block.tensor
        def _(pe):
            def query(bank, g):
                for m in range(DC):
                    for c in range(DC):
                        for n, (x, y) in enumerate(PARTS):
                            ins = pe.matmul(half(bank, m), fold[x][:, c, P * m:P * (m + 1)],
                                            xnT[y][:, c, bass.ds(g * GRP, GRP)], start=(c == 0 and n == 0),
                                            stop=(c == DC - 1 and n == 2))
                ins.then_inc(query_done, 1)

            def turn(bank, t):
                for s in range(NT):
                    ins = pe.transpose(bank[0:TOK, s // 4, TOK * (s % 4):TOK * (s % 4 + 1)],
                                       score[t][:, TOK * s:TOK * (s + 1)], ident[0:TOK, 0:TOK])
                ins.then_inc(turned, 1)

            def group(h, g, last):
                nth = h * NG + (g + 1)
                pe.wait_ge(query_ready, 4 * nth)
                for t, bank in ((0, bank_a), (1, bank_b)):
                    if t == 1:
                        pe.wait_ge(added, 2 * nth - 1)
                    for c in range(DC):
                        for n, (x, y) in enumerate(PARTS):
                            for m in range(NB):
                                ins = pe.matmul(bank[0:TOK, m, 0:BW], query_t[x][:, c, TOK * t:TOK * (t + 1)],
                                                xnT[y][:, c, BW * m:BW * (m + 1)], start=(c == 0 and n == 0),
                                                stop=(c == DC - 1 and n == 2))
                    ins.then_inc(scored, 1)
                pe.wait_ge(attn_ready, 4 * nth - 3)
                pe.wait_ge(split_done, 3 * h + 3)
                for m in range(DC):
                    for c in range(DC):
                        for n, (x, y) in enumerate(PARTS):
                            pe.matmul(half(bank_c, m), skip_w[x][:, c, P * m:P * (m + 1)],
                                      xnT[y][:, c, bass.ds(g * GRP, GRP)], start=(m % 2 == 0 and c == 0 and n == 0),
                                      stop=False, skip_group_check=True)
                if not last:
                    pe.wait_ge(masked, 2 * nth - 1)
                    query(bank_a, g + 1)
                pe.wait_ge(masked, 2 * nth)
                pe.wait_ge(prob_ready, 2 * nth - 1)
                turn(bank_b, 0)
                if not last:
                    pe.wait_ge(query_ready, 4 * nth + 4)
                pe.wait_ge(prob_ready, 2 * nth)
                turn(bank_a, 1)
                pe.wait_ge(prob_t_ready, 2 * nth)
                for m in range(DC):
                    for s in range(NT):
                        for n, (x, y) in enumerate(PARTS):
                            ins = pe.matmul(half(bank_c, m), value[x][:, s, P * m:P * (m + 1)], prob_t[y][:, s, :],
                                            start=False, stop=(s == NT - 1 and n == 2), skip_group_check=True)
                    if m % 2:
                        ins.then_inc(attn_done, 1)
                pe.wait_ge(split_done, 3 * h + 4)
                for c in range(DC):
                    pe.wait_ge(attn_ready, 4 * nth - 2 + c)
                    for t in range(2):
                        for n, (x, y) in enumerate(PARTS):
                            ins = pe.matmul(bank_b[0:TOK, t, :], attn_t[x][:, c, TOK * t:TOK * (t + 1)],
                                            lin_w[y][:, c, :], start=(c == 0 and n == 0), stop=(c == DC - 1 and n == 2))
                ins.then_inc(lin_done, 1)

            pe.sem_inc(query_done, 1)
            pe.sem_inc(lin_done, 1)
            with pe.Fori(0, HEADS) as h:
                pe.wait_ge(split_done, 3 * h + 2)
                for s in range(NT):
                    bank = (bank_a, bank_b)[(s // 2) % 2]
                    if s == 2:
                        pe.wait_ge(added, 2 * NG * h + 1)
                    if s >= 4:
                        pe.wait_ge(value_summed, NT * h + s - 3)
                    for c in range(DC):
                        for n, (x, y) in enumerate(PARTS):
                            ins = pe.matmul(bank[0:TOK, s % 2, :], xnT[x][:, c, TOK * s:TOK * (s + 1)],
                                            value_w[y][:, c, :], start=(c == 0 and n == 0), stop=(c == DC - 1 and n == 2))
                    ins.then_inc(value_done, 1)
                pe.wait_ge(attn_ready, 4 * NG * h + 1)
                pe.wait_ge(fold_loaded, 32 * h + 32)
                query(bank_c, 0)
                groups(pe, group, h)


def wide(bank, rows, n=N):
    return ((bank[rows, 0:2, 0:500], slice(0, 1000)), (bank[rows, 2, 0:250], slice(1000, 1250)))


def stage_mix(nc, xrow, ident, w_qkv, w_out, norm_gamma, mixed):
    FEAT = MIX_HEADS * MIX_DIM
    with ExitStack() as outer:
        b = Buffers(nc, outer)
        xm_t = [b.sb(f"m_xm_t_{k}", [P, DC, N], F32R) for k in ("hi", "lo")]
        wt = [[b.sb(f"m_wt_{i}_{k}", [P, DC, FEAT], F32R) for k in ("hi", "lo")] for i in "qkv"]
        shared = b.sb("m_shared", [P, NT * D])
        raw = [shared[:, 2048 * i:2048 * (i + 1)].rearrange("p (c n) -> p c n", c=DC) for i in range(2)]
        key = shared[0:TOK, :].rearrange("p (t n) -> p t n", t=NT)
        w_out_raw = b.sb("m_w_out_raw", [P, DC, FEAT])
        w_out_loaded = b.sem("m_w_out_loaded")

        with ExitStack() as ctx:
            b = Buffers(nc, ctx)
            stats = b.sb("m_stats", [TOK, NT, 6])
            mean_var = b.sb("m_mean_var", [TOK, NT, 2])
            root_in = b.sb("m_root_in", [TOK, NT])
            root = b.sb("m_root", [TOK, NT])
            scratch = b.sb("m_scratch", [TOK, NT])
            rstd = b.sb("m_rstd", [TOK, NT])
            gamma_in = b.sb("m_gamma_in", [DC, P])
            gamma = b.sb("m_gamma", [P, DC])
            bank = [b.ps(f"m_bank{i}", [P, 512]) for i in range(4)]
            gamma_bank = b.ps("m_gamma_bank", [P, 512])
            gamma_loaded = b.sem("m_gamma_loaded")
            gamma_turned = b.sem("m_gamma_turned")
            gamma_ready = b.sem("m_gamma_ready")
            raw_loaded = [b.sem(f"m_raw_loaded{i}") for i in range(2)]
            dve_step = b.sem("m_dve_step")
            var_ready = b.sem("m_var_ready")
            root_ready = b.sem("m_root_ready")
            row_ready = b.sem("m_row_ready")
            turned = b.sem("m_turned")
            hi_ready = b.sem("m_hi_ready")
            lo_ready = b.sem("m_lo_ready")
            block = ctx.enter_context(nc.Block())
            units = [("w", i, c) for i in range(3) for c in range(DC)] + [("x", g, c) for g in range(3) for c in range(DC)]

            def place(kind, i, c):
                if kind == "w":
                    return [wt[i][k][:, c, :] for k in range(2)], FEAT
                n = TOK * len(tile_parts(i))
                return [xm_t[k][:, c, 500 * i:500 * i + n] for k in range(2)], n

            @block.sync
            def _(sp):
                sp.dma_start(gamma_in[:, :], norm_gamma.rearrange("(c p) -> c p", p=P)).then_inc(gamma_loaded, 16)
                for i in range(3):
                    if i == 2:
                        sp.wait_ge(turned, DC)
                    sp.dma_start(raw[i % 2][:, :, :], w_qkv[FEAT * i:FEAT * (i + 1), :].rearrange(
                        "(r p) n -> p r n", p=P)).then_inc(raw_loaded[i % 2], 16)
                sp.dma_start(w_out_raw[:, :, :], w_out.rearrange("(r p) n -> p r n", p=P)).then_inc(w_out_loaded, 16)

            @block.vector
            def _(dve):
                link = chain(dve, dve_step)
                node_stats(dve, link, xrow, stats, mean_var, root_in).then_inc(var_ready, 1)
                dve.wait_ge(root_ready, 1)
                inverse_root(dve, link, root_in[:, :], root[:, :], scratch[:, :], rstd[:, :])
                for t in range(NT):
                    dve.tensor_scalar(xrow[:, t, :], xrow[:, t, :], mean_var[:, t, 0:1], rstd[:, t:t + 1],
                                      ALU.subtract, ALU.mult).then_inc(row_ready, 1)
                dve.wait_ge(gamma_turned, 1)
                dve.tensor_copy(gamma[:, :], gamma_bank[:, 0:DC]).then_inc(gamma_ready, 1)
                dve.wait_ge(gamma_ready, 1)
                for u, (kind, i, c) in enumerate(units):
                    (hi, lo), n = place(kind, i, c)
                    dve.wait_ge(hi_ready, u + 1)
                    if kind == "w":
                        ins = dve.tensor_tensor(lo, bank[u % 4][:, 0:n], hi.bitcast(F32), ALU.subtract)
                    else:
                        ins = dve.scalar_tensor_tensor(lo, bank[u % 4][:, 0:n], gamma[:, c:c + 1], hi.bitcast(F32),
                                                       ALU.mult, ALU.subtract)
                    ins.then_inc(lo_ready, 1)

            @block.scalar
            def _(act):
                act.wait_ge(var_ready, 1)
                act.activation(root[:, :], root_in[:, :], ACT.Sqrt).then_inc(root_ready, 1)
                act.wait_ge(gamma_ready, 1)
                for u, (kind, i, c) in enumerate(units):
                    (hi, lo), n = place(kind, i, c)
                    act.wait_ge(turned, u + 1)
                    act.activation(hi, bank[u % 4][:, 0:n], ACT.Copy,
                                   scale=1.0 if kind == "w" else gamma[:, c:c + 1]).then_inc(hi_ready, 1)

            @block.tensor
            def _(pe):
                pe.wait_ge(gamma_loaded, 16)
                pe.transpose(gamma_bank[:, 0:DC], gamma_in[:, :], ident[0:DC, 0:DC]).then_inc(gamma_turned, 1)
                for u, (kind, i, c) in enumerate(units):
                    if u >= 4:
                        pe.wait_ge(lo_ready, u - 3)
                    if kind == "w":
                        pe.wait_ge(raw_loaded[i % 2], 16 * (i // 2 + 1))
                        for r in range(DC):
                            ins = pe.transpose(bank[u % 4][:, P * r:P * (r + 1)], raw[i % 2][:, r, P * c:P * (c + 1)],
                                               ident[:, :])
                    else:
                        pe.wait_ge(row_ready, tile_parts(i)[-1] + 1)
                        for j, t in enumerate(tile_parts(i)):
                            ins = pe.transpose(bank[u % 4][:, TOK * j:TOK * (j + 1)], xrow[:, t, P * c:P * (c + 1)],
                                               ident[0:TOK, 0:TOK])
                    ins.then_inc(turned, 1)

        with ExitStack() as ctx:
            b = Buffers(nc, ctx)
            value = xrow
            key_exp = [b.sb(f"m_key_exp{i}", [P, N]) for i in range(2)]
            key_top = b.sb("m_key_top", [P, DC])
            key_sum = b.sb("m_key_sum", [P, DC])
            key_scale = b.sb("m_key_scale", [P, DC])
            context = [b.sb(f"m_context_{k}", [P, DC, P], F32R) for k in ("hi", "lo")]
            key_bank = [b.ps(f"m_key_bank{i}", [P, 3, 512]) for i in range(2)]
            row_bank = [b.ps(f"m_row_bank{i}", [P, 512]) for i in range(2)]
            key_done = b.sem("m_key_done")
            key_copied = b.sem("m_key_copied")
            top_ready = b.sem("m_top_ready")
            exp_done = b.sem("m_exp_done")
            key_turned = b.sem("m_key_turned")
            key_ready = b.sem("m_key_ready")
            row_done = b.sem("m_row_done")
            row_hi = b.sem("m_row_hi")
            row_ready = b.sem("m_row2_ready")
            clear = b.sem("m_clear")
            scale_ready = b.sem("m_scale_ready")
            dve_step = b.sem("m_dve_step2")
            block = ctx.enter_context(nc.Block())
            VALUES, TURNS, CONTEXTS = 0, NT, NT + DC
            PRODUCTS = NT + 2 * DC
            USES = NT + 3 * DC

            @block.gpsimd
            def _(pool):
                for k in range(2):
                    pool.memset(context[k][:, :, :].bitcast(F32), 0.0).then_inc(clear, 1)

            @block.scalar
            def _(act):
                def key_part(f):
                    act.wait_ge(key_done, f + 1)
                    for part, cols in wide(key_bank[f % 2], slice(0, P)):
                        out = key_exp[f % 2][:, cols]
                        ins = act.activation(out.rearrange("p (b n) -> p b n", n=500) if cols.start == 0 else out,
                                             part, ACT.Copy)
                    ins.then_inc(key_copied, 1)
                    act.wait_ge(top_ready, f + 1)
                    act.activation(key_exp[f % 2][:, :], key_exp[f % 2][:, :], ACT.Exp, bias=key_top[:, f:f + 1],
                                   accum_out=key_sum[:, f:f + 1]).then_inc(exp_done, 1)

                def row(u):
                    act.wait_ge(row_done, u + 1)
                    src = row_bank[u % 2]
                    if u < TURNS:
                        act.activation(value[:, u, :], src[0:TOK, :], ACT.Copy).then_inc(row_hi, 1)
                    elif u < CONTEXTS:
                        act.activation(wt[2][0][:, u - TURNS, :], src[:, :], ACT.Copy).then_inc(row_hi, 1)
                    elif u < PRODUCTS:
                        f = u - CONTEXTS
                        act.activation(context[0][0:64, f, 0:64], src[0:64, 0:64], ACT.Copy)
                        act.activation(context[0][64:128, f, 64:128], src[64:128, 64:128], ACT.Copy).then_inc(row_hi, 1)
                    else:
                        f = u - PRODUCTS
                        act.activation(wt[1][0][:, f, :], src[:, :], ACT.Copy, scale=key_scale[:, f:f + 1]).then_inc(row_hi, 1)

                key_part(0)
                key_part(1)
                for u in range(5):
                    row(u)
                key_part(2)
                key_part(3)
                for u in range(5, CONTEXTS):
                    row(u)
                act.wait_ge(clear, 2)
                act.wait_ge(scale_ready, 1)
                for u in range(CONTEXTS, USES):
                    row(u)

            @block.vector
            def _(dve):
                link = chain(dve, dve_step)

                def top(f):
                    dve.wait_ge(key_copied, f + 1)
                    dve.tensor_reduce(key_top[:, f:f + 1], key_exp[f % 2][:, :], AX.X, ALU.max,
                                      negate=True).then_inc(top_ready, 1)

                def turn(f):
                    dve.wait_ge(key_turned, f + 1)
                    for part, tiles in ((key_bank[f % 2][0:TOK, 0:2, :], slice(0, 8)), (key_bank[f % 2][0:TOK, 2, 0:256], slice(8, 10))):
                        out = key[:, tiles, P * f:P * (f + 1)]
                        ins = dve.tensor_copy(out.rearrange("p (b i) n -> p b i n", i=4) if tiles.start == 0 else out,
                                              part.rearrange("p b (i n) -> p b i n", n=P) if tiles.start == 0
                                              else part.rearrange("p (i n) -> p i n", n=P))
                    ins.then_inc(key_ready, 1)

                def row(u):
                    dve.wait_ge(row_hi, u + 1)
                    src = row_bank[u % 2]
                    if u < CONTEXTS:
                        f = u - TURNS
                        dve.tensor_tensor(wt[2][1][:, f, :], src[:, :], wt[2][0][:, f, :].bitcast(F32),
                                          ALU.subtract).then_inc(row_ready, 1)
                    elif u < PRODUCTS:
                        f = u - CONTEXTS
                        for lo in (0, 64):
                            at = slice(lo, lo + 64)
                            ins = dve.tensor_tensor(context[1][at, f, at], src[at, at], context[0][at, f, at].bitcast(F32),
                                                    ALU.subtract)
                        ins.then_inc(row_ready, 1)
                    else:
                        f = u - PRODUCTS
                        dve.scalar_tensor_tensor(wt[1][1][:, f, :], src[:, :], key_scale[:, f:f + 1],
                                                 wt[1][0][:, f, :].bitcast(F32), ALU.mult, ALU.subtract
                                                 ).then_inc(row_ready, 1)

                top(0)
                top(1)
                turn(0)
                top(2)
                turn(1)
                top(3)
                turn(2)
                turn(3)
                for u in range(TURNS, CONTEXTS):
                    row(u)
                dve.wait_ge(exp_done, DC)
                link(dve.reciprocal(key_scale[:, :], key_sum[:, :]))
                dve.tensor_scalar(key_scale[:, :], key_scale[:, :], MIX_DIM ** -0.5, None, ALU.mult).then_inc(scale_ready, 1)
                dve.wait_ge(scale_ready, 1)
                dve.wait_ge(clear, 2)
                for u in range(CONTEXTS, USES):
                    row(u)

            @block.tensor
            def _(pe):
                def keys(f):
                    if f >= 2:
                        pe.wait_ge(key_ready, f - 1)
                    for c in range(DC):
                        for n, (x, y) in enumerate(PARTS):
                            for m, w in enumerate((500, 500, 250)):
                                ins = pe.matmul(key_bank[f % 2][:, m, 0:w], wt[1][x][:, c, P * f:P * (f + 1)],
                                                xm_t[y][:, c, 500 * m:500 * m + w], start=(c == 0 and n == 0),
                                                stop=(c == DC - 1 and n == 2))
                    ins.then_inc(key_done, 1)

                def turn(f):
                    pe.wait_ge(exp_done, f + 1)
                    for t in range(NT):
                        ins = pe.transpose(key_bank[f % 2][0:TOK, t // 4, P * (t % 4):P * (t % 4 + 1)],
                                           key_exp[f % 2][:, TOK * t:TOK * (t + 1)], ident[:, :])
                    ins.then_inc(key_turned, 1)

                def bank_free(u):
                    if u >= 2:
                        if u - 2 < TURNS:
                            pe.wait_ge(row_hi, u - 1)
                        else:
                            pe.wait_ge(row_ready, u - 1 - TURNS)

                def values(t):
                    bank_free(t)
                    for c in range(DC):
                        for n, (x, y) in enumerate(PARTS):
                            ins = pe.matmul(row_bank[t % 2][0:TOK, :], xm_t[x][:, c, TOK * t:TOK * (t + 1)],
                                            wt[2][y][:, c, :], start=(c == 0 and n == 0), stop=(c == DC - 1 and n == 2))
                    ins.then_inc(row_done, 1)

                keys(0)
                keys(1)
                for t in range(5):
                    values(t)
                turn(0)
                keys(2)
                turn(1)
                keys(3)
                for t in range(5, NT):
                    values(t)
                turn(2)
                turn(3)
                pe.wait_ge(w_out_loaded, 16)
                for f in range(DC):
                    u = TURNS + f
                    bank_free(u)
                    for r in range(DC):
                        ins = pe.transpose(row_bank[u % 2][:, P * r:P * (r + 1)], w_out_raw[:, r, P * f:P * (f + 1)], ident[:, :])
                    ins.then_inc(row_done, 1)
                for f in range(DC):
                    u = CONTEXTS + f
                    bank_free(u)
                    pe.wait_ge(key_ready, DC)
                    for t in range(NT):
                        ins = pe.matmul(row_bank[u % 2][:, 0:P], value[:, t, P * f:P * (f + 1)], key[:, t, P * f:P * (f + 1)],
                                        start=(t == 0), stop=(t == NT - 1))
                    ins.then_inc(row_done, 1)
                for f in range(DC):
                    u = PRODUCTS + f
                    pe.wait_ge(row_ready, DC + f + 1)
                    bank_free(u)
                    for n, (x, y) in enumerate(PARTS):
                        ins = pe.matmul(row_bank[u % 2][:, :], context[x][:, f, :], wt[2][y][:, f, :], start=(n == 0), stop=(n == 2))
                    ins.then_inc(row_done, 1)

            @block.sync
            def _(sp):
                sp.wait_ge(w_out_loaded, 16)

        with ExitStack() as ctx:
            b = Buffers(nc, ctx)
            query = [b.sb(f"m_query{i}", [TOK, FEAT]) for i in range(2)]
            top = b.sb("m_top", [TOK, 2, MIX_HEADS])
            total = b.sb("m_total", [TOK, 2, MIX_HEADS])
            query_t = [b.sb(f"m_query_t_{k}", [P, DC, TOK], F32R) for k in ("hi", "lo")]
            out_row = [b.sb(f"m_out_row{i}", [TOK, D]) for i in range(2)]
            query_bank = [b.ps(f"m_query_bank{i}", [P, 512]) for i in range(2)]
            turn_bank = b.ps("m_turn_bank", [P, 512])
            out_bank = [b.ps(f"m_out_bank{i}", [P, 512]) for i in range(2)]
            query_done = b.sem("m_query_done")
            centred = b.sem("m_centred")
            exp_done = b.sem("m_exp_done2")
            query_ready = b.sem("m_query_ready")
            turned = b.sem("m_turned2")
            turn_hi = b.sem("m_turn_hi")
            turn_ready = b.sem("m_turn_ready")
            out_done = b.sem("m_out_done")
            out_copied = b.sem("m_out_copied")
            stored = [b.sem(f"m_stored{i}") for i in range(2)]
            dve_step = b.sem("m_dve_step3")
            block = ctx.enter_context(nc.Block())

            def heads(ap):
                return ap.rearrange("p (h e) -> p h e", h=MIX_HEADS)

            def spread(ap):
                return ap.unsqueeze(2).to_broadcast([TOK, MIX_HEADS, MIX_DIM])

            @block.sync
            def _(sp):
                for t in range(NT):
                    sp.wait_ge(out_copied, t + 1)
                    sp.dma_start(mixed[TOK * t:TOK * (t + 1), :], out_row[t % 2][:, :]).then_inc(stored[t % 2], 16)
                for i in range(2):
                    sp.wait_ge(stored[i], 16 * NT // 2)

            @block.scalar
            def _(act):
                def out(t):
                    act.wait_ge(out_done, t + 1)
                    if t >= 2:
                        act.wait_ge(stored[t % 2], 16 * (t // 2))
                    act.activation(out_row[t % 2][:, :], out_bank[t % 2][0:TOK, :], ACT.Copy).then_inc(out_copied, 1)

                for t in range(NT):
                    act.wait_ge(centred, t + 1)
                    act.activation(query[t % 2][:, :], query[t % 2][:, :], ACT.Exp).then_inc(exp_done, 1)
                    act.wait_ge(turned, t + 1)
                    act.activation(query_t[0][:, :, :].rearrange("p c n -> p (c n)"), turn_bank[:, 0:4 * TOK],
                                   ACT.Copy).then_inc(turn_hi, 1)
                    if t:
                        out(t - 1)
                out(NT - 1)

            @block.vector
            def _(dve):
                link = chain(dve, dve_step)

                def centre(t):
                    dve.wait_ge(query_done, t + 1)
                    link(dve.tensor_reduce(top[:, t % 2, :], heads(query_bank[t % 2][0:TOK, :]), AX.X, ALU.max))
                    dve.tensor_tensor(heads(query[t % 2][:, :]), heads(query_bank[t % 2][0:TOK, :]), spread(top[:, t % 2, :]),
                                      ALU.subtract).then_inc(centred, 1)

                centre(0)
                for t in range(NT):
                    dve.wait_ge(exp_done, t + 1)
                    link(dve.tensor_reduce(total[:, t % 2, :], heads(query[t % 2][:, :]), AX.X, ALU.add))
                    link(dve.reciprocal(total[:, t % 2, :], total[:, t % 2, :]))
                    dve.tensor_tensor(heads(query[t % 2][:, :]), heads(query[t % 2][:, :]), spread(total[:, t % 2, :]),
                                      ALU.mult).then_inc(query_ready, 1)
                    if t + 1 < NT:
                        centre(t + 1)
                    dve.wait_ge(turn_hi, t + 1)
                    dve.tensor_tensor(query_t[1][:, :, :].rearrange("p c n -> p (c n)"), turn_bank[:, 0:4 * TOK],
                                      query_t[0][:, :, :].rearrange("p c n -> p (c n)").bitcast(F32),
                                      ALU.subtract).then_inc(turn_ready, 1)

            @block.tensor
            def _(pe):
                def queries(t):
                    if t >= 2:
                        pe.wait_ge(centred, t - 1)
                    for c in range(DC):
                        for n, (x, y) in enumerate(PARTS):
                            ins = pe.matmul(query_bank[t % 2][0:TOK, :], xm_t[x][:, c, TOK * t:TOK * (t + 1)],
                                            wt[0][y][:, c, :], start=(c == 0 and n == 0), stop=(c == DC - 1 and n == 2))
                    ins.then_inc(query_done, 1)

                def outs(t):
                    pe.wait_ge(turn_ready, t + 1)
                    if t >= 2:
                        pe.wait_ge(out_copied, t - 1)
                    for f in range(DC):
                        for n, (x, y) in enumerate(PARTS):
                            ins = pe.matmul(out_bank[t % 2][0:TOK, :], query_t[x][:, f, :], wt[1][y][:, f, :],
                                            start=(f == 0 and n == 0), stop=(f == DC - 1 and n == 2))
                    ins.then_inc(out_done, 1)

                queries(0)
                queries(1)
                for t in range(NT):
                    pe.wait_ge(query_ready, t + 1)
                    for f in range(DC):
                        ins = pe.transpose(turn_bank[:, TOK * f:TOK * (f + 1)], query[t % 2][:, P * f:P * (f + 1)],
                                           ident[0:TOK, 0:TOK])
                    ins.then_inc(turned, 1)
                    if t + 2 < NT:
                        queries(t + 2)
                    outs(t)


def stage_join(nc, x, hidden, mixed, gamma, beta, out_gamma, w_gate, ident, x1, xn2, route, slots_in):
    scatter_at, gather_at, weight, select_t, some, none = route
    E = EXPERTS
    with ExitStack() as ctx:
        b = Buffers(nc, ctx)
        rows = [b.sb(f"j_{k}", [TOK, NT, D]) for k in ("hidden", "mixed")]
        vec = [b.sb(f"j_vec{i}", [TOK, D]) for i in range(3)]
        stats = b.sb("j_stats", [TOK, 3, NT, 6])
        mean_var = b.sb("j_mean_var", [TOK, 3, NT, 2])
        root_in = b.sb("j_root_in", [TOK, 3, NT])
        root = b.sb("j_root", [TOK, 3, NT])
        scratch = b.sb("j_scratch", [TOK, 3, NT])
        rstd = b.sb("j_rstd", [TOK, 3, NT])
        zero = b.sb("j_zero", [CAP, D])
        xn2_t = b.sb("j_xn2_t", [P, DC, N])
        gate_w = b.sb("j_gate_w", [P, DC, E])
        before = b.sb("j_before", [TOK, TOK], BF16)
        ones = b.sb("j_ones", [TOK, TOK], BF16)
        expert_no = b.sb("j_expert_no", [TOK, E])
        dump = b.sb("j_dump", [TOK, TOPK, NT])
        prob = b.sb("j_prob", [TOK, NT, E])
        left = b.sb("j_left", [TOK, NT, E])
        same = b.sb("j_same", [TOK, NT, E])
        hot = b.sb("j_hot", [TOK, TOPK, NT, E])
        taken = b.sb("j_taken", [TOK, NT, E], BF16)
        best = b.sb("j_best", [TOK, TOPK, NT])
        expert = b.sb("j_expert", [TOK, TOPK, NT])
        rank = b.sb("j_rank", [TOK, TOPK, NT])
        keep = b.sb("j_keep", [TOK, TOPK, NT])
        dest = b.sb("j_dest", [TOK, TOPK, NT])
        place = b.sb("j_place", [TOK, TOPK, NT])
        norm = b.sb("j_norm", [TOK, NT])
        bank = [b.ps(f"j_bank{i}", [P, 512]) for i in range(4)]
        logit = b.ps("j_logit", [P, 512])
        rank_bank = b.ps("j_rank_bank", [P, 512])
        loaded = [b.sem(f"j_loaded{i}") for i in range(3)]
        vec_loaded = b.sem("j_vec_loaded")
        gate_loaded = b.sem("j_gate_loaded")
        consts = b.sem("j_consts")
        zero_ready = b.sem("j_zero_ready")
        cleared = b.sem("j_cleared")
        dve_step = b.sem("j_dve_step")
        var_ready = b.sem("j_var_ready")
        root_ready = b.sem("j_root_ready")
        normed = b.sem("j_normed")
        base_ready = b.sem("j_base_ready")
        pool_step = b.sem("j_pool_step")
        row_ready = b.sem("j_row_ready")
        turned = b.sem("j_turned")
        copied = b.sem("j_copied")
        gated = b.sem("j_gated")
        centred = b.sem("j_centred")
        exp_done = b.sem("j_exp_done")
        taken_ready = b.sem("j_taken_ready")
        ranked = b.sem("j_ranked")
        places_ready = b.sem("j_places_ready")
        select_ready = b.sem("j_select_ready")
        scattered = b.sem("j_scattered")
        block = ctx.enter_context(nc.Block())
        units = [(g, c) for g in range(3) for c in range(DC)]

        def tiles(dram):
            return dram.rearrange("(t p) c -> p t c", p=TOK)

        def over_experts(ap):
            return ap.unsqueeze(2).to_broadcast([TOK, NT, E])

        @block.sync
        def _(sp):
            sp.dma_start(rows[0][:, :, :], tiles(hidden)).then_inc(loaded[0], 16)
            sp.dma_start(rows[1][:, :, :], tiles(mixed)).then_inc(loaded[1], 16)
            sp.dma_start(x1[:, :, :], tiles(x)).then_inc(loaded[2], 16)
            for i, v in enumerate((gamma, beta, out_gamma)):
                sp.dma_start(vec[i][:, :], v.unsqueeze(0).to_broadcast([TOK, D])).then_inc(vec_loaded, 16)
            sp.dma_start(gate_w[:, :, :], w_gate.rearrange("(c p) e -> p c e", p=P)).then_inc(gate_loaded, 16)
            sp.wait_ge(zero_ready, 1)
            sp.dma_start(slots_in[0:SLOTS, :].rearrange("(e p) c -> p e c", p=CAP),
                         zero[:, :].unsqueeze(1).to_broadcast([CAP, E, D])).then_inc(cleared, 16)

        @block.gpsimd
        def _(pool):
            pool.memset(zero[:, :], 0.0).then_inc(zero_ready, 1)
            pool.memset(ones[:, :], 1.0).then_inc(consts, 1)
            pool.iota(expert_no[:, :], [[1, E]], base=-E, channel_multiplier=0,
                      allow_small_or_imprecise_dtypes=True).then_inc(consts, 1)
            pool.iota(dump[:, :, :], [[N, TOPK], [TOK, NT]], base=SLOTS, channel_multiplier=1,
                      allow_small_or_imprecise_dtypes=True).then_inc(consts, 1)
            pool.wait_ge(consts, 3)
            pool.affine_select(out=before[:, :], in_=ones[:, :], compare_op=ALU.is_gt, fill=0.0, base=0,
                               pattern=[[1, TOK]], channel_multiplier=-1).then_inc(consts, 1)
            pool.wait_ge(vec_loaded, 48)
            pool.wait_ge(loaded[2], 16)
            steps = 0
            for t in range(NT):
                pool.wait_ge(normed, t + 1)
                for out, other, op in ((rows[1], vec[2][:, :], ALU.mult), (x1, vec[1][:, :], ALU.add), (x1, rows[1][:, t, :], ALU.add)):
                    pool.tensor_tensor(out[:, t, :], out[:, t, :], other, op).then_inc(pool_step, 1)
                    steps += 1
                    pool.wait_ge(pool_step, steps)
                pool.sem_inc(base_ready, 1)
            pool.wait_ge(cleared, 16)
            pool.wait_ge(places_ready, 1)
            for k in range(TOPK):
                for t in range(NT):
                    pool.indirect_dma_start(
                        out=slots_in[:, :],
                        out_offset=bass.IndirectOffsetOnAxis(ap=scatter_at[:, k * NT + t:k * NT + t + 1], axis=0),
                        in_=xn2[:, t, :], in_offset=None).then_inc(scattered, 16)
            pool.wait_ge(scattered, 16 * TOPK * NT)

        @block.scalar
        def _(act):
            act.wait_ge(var_ready, 1)
            act.activation(root[:, 0:2, :], root_in[:, 0:2, :], ACT.Sqrt).then_inc(root_ready, 1)
            act.wait_ge(var_ready, 2)
            act.activation(root[:, 2, :], root_in[:, 2, :], ACT.Sqrt).then_inc(root_ready, 1)
            for u, (g, c) in enumerate(units):
                n = TOK * len(tile_parts(g))
                act.wait_ge(turned, u + 1)
                act.activation(xn2_t[:, c, 500 * g:500 * g + n], bank[u % 4][:, 0:n], ACT.Copy).then_inc(copied, 1)
            act.wait_ge(centred, 1)
            act.activation(prob[:, :, :], prob[:, :, :], ACT.Exp).then_inc(exp_done, 1)
            for t in range(NT):
                act.wait_ge(turned, len(units) + t + 1)
                act.activation(select_t[:, TOK * t:TOK * (t + 1)], bank[t % 4][0:E, 0:TOK], ACT.Copy).then_inc(copied, 1)

        @block.vector
        def _(dve):
            link = chain(dve, dve_step)

            def moments(i, source):
                for t in range(NT):
                    ins = dve.bn_stats(stats[:, i, t, :], source[:, t, :])
                link(ins)
                for t in range(NT):
                    ins = dve.bn_aggr(mean_var[:, i, t, :], stats[:, i, t, :])
                link(ins)
                return dve.tensor_scalar(root_in[:, i, :], mean_var[:, i, :, 1], EPS, None, ALU.add)

            for i in range(2):
                dve.wait_ge(loaded[i], 16)
                ins = moments(i, rows[i])
            ins.then_inc(var_ready, 1)
            dve.wait_ge(root_ready, 1)
            for i in (1, 0):
                inverse_root(dve, link, root_in[:, i, :], root[:, i, :], scratch[:, i, :], rstd[:, i, :])
                for t in range(NT):
                    ins = dve.tensor_scalar(rows[i][:, t, :], rows[i][:, t, :], mean_var[:, i, t, 0:1], rstd[:, i, t:t + 1],
                                            ALU.subtract, ALU.mult)
                    if i == 1:
                        ins.then_inc(normed, 1)
                if i == 0:
                    link(ins)
            dve.wait_ge(vec_loaded, 48)
            for t in range(NT):
                ins = dve.tensor_tensor(rows[0][:, t, :], rows[0][:, t, :], vec[0][:, :], ALU.mult)
            link(ins)
            for t in range(NT):
                dve.wait_ge(base_ready, t + 1)
                ins = dve.tensor_tensor(x1[:, t, :], x1[:, t, :], rows[0][:, t, :], ALU.add)
            link(ins)
            moments(2, x1).then_inc(var_ready, 1)
            dve.wait_ge(root_ready, 2)
            inverse_root(dve, link, root_in[:, 2, :], root[:, 2, :], scratch[:, 2, :], rstd[:, 2, :])
            for t in range(NT):
                dve.tensor_scalar(xn2[:, t, :], x1[:, t, :], mean_var[:, 2, t, 0:1], rstd[:, 2, t:t + 1],
                                  ALU.subtract, ALU.mult).then_inc(row_ready, 1)

            dve.wait_ge(gated, 1)
            dve.wait_ge(consts, 4)
            logits = logit[0:TOK, 0:NT * E].rearrange("p (t e) -> p t e", e=E)
            link(dve.tensor_reduce(norm[:, :], logits, AX.X, ALU.max))
            dve.tensor_tensor(prob[:, :, :], logits, over_experts(norm[:, :]), ALU.subtract).then_inc(centred, 1)
            dve.wait_ge(exp_done, 1)
            link(dve.tensor_reduce(norm[:, :], prob[:, :, :], AX.X, ALU.add))
            link(dve.reciprocal(norm[:, :], norm[:, :]))
            link(dve.tensor_tensor(prob[:, :, :], prob[:, :, :], over_experts(norm[:, :]), ALU.mult))
            number = expert_no[:, :].unsqueeze(1).to_broadcast([TOK, NT, E])
            for k in range(TOPK):
                source = (prob, left)[k]
                link(dve.tensor_reduce(best[:, k, :], source[:, :, :], AX.X, ALU.max))
                link(dve.tensor_tensor(same[:, :, :], source[:, :, :], over_experts(best[:, k, :]), ALU.is_equal))
                link(dve.tensor_tensor(same[:, :, :], same[:, :, :], number, ALU.mult))
                link(dve.tensor_reduce(expert[:, k, :], same[:, :, :], AX.X, ALU.min))
                link(dve.tensor_tensor(hot[:, k, :, :], over_experts(expert[:, k, :]), number, ALU.is_equal))
                if k == 0:
                    link(dve.scalar_tensor_tensor(left[:, :, :], hot[:, 0, :, :], -2.0, prob[:, :, :], ALU.mult, ALU.add))
            dve.tensor_tensor(taken[:, :, :], hot[:, 0, :, :], hot[:, 1, :, :], ALU.add).then_inc(taken_ready, 1)
            link(dve.tensor_tensor(norm[:, :], best[:, 0, :], best[:, 1, :], ALU.add))
            link(dve.tensor_scalar(norm[:, :], norm[:, :], 1e-9, None, ALU.max))
            link(dve.reciprocal(norm[:, :], norm[:, :]))
            dve.wait_ge(ranked, 1)
            ranks = rank_bank[0:TOK, 0:NT * E].rearrange("p (t e) -> p t e", e=E)
            for k in range(TOPK):
                link(dve.tensor_tensor(same[:, :, :], hot[:, k, :, :], ranks, ALU.mult))
                link(dve.tensor_reduce(rank[:, k, :], same[:, :, :], AX.X, ALU.add))
            dve.tensor_scalar(keep[:, :, :], rank[:, :, :], float(CAP), None, ALU.is_lt)
            link(dve.scalar_tensor_tensor(dest[:, :, :], expert[:, :, :], float(CAP), rank[:, :, :], ALU.mult, ALU.add))
            link(dve.tensor_scalar(dest[:, :, :], dest[:, :, :], float(E * CAP), None, ALU.add))
            link(dve.tensor_tensor(place[:, :, :], dest[:, :, :], dump[:, :, :], ALU.subtract))
            link(dve.tensor_tensor(place[:, :, :], place[:, :, :], keep[:, :, :], ALU.mult))
            link(dve.tensor_tensor(place[:, :, :], place[:, :, :], dump[:, :, :], ALU.add))
            dve.tensor_copy(scatter_at[:, :], place[:, :, :].rearrange("p k t -> p (k t)")).then_inc(places_ready, 1)
            dve.wait_ge(places_ready, 1)
            link(dve.scalar_tensor_tensor(place[:, :, :], dest[:, :, :], -float(SLOTS - 1), keep[:, :, :], ALU.add, ALU.mult))
            link(dve.tensor_scalar(place[:, :, :], place[:, :, :], float(SLOTS - 1), None, ALU.add))
            link(dve.tensor_copy(gather_at[:, :], place[:, :, :].rearrange("p k t -> p (k t)")))
            link(dve.tensor_tensor(weight[:, :, :], best[:, :, :], norm[:, :].unsqueeze(1).to_broadcast([TOK, TOPK, NT]), ALU.mult))
            link(dve.tensor_tensor(weight[:, :, :], weight[:, :, :], keep[:, :, :], ALU.mult))
            link(dve.tensor_tensor(norm[:, :], weight[:, 0, :], weight[:, 1, :], ALU.add))
            dve.tensor_scalar(none[:, :], norm[:, :], 1e-12, None, ALU.is_le)
            link(dve.tensor_scalar(some[:, :], norm[:, :], 1e-12, None, ALU.is_gt))
            for k in range(TOPK):
                link(dve.tensor_tensor(hot[:, k, :, :], hot[:, k, :, :], over_experts(weight[:, k, :]), ALU.mult))
            dve.tensor_tensor(same[:, :, :], hot[:, 0, :, :], hot[:, 1, :, :], ALU.add).then_inc(select_ready, 1)

        @block.tensor
        def _(pe):
            for u, (g, c) in enumerate(units):
                if u >= 4:
                    pe.wait_ge(copied, u - 3)
                pe.wait_ge(row_ready, tile_parts(g)[-1] + 1)
                for i, t in enumerate(tile_parts(g)):
                    ins = pe.transpose(bank[u % 4][:, TOK * i:TOK * (i + 1)], xn2[:, t, P * c:P * (c + 1)],
                                       ident[0:TOK, 0:TOK])
                ins.then_inc(turned, 1)
            pe.wait_ge(gate_loaded, 16)
            pe.wait_ge(copied, len(units))
            for t in range(NT):
                for c in range(DC):
                    ins = pe.matmul(logit[0:TOK, E * t:E * (t + 1)], xn2_t[:, c, TOK * t:TOK * (t + 1)], gate_w[:, c, :],
                                    start=(c == 0), stop=(c == DC - 1))
            ins.then_inc(gated, 1)
            pe.wait_ge(taken_ready, 1)
            for t in range(NT):
                for s in range(t + 1):
                    ins = pe.matmul(rank_bank[0:TOK, E * t:E * (t + 1)], (before if s == t else ones)[:, :], taken[:, s, :],
                                    start=(s == 0), stop=(s == t))
            ins.then_inc(ranked, 1)
            pe.wait_ge(select_ready, 1)
            for t in range(NT):
                if t >= 4:
                    pe.wait_ge(copied, len(units) + t - 3)
                pe.transpose(bank[t % 4][0:E, 0:TOK], same[:, t, :], ident[0:TOK, 0:TOK]).then_inc(turned, 1)


def stage_experts(nc, slots_in, slots_out, w1, b1, w2, ident):
    E = EXPERTS
    with ExitStack() as ctx:
        b = Buffers(nc, ctx)
        up = [b.sb(f"e_up{i}", [P, DC, D]) for i in range(2)]
        down = [b.sb(f"e_down{i}", [P, DC, D]) for i in range(2)]
        rows = [b.sb(f"e_rows{i}", [CAP, D]) for i in range(2)]
        rows_t = [b.sb(f"e_rows_t{i}", [P, DC, CAP]) for i in range(2)]
        mid_t = [b.sb(f"e_mid_t{i}", [P, DC, CAP]) for i in range(2)]
        out = [b.sb(f"e_out{i}", [CAP, D]) for i in range(2)]
        bias_in = b.sb("e_bias_in", [E, D])
        bias_t = b.sb("e_bias_t", [P, DC, E])
        turn_bank = [b.ps(f"e_turn_bank{i}", [P, 512]) for i in range(2)]
        mid_bank = [b.ps(f"e_mid_bank{i}", [P, 512]) for i in range(2)]
        out_bank = [b.ps(f"e_out_bank{i}", [P, 512]) for i in range(2)]
        bias_loaded = b.sem("e_bias_loaded")
        bias_turned = b.sem("e_bias_turned")
        bias_ready = b.sem("e_bias_ready")
        up_loaded = [b.sem(f"e_up_loaded{i}") for i in range(2)]
        down_loaded = [b.sem(f"e_down_loaded{i}") for i in range(2)]
        rows_loaded = [b.sem(f"e_rows_loaded{i}") for i in range(2)]
        stored = [b.sem(f"e_stored{i}") for i in range(2)]
        turned = b.sem("e_turned")
        rows_ready = b.sem("e_rows_ready")
        mid_done = b.sem("e_mid_done")
        mid_ready = b.sem("e_mid_ready")
        out_done = b.sem("e_out_done")
        out_ready = b.sem("e_out_ready")
        block = ctx.enter_context(nc.Block())


        @block.sync
        def _(sp):
            sp.dma_start(bias_in[:, :], b1).then_inc(bias_loaded, 16)
            with sp.Fori(0, E // 2) as i:
                for k in range(2):
                    e = 2 * i + k
                    sp.wait_ge(turned, e + 1)
                    sp.dma_start(rows[k][:, :], slots_in[bass.ds(e * CAP, CAP), :]).then_inc(rows_loaded[k], 16)
                    sp.wait_ge(mid_done, e + 1)
                    sp.dma_start(up[k][:, :, :], w1[bass.ds(e, 1), :, :].rearrange("o (c p) n -> p (o c) n", p=P)
                                 ).then_inc(up_loaded[k], 16)
                    sp.wait_ge(out_done, e + 1)
                    sp.dma_start(down[k][:, :, :], w2[bass.ds(e, 1), :, :].rearrange("o (c p) n -> p (o c) n", p=P)
                                 ).then_inc(down_loaded[k], 16)

        @block.scalar
        def _(act):
            def rows_out(i, k):
                act.wait_ge(turned, 2 * i + k + 3)
                act.activation(rows_t[k][:, :, :].rearrange("p c n -> p (c n)"), turn_bank[k][:, 0:DC * CAP],
                               ACT.Copy).then_inc(rows_ready, 1)

            rows_out(0, 0)
            act.sem_inc(stored[0], 16)
            act.sem_inc(stored[1], 16)

            def expert(i, k, last):
                if not last:
                    rows_out(i + (k == 1), 1 - k)
                act.wait_ge(out_done, 2 * i + k + 3)
                act.wait_ge(stored[k], 16 * i + 16)
                act.activation(out[k][:, :], out_bank[k][0:CAP, :], ACT.Copy).then_inc(out_ready, 1)
                act.wait_ge(out_ready, 2 * i + k + 3)
                act.dma_start(slots_out[bass.ds((2 * i + k) * CAP, CAP), :], out[k][:, :]).then_inc(stored[k], 16)

            with act.Fori(0, E // 2 - 1) as i:
                expert(i, 0, False)
                expert(i, 1, False)
            expert(E // 2 - 1, 0, False)
            expert(E // 2 - 1, 1, True)
            for k in range(2):
                act.wait_ge(stored[k], 16 * (E // 2 + 1))

        @block.vector
        def _(dve):
            dve.wait_ge(bias_turned, 1)
            dve.tensor_copy(bias_t[:, :, :].rearrange("p c e -> p (c e)"), turn_bank[1][:, 0:DC * E]).then_inc(bias_ready, 1)
            dve.wait_ge(bias_ready, 1)
            with dve.Fori(0, E // 2) as i:
                for k in range(2):
                    e = 2 * i + k
                    dve.wait_ge(mid_done, e + 3)
                    for c in range(DC):
                        ins = dve.tensor_scalar(mid_t[k][:, c, :], mid_bank[k][:, CAP * c:CAP * (c + 1)],
                                                bias_t[:, c, bass.ds(e, 1)], 0.0, ALU.add, ALU.max)
                    ins.then_inc(mid_ready, 1)

        @block.tensor
        def _(pe):
            pe.wait_ge(bias_loaded, 16)
            for c in range(DC):
                ins = pe.transpose(turn_bank[1][:, E * c:E * (c + 1)], bias_in[:, P * c:P * (c + 1)], ident[0:E, 0:E])
            ins.then_inc(bias_turned, 1)
            pe.sem_inc(turned, 2)
            pe.sem_inc(mid_done, 2)
            pe.sem_inc(out_done, 2)
            pe.sem_inc(out_ready, 2)

            def turn(i, k):
                pe.wait_ge(rows_loaded[k], 16 * i + 16)
                for c in range(DC):
                    ins = pe.transpose(turn_bank[k][:, CAP * c:CAP * (c + 1)], rows[k][:, P * c:P * (c + 1)], ident[0:CAP, 0:CAP])
                ins.then_inc(turned, 1)

            def expert(i, k, last):
                e = 2 * i + k
                pe.wait_ge(rows_ready, e + 1)
                pe.wait_ge(up_loaded[k], 16 * i + 16)
                for h in range(DC):
                    for c in range(DC):
                        ins = pe.matmul(mid_bank[k][:, CAP * h:CAP * (h + 1)], up[k][:, c, P * h:P * (h + 1)],
                                        rows_t[k][:, c, :], start=(c == 0), stop=(c == DC - 1))
                ins.then_inc(mid_done, 1)
                if not last:
                    turn(i + (k == 1), 1 - k)
                pe.wait_ge(mid_ready, e + 1)
                pe.wait_ge(down_loaded[k], 16 * i + 16)
                pe.wait_ge(out_ready, e + 1)
                for h in range(DC):
                    ins = pe.matmul(out_bank[k][0:CAP, :], mid_t[k][:, h, :], down[k][:, h, :], start=(h == 0), stop=(h == DC - 1))
                ins.then_inc(out_done, 1)

            pe.wait_ge(bias_ready, 1)
            turn(0, 0)
            with pe.Fori(0, E // 2 - 1) as i:
                expert(i, 0, False)
                expert(i, 1, False)
            expert(E // 2 - 1, 0, False)
            expert(E // 2 - 1, 1, True)


def stage_combine(nc, slots_out, b2, x1, xn2, route, out):
    _, gather_at, weight, select_t, some, none = route
    with ExitStack() as ctx:
        b = Buffers(nc, ctx)
        got = [b.sb(f"o_got{k}", [TOK, NT, D]) for k in range(TOPK)]
        bias = b.sb("o_bias", [EXPERTS, D])
        bank = [b.ps(f"o_bank{i}", [P, 512]) for i in range(4)]
        bias_loaded = b.sem("o_bias_loaded")
        gathered = [b.sem(f"o_gathered{t}") for t in range(NT)]
        biased = b.sem("o_biased")
        first = b.sem("o_first")
        both = b.sem("o_both")
        kept = b.sem("o_kept")
        row_ready = b.sem("o_row_ready")
        stored = b.sem("o_stored")
        block = ctx.enter_context(nc.Block())

        @block.sync
        def _(sp):
            sp.dma_start(bias[:, :], b2).then_inc(bias_loaded, 16)
            for t in range(NT):
                sp.wait_ge(row_ready, t + 1)
                sp.dma_start(out[TOK * t:TOK * (t + 1), :], x1[:, t, :]).then_inc(stored, 16)
            sp.wait_ge(stored, 16 * NT)

        @block.gpsimd
        def _(pool):
            for t in range(NT):
                for k in range(TOPK):
                    pool.indirect_dma_start(
                        out=got[k][:, t, :], out_offset=None, in_=slots_out[:, :],
                        in_offset=bass.IndirectOffsetOnAxis(ap=gather_at[:, k * NT + t:k * NT + t + 1], axis=0)
                    ).then_inc(gathered[t], 16)

        @block.tensor
        def _(pe):
            pe.wait_ge(bias_loaded, 16)
            for t in range(NT):
                if t >= 4:
                    pe.wait_ge(first, t - 3)
                pe.matmul(bank[t % 4][0:TOK, :], select_t[:, TOK * t:TOK * (t + 1)], bias[:, :], start=True,
                          stop=True).then_inc(biased, 1)

        @block.vector
        def _(dve):
            for t in range(NT):
                dve.scalar_tensor_tensor(x1[:, t, :], xn2[:, t, :], none[:, t:t + 1], x1[:, t, :], ALU.mult,
                                         ALU.add).then_inc(kept, 1)
            for t in range(NT):
                dve.wait_ge(gathered[t], 32)
                dve.wait_ge(biased, t + 1)
                dve.scalar_tensor_tensor(got[0][:, t, :], got[0][:, t, :], weight[:, 0, t:t + 1], bank[t % 4][0:TOK, :],
                                         ALU.mult, ALU.add).then_inc(first, 1)
                dve.wait_ge(first, t + 1)
                dve.scalar_tensor_tensor(got[1][:, t, :], got[1][:, t, :], weight[:, 1, t:t + 1], got[0][:, t, :],
                                         ALU.mult, ALU.add).then_inc(both, 1)
                dve.wait_ge(both, t + 1)
                dve.wait_ge(kept, t + 1)
                dve.scalar_tensor_tensor(x1[:, t, :], got[1][:, t, :], some[:, t:t + 1], x1[:, t, :], ALU.mult,
                                         ALU.add).then_inc(row_ready, 1)


def gps_layer(nc, x, src, dst, gnn, mix, ffn, out):
    counts = nc.dram_tensor("counts_dram", (N, NS), U16, kind="Internal").ap()
    fold_dram = [nc.dram_tensor(f"fold_{k}_dram", (HEADS * DC, P, D), F32, kind="Internal").ap() for k in ("hi", "lo")]
    hidden = nc.dram_tensor("hidden_dram", (N, D), F32, kind="Internal").ap()
    mixed = nc.dram_tensor("mixed_dram", (N, D), F32, kind="Internal").ap()
    slots_in = nc.dram_tensor("slots_in_dram", (SLOTS + TOPK * N, D), F32, kind="Internal").ap()
    slots_out = nc.dram_tensor("slots_out_dram", (SLOTS, D), F32, kind="Internal").ap()
    Buffers.used.clear()
    with ExitStack() as ctx:
        b = Buffers(nc, ctx)
        ident = b.sb("ident", [P, P])
        with ExitStack() as nodes:
            b_nodes = Buffers(nc, nodes)
            xnT = [b_nodes.sb(f"xnT_{k}", [P, DC, NS], F32R) for k in ("hi", "lo")]
            with ExitStack() as rows:
                xrow = Buffers(nc, rows).sb("xrow", [TOK, NT, D])
                stage_norm(nc, x, ident, xnT[0], xnT[1], xrow)
                stage_mix(nc, xrow, ident, mix["w_qkv"], mix["w_out"], mix["norm_gamma"], mixed)
            stage_count(nc, src, dst, ident, counts)
            fold_bias = b_nodes.sb("fold_bias", [P, HEADS, DC])
            row_shift = b_nodes.sb("row_shift", [TOK, NT, HEADS])
            skip_bias = b_nodes.sb("skip_bias", [P, HEADS * DC])
            stage_fold(nc, gnn["Wq"], gnn["Wk"], (gnn["bq"], gnn["bk"], gnn["bskip"]), ident, xnT[0], xnT[1],
                       fold_dram[0], fold_dram[1], fold_bias, row_shift, skip_bias)
            Buffers.reset(nc)
            stage_attend(nc, xnT, counts, fold_dram, fold_bias, row_shift, skip_bias, ident,
                         gnn["Wv"], gnn["bv"], gnn["Wskip"], gnn["Wlin"], gnn["blin"], hidden)
        x1 = b.sb("x1", [TOK, NT, D])
        xn2 = b.sb("xn2", [TOK, NT, D])
        route = (b.sb("scatter_at", [TOK, TOPK * NT], U32), b.sb("gather_at", [TOK, TOPK * NT], U32),
                 b.sb("weight", [TOK, TOPK, NT]), b.sb("select_t", [EXPERTS, N]),
                 b.sb("some", [TOK, NT]), b.sb("none", [TOK, NT]))
        stage_join(nc, x, hidden, mixed, gnn["gamma"], gnn["beta"], mix["out_gamma"], ffn["Wg"], ident, x1, xn2,
                   route, slots_in)
        stage_experts(nc, slots_in, slots_out, ffn["W1"], ffn["b1"], ffn["W2"], ident)
        stage_combine(nc, slots_out, ffn["b2"], x1, xn2, route, out)


def kernel(**inputs):
    import concourse.bacc as bacc
    from concourse.bass_utils import run_bass_kernel_spmd

    nc = bacc.Bacc("TRN2", target_bir_lowering=False, num_devices=1)
    arrays, aps = {}, {}
    for name, a in inputs.items():
        arrays[f"in_{name}"] = np.ascontiguousarray(a)
        aps[name] = nc.dram_tensor(f"in_{name}", a.shape, mybir.dt.from_np(a.dtype), kind="ExternalInput").ap()
    out = nc.dram_tensor("out", (N, D), F32, kind="ExternalOutput").ap()

    def part(prefix):
        return {name[len(prefix):]: ap for name, ap in aps.items() if name.startswith(prefix)}

    gps_layer(nc, aps["x"], aps["src"], aps["dst"], part("L0_gnn_"), part("L0_mix_"), part("L0_ffn_"), out)
    result = run_bass_kernel_spmd(nc, [arrays], core_ids=[0])
    return result.results[0]["out"]
```

```python
from contextlib import ExitStack

import numpy as np

import concourse.bass as bass
from concourse import mybir

F32 = mybir.dt.float32
F32R = mybir.dt.float32r
F16 = mybir.dt.float16
BF16 = mybir.dt.bfloat16
I32 = mybir.dt.int32
U32 = mybir.dt.uint32
U16 = mybir.dt.uint16
ALU = mybir.AluOpType
ACT = mybir.ActivationFunctionType
AX = mybir.AxisListType

P = 128
N = 1250
TOK = 125
NT = N // TOK
D = 512
DC = D // P
HEADS = 4
BW = 418
NB = 3
NS = BW * NB
GRP = 2 * TOK
NG = N // GRP
EDGES = 41250
EB = 375
NEB = EDGES // EB
SUB = EB // TOK
EPS = 1e-5
FAR = 1.0e30
MIX_HEADS, MIX_DIM = 8, 64
EXPERTS = 32
CAP = 98
SLOTS = EXPERTS * CAP
TOPK = 2


class Buffers:

    used = []

    def __init__(self, nc, ctx):
        self.nc, self.ctx = nc, ctx

    def sb(self, name, shape, dt=F32):
        return self.ctx.enter_context(self.nc.sbuf_tensor(name, shape, dt))

    def ps(self, name, shape, dt=F32):
        return self.ctx.enter_context(self.nc.psum_tensor(name, shape, dt))

    def sem(self, name):
        self.used.append(self.nc.alloc_semaphore(name))
        return self.used[-1]

    @classmethod
    def reset(cls, nc):
        nc.clear_and_free_semaphores(list(cls.used))
        cls.used.clear()
        nc.all_engine_barrier()


def chain(engine, sem):
    done = [0]

    def link(ins):
        done[0] += 1
        ins.then_inc(sem, 1)
        engine.wait_ge(sem, done[0])

    return link


def tile_parts(g):
    return range(4 * g, min(4 * g + 4, NT))


def node_stats(dve, link, source, stats, mean_var, root_in):
    for t in range(NT):
        ins = dve.bn_stats(stats[:, t, :], source[:, t, :])
    link(ins)
    for t in range(NT):
        ins = dve.bn_aggr(mean_var[:, t, :], stats[:, t, :])
    link(ins)
    return dve.tensor_scalar(root_in[:, :], mean_var[:, :, 1], EPS, None, ALU.add)


def inverse_root(dve, link, root_in, root, scratch, rstd):
    link(dve.reciprocal(rstd, root))
    link(dve.tensor_tensor(scratch, rstd, rstd, ALU.mult))
    link(dve.tensor_tensor(scratch, scratch, root_in, ALU.mult))
    link(dve.tensor_scalar(scratch, scratch, -0.5, 1.5, ALU.mult, ALU.add))
    link(dve.tensor_tensor(rstd, rstd, scratch, ALU.mult))


def stage_norm(nc, x, ident, xnT_hi, xnT_lo, xrow):
    with ExitStack() as ctx:
        b = Buffers(nc, ctx)
        stats = b.sb("n_stats", [TOK, NT, 6])
        mean_var = b.sb("n_mean_var", [TOK, NT, 2])
        root_in = b.sb("n_root_in", [TOK, NT])
        root = b.sb("n_root", [TOK, NT])
        scratch = b.sb("n_scratch", [TOK, NT])
        rstd = b.sb("n_rstd", [TOK, NT])
        bank = [b.ps(f"n_bank{i}", [P, 512]) for i in range(4)]
        x_loaded = b.sem("n_x_loaded")
        dve_step = b.sem("n_dve_step")
        ident_ready = b.sem("n_ident_ready")
        var_ready = b.sem("n_var_ready")
        root_ready = b.sem("n_root_ready")
        row_ready = b.sem("n_row_ready")
        turned = b.sem("n_turned")
        hi_ready = b.sem("n_hi_ready")
        lo_ready = b.sem("n_lo_ready")
        block = ctx.enter_context(nc.Block())
        units = [(g, c) for g in range(3) for c in range(DC)]

        @block.sync
        def _(sp):
            view = x.rearrange("(t p) c -> p t c", p=TOK)
            for t in range(NT):
                sp.dma_start(xrow[:, t, :], view[:, t, :]).then_inc(x_loaded, 16)

        @block.gpsimd
        def _(pool):
            pool.memset(ident[:, :], 0.0).then_inc(ident_ready, 1)
            pool.wait_ge(ident_ready, 1)
            pool.affine_select(out=ident[:, :], in_=ident[:, :], compare_op=ALU.not_equal, fill=1.0,
                               base=0, pattern=[[-1, P]], channel_multiplier=1).then_inc(ident_ready, 1)
            pool.memset(xnT_hi[:, :, N:NS].bitcast(F32), 0.0)
            pool.memset(xnT_lo[:, :, N:NS].bitcast(F32), 0.0)

        @block.vector
        def _(dve):
            link = chain(dve, dve_step)
            dve.wait_ge(x_loaded, 16 * NT)
            node_stats(dve, link, xrow, stats, mean_var, root_in).then_inc(var_ready, 1)
            dve.wait_ge(root_ready, 1)
            inverse_root(dve, link, root_in[:, :], root[:, :], scratch[:, :], rstd[:, :])
            for t in range(NT):
                dve.tensor_scalar(xrow[:, t, :], xrow[:, t, :], mean_var[:, t, 0:1], rstd[:, t:t + 1],
                                  ALU.subtract, ALU.mult).then_inc(row_ready, 1)
            for u, (g, c) in enumerate(units):
                n = TOK * len(tile_parts(g))
                cols = slice(500 * g, 500 * g + n)
                dve.wait_ge(hi_ready, u + 1)
                dve.tensor_tensor(xnT_lo[:, c, cols], bank[u % 4][:, 0:n], xnT_hi[:, c, cols].bitcast(F32),
                                  ALU.subtract).then_inc(lo_ready, 1)

        @block.scalar
        def _(act):
            act.wait_ge(var_ready, 1)
            act.activation(root[:, :], root_in[:, :], ACT.Sqrt).then_inc(root_ready, 1)
            for u, (g, c) in enumerate(units):
                n = TOK * len(tile_parts(g))
                act.wait_ge(turned, u + 1)
                act.activation(xnT_hi[:, c, 500 * g:500 * g + n], bank[u % 4][:, 0:n],
                               ACT.Copy).then_inc(hi_ready, 1)

        @block.tensor
        def _(pe):
            pe.wait_ge(ident_ready, 2)
            for u, (g, c) in enumerate(units):
                if u >= 4:
                    pe.wait_ge(lo_ready, u - 3)
                pe.wait_ge(row_ready, tile_parts(g)[-1] + 1)
                for i, t in enumerate(tile_parts(g)):
                    ins = pe.transpose(bank[u % 4][:, TOK * i:TOK * (i + 1)], xrow[:, t, P * c:P * (c + 1)],
                                       ident[0:TOK, 0:TOK])
                ins.then_inc(turned, 1)


def stage_count(nc, src, dst, ident, counts):
    with ExitStack() as ctx:
        b = Buffers(nc, ctx)
        edge_in = b.sb("c_edge_in", [NEB, 2, EB], I32)
        edge_row = b.sb("c_edge_row", [NEB, 2, EB])
        edge_col = b.sb("c_edge_col", [TOK, 2, SUB, NEB])
        reach = b.sb("c_reach", [NEB, 2])
        block_no = b.sb("c_block_no", [NT, NEB])
        tile_lo = b.sb("c_tile_lo", [NT, 2])
        over = b.sb("c_over", [NT, 2, NEB])
        at = b.sb("c_at", [NT, 2, NEB])
        span = b.sb("c_span", [NT, 2])
        span_int = b.sb("c_span_int", [NT, 2], I32)
        span_row = b.sb("c_span_row", [1, 2 * NT], I32)
        node_no = b.sb("c_node_no", [TOK, NS], F16)
        src_hot = b.sb("c_src_hot", [TOK, SUB, NS], BF16)
        dst_hot = b.sb("c_dst_hot", [TOK, SUB, TOK], BF16)
        zeros = b.sb("c_zeros", [TOK, 512], BF16)
        count_out = b.sb("c_count_out", [TOK, NS], U16)
        turn_bank = [b.ps(f"c_turn{i}", [P, 512]) for i in range(2)]
        reach_bank = b.ps("c_reach_bank", [P, 512])
        acc = b.ps("c_acc", [P, NB, 512])
        edges_loaded = b.sem("c_edges_loaded")
        iota_ready = b.sem("c_iota_ready")
        dve_step = b.sem("c_dve_step")
        rows_ready = b.sem("c_rows_ready")
        turned = b.sem("c_turned")
        cols_ready = b.sem("c_cols_ready")
        reach_ready = b.sem("c_reach_ready")
        reach_spread = b.sem("c_reach_spread")
        span_ready = b.sem("c_span_ready")
        span_loaded = b.sem("c_span_loaded")
        hot_ready = b.sem("c_hot_ready")
        hot_used = b.sem("c_hot_used")
        tile_counted = b.sem("c_tile_counted")
        tile_copied = b.sem("c_tile_copied")
        tile_stored = b.sem("c_tile_stored")
        block = ctx.enter_context(nc.Block())

        @block.sync
        def _(sp):
            sp.dma_start(edge_in[:, 0, :], src.rearrange("(r e) -> r e", e=EB)).then_inc(edges_loaded, 16)
            sp.dma_start(edge_in[:, 1, :], dst.rearrange("(r e) -> r e", e=EB)).then_inc(edges_loaded, 16)
            sp.wait_ge(span_ready, 1)
            sp.dma_start(span_row[0:1, :].rearrange("o (t k) -> o t k", k=2), span_int[:, :]).then_inc(span_loaded, 16)
            with sp.Fori(0, NT) as t:
                sp.wait_ge(tile_copied, t + 2)
                sp.dma_start(counts[bass.ds(t * TOK, TOK), :], count_out[:, :]).then_inc(tile_stored, 16)
            sp.wait_ge(tile_stored, 16 * (NT + 1))

        @block.gpsimd
        def _(pool):
            pool.iota(node_no[:, :], [[1, NS]], base=0, channel_multiplier=0,
                      allow_small_or_imprecise_dtypes=True).then_inc(iota_ready, 1)
            pool.iota(block_no[:, :], [[1, NEB]], base=0, channel_multiplier=0,
                      allow_small_or_imprecise_dtypes=True).then_inc(iota_ready, 1)
            pool.iota(tile_lo[:, :], [[TOK - 1, 2]], base=0, channel_multiplier=TOK,
                      allow_small_or_imprecise_dtypes=True).then_inc(iota_ready, 1)
            pool.memset(zeros[:, :], 0.0).then_inc(iota_ready, 1)

        @block.vector
        def _(dve):
            link = chain(dve, dve_step)
            dve.wait_ge(edges_loaded, 32)
            link(dve.tensor_copy(edge_row[:, :, :], edge_in[:, :, :]))
            dve.tensor_reduce(reach[:, 0:1], edge_row[:, 1, :], AX.X, ALU.min)
            link(dve.tensor_reduce(reach[:, 1:2], edge_row[:, 1, :], AX.X, ALU.max))
            dve.sem_inc(rows_ready, 1)
            for w in range(2):
                dve.wait_ge(turned, w + 1)
                dve.tensor_copy(edge_col[:, w, :, :], turn_bank[w][0:TOK, 0:SUB * NEB].rearrange(
                    "p (k r) -> p k r", k=SUB)).then_inc(cols_ready, 1)
            dve.wait_ge(reach_spread, 1)
            dve.wait_ge(iota_ready, 4)
            dve.tensor_scalar(over[:, 0, :], reach_bank[0:NT, 0:NEB], tile_lo[:, 1:2], None, ALU.is_le)
            link(dve.tensor_scalar(over[:, 1, :], reach_bank[0:NT, NEB:2 * NEB], tile_lo[:, 0:1], None, ALU.is_ge))
            link(dve.tensor_tensor(over[:, 0, :], over[:, 0, :], over[:, 1, :], ALU.mult))
            dve.scalar_tensor_tensor(at[:, 0, :], block_no[:, :], -float(NEB - 1), over[:, 0, :], ALU.add, ALU.mult)
            link(dve.scalar_tensor_tensor(at[:, 1, :], block_no[:, :], 1.0, over[:, 0, :], ALU.add, ALU.mult))
            dve.tensor_reduce(span[:, 0:1], at[:, 0, :], AX.X, ALU.min)
            link(dve.tensor_reduce(span[:, 1:2], at[:, 1, :], AX.X, ALU.max))
            link(dve.tensor_scalar(span[:, 0:1], span[:, 0:1], float(NEB - 1), None, ALU.add))
            link(dve.scalar_tensor_tensor(span[:, 1:2], span[:, 0:1], 1.0, span[:, 1:2], ALU.add, ALU.max))
            dve.tensor_copy(span_int[:, :], span[:, :]).then_inc(span_ready, 1)
            dve.wait_ge(cols_ready, 2)
            dve.wait_ge(span_loaded, 16)
            serial = dve.alloc_register("c_dve_serial")
            dve.reg_mov(serial, 1)
            dve.sem_inc(hot_used, SUB)
            dve.sem_inc(hot_ready, 1)
            with dve.Fori(0, NT) as t:
                first = dve.value_load(span_row[0:1, bass.ds(2 * t, 1)], min_val=0, max_val=NEB - 1)
                stop = dve.value_load(span_row[0:1, bass.ds(2 * t + 1, 1)], min_val=1, max_val=NEB)
                with dve.Fori(first, stop) as r:
                    for k in range(SUB):
                        dve.wait_ge(hot_used, serial)
                        dve.tensor_scalar(src_hot[:, k, :], node_no[:, :], edge_col[:, 0, k, bass.ds(r, 1)],
                                          None, ALU.is_equal)
                        dve.tensor_scalar(dst_hot[:, k, :], node_no[:, 0:TOK], edge_col[:, 1, k, bass.ds(r, 1)],
                                          None, ALU.is_equal).then_inc(hot_ready, 1)
                        dve.reg_add(serial, serial, 1)
                dve.wait_ge(hot_ready, serial)
                dve.tensor_scalar(edge_col[:, 1, :, :], edge_col[:, 1, :, :], -float(TOK), None,
                                  ALU.add).then_inc(cols_ready, 1)
                dve.wait_ge(cols_ready, t + 3)

        @block.scalar
        def _(act):
            act.sem_inc(tile_copied, 1)
            with act.Fori(0, NT) as t:
                act.wait_ge(tile_counted, t + 1)
                act.wait_ge(tile_stored, 16 * t + 16)
                act.activation(count_out[:, :].rearrange("p (b n) -> p b n", b=NB), acc[0:TOK, :, 0:BW],
                               ACT.Copy).then_inc(tile_copied, 1)

        @block.tensor
        def _(pe):
            pe.wait_ge(rows_ready, 1)
            for w in range(2):
                for k in range(SUB):
                    ins = pe.transpose(turn_bank[w][0:TOK, NEB * k:NEB * (k + 1)],
                                       edge_row[:, w, TOK * k:TOK * (k + 1)], ident[0:NEB, 0:NEB])
                ins.then_inc(turned, 1)
            for w in range(2):
                ins = pe.matmul(reach_bank[0:NT, NEB * w:NEB * (w + 1)],
                                reach[:, w:w + 1].to_broadcast([NEB, NT]), ident[0:NEB, 0:NEB],
                                start=True, stop=True)
            ins.then_inc(reach_spread, 1)
            pe.wait_ge(span_loaded, 16)
            pe.sem_inc(tile_stored, 16)
            serial = pe.alloc_register("c_pe_serial")
            pe.reg_mov(serial, 2)
            with pe.Fori(0, NT) as t:
                first = pe.value_load(span_row[0:1, bass.ds(2 * t, 1)], min_val=0, max_val=NEB - 1)
                stop = pe.value_load(span_row[0:1, bass.ds(2 * t + 1, 1)], min_val=1, max_val=NEB)
                pe.wait_ge(tile_copied, t + 1)
                for n in range(NB):
                    pe.matmul(acc[0:TOK, n, 0:BW], zeros[:, 0:TOK], zeros[:, 0:BW], start=True, stop=False)
                with pe.Fori(first, stop) as r:
                    for k in range(SUB):
                        pe.wait_ge(hot_ready, serial)
                        for n in range(NB):
                            ins = pe.matmul(acc[0:TOK, n, 0:BW], dst_hot[:, k, :], src_hot[:, k, BW * n:BW * (n + 1)],
                                            start=False, stop=False)
                        ins.then_inc(hot_used, 1)
                        pe.reg_add(serial, serial, 1)
                for n in range(NB):
                    ins = pe.matmul(acc[0:TOK, n, 0:BW], zeros[:, 0:TOK], zeros[:, 0:BW], start=False, stop=True)
                ins.then_inc(tile_counted, 1)


PARTS = ((0, 0), (0, 1), (1, 0))


def stage_fold(nc, gnn, ident, xnT, query_dram, value_dram, fold_bias, row_shift, value_bias, hidden):
    HC = HEADS * DC
    with ExitStack() as ctx:
        b = Buffers(nc, ctx)
        raw = [b.sb(f"f_raw{w}", [P, DC, D]) for w in range(4)]
        turn = [[b.sb(f"f_turn{w}_{k}", [P, DC, D], F32R) for k in ("hi", "lo")] for w in range(4)]
        lin_raw = b.sb("f_lin_raw", [P, DC, D])
        lin = [b.sb(f"f_lin_{k}", [P, DC, D], F32R) for k in ("hi", "lo")]
        made_out = [b.sb(f"f_made_out{i}", [P, DC, D]) for i in range(2)]
        skip_sum = b.sb("f_skip_sum", [P, DC, D])
        head0 = b.sb("f_head0", [P, P])
        bias_in = b.sb("f_bias_in", [4 * HC, P])
        bias_col = b.sb("f_bias_col", [P, 4, HC])
        bias_pair = b.sb("f_bias_pair", [P, 4, HC, 2], F32R)
        small_col = b.sb("f_small_col", [P, HEADS, 3, DC])
        shift_pair = b.sb("f_shift_pair", [P, DC, HEADS, 2], F32R)
        skip_col = b.sb("f_skip_col", [P, DC])
        bias_dot = b.sb("f_bias_dot", [P, HC])
        bias_dots = b.sb("f_bias_dots", [P, HEADS])
        ones = b.sb("f_ones", [P, TOK])
        lin_bias = b.sb("f_lin_bias", [TOK, D])
        hidden_row = [b.sb(f"f_hidden_row{i}", [TOK, D]) for i in range(2)]
        shift_sum = b.sb("f_shift_sum", [TOK, NT, HEADS])
        turn_bank = [b.ps(f"f_turn_bank{i}", [P, 512]) for i in range(2)]
        bank = [b.ps(f"f_bank{i}", [P, 512]) for i in range(2)]
        small = b.ps("f_small", [P, 512])
        shift_bank = b.ps("f_shift", [P, 512])
        row_bank = [b.ps(f"f_row_bank{i}", [P, 512]) for i in range(2)]
        bias_loaded = b.sem("f_bias_loaded")
        lin_bias_loaded = b.sem("f_lin_bias_loaded")
        bias_turned = b.sem("f_bias_turned")
        pair_ready = b.sem("f_pair_ready")
        ones_ready = b.sem("f_ones_ready")
        dve_step = b.sem("f_dve_step")
        raw_loaded = [b.sem(f"f_raw_loaded{w}") for w in range(4)]
        lin_loaded = b.sem("f_lin_loaded")
        lin_raw_ready = b.sem("f_lin_raw_ready")
        lin_hi = b.sem("f_lin_hi")
        lin_ready = b.sem("f_lin_ready")
        turned = b.sem("f_turned")
        turn_hi = b.sem("f_turn_hi")
        turn_ready = b.sem("f_turn_ready")
        made = b.sem("f_made")
        moved = b.sem("f_moved")
        summed = b.sem("f_summed")
        stored = [b.sem(f"f_stored{i}") for i in range(2)]
        small_done = b.sem("f_small_done")
        small_read = b.sem("f_small_read")
        dots_ready = b.sem("f_dots_ready")
        skip_hi = b.sem("f_skip_hi")
        skip_ready = b.sem("f_skip_ready")
        rows_done = b.sem("f_rows_done")
        row_read = b.sem("f_row_read")
        shift_done = b.sem("f_shift_done")
        row_stored = [b.sem(f"f_row_stored{i}") for i in range(2)]
        block = ctx.enter_context(nc.Block())


        def unit(w0, u):
            return turn[w0 + u // DC], u % DC

        def heads(engine, head):
            with engine.Fori(0, HEADS - 1) as h:
                head(h, False)
            head(HEADS - 1, True)

        @block.sync
        def _(sp):
            for i, name in enumerate(("bq", "bk", "bv", "bskip")):
                sp.dma_start(bias_in[HC * i:HC * (i + 1), :], gnn[name].rearrange("(r p) -> r p", p=P)).then_inc(bias_loaded, 16)

            def load(w, name, h):
                sp.dma_start(raw[w][:, :, :], gnn[name].rearrange("(c p) n -> p c n", p=P)[:, :, bass.ds(h * D, D)]
                             ).then_inc(raw_loaded[w], 16)

            def load_lin(h):
                sp.dma_start(lin_raw[:, :, :], gnn["Wlin"].rearrange("(c p) n -> p c n", p=P)[:, bass.ds(h * DC, DC), :]
                             ).then_inc(lin_loaded, 16)

            for w, name in enumerate(("Wq", "Wk", "Wv", "Wskip")):
                load(w, name, 0)
            load_lin(0)
            sp.dma_start(lin_bias[:, :], gnn["blin"].unsqueeze(0).to_broadcast([TOK, D])).then_inc(lin_bias_loaded, 16)
            with sp.Fori(0, HEADS - 1) as h:
                sp.wait_ge(turned, 16 * h + 8)
                load(0, "Wq", h + 1)
                load(1, "Wk", h + 1)
                sp.wait_ge(lin_ready, h + 1)
                load_lin(h + 1)
                sp.wait_ge(turned, 16 * h + 16)
                load(2, "Wv", h + 1)
                load(3, "Wskip", h + 1)
            for t in range(NT):
                sp.wait_ge(row_read, HEADS + 1 + t + 1)
                sp.dma_start(hidden[TOK * t:TOK * (t + 1), :], hidden_row[t % 2][:, :]).then_inc(row_stored[t % 2], 16)
            for i in range(2):
                sp.wait_ge(row_stored[i], 16 * NT // 2)

        @block.gpsimd
        def _(pool):
            pool.memset(ones[:, :], 1.0).then_inc(ones_ready, 1)

        @block.scalar
        def _(act):
            def turn_part(w0, u, first_unit):
                part, j = unit(w0, u)
                act.wait_ge(turned, first_unit + (u + 1))
                act.activation(part[0][:, j, :], turn_bank[u % 2][:, :], ACT.Copy).then_inc(turn_hi, 1)

            def product(h, k):
                i, c = divmod(k, DC)
                if c == 0:
                    act.wait_ge(stored[i], 16 * h + 16)
                act.wait_ge(made, 12 * h + (k + 2))
                act.activation(made_out[i][:, c, :], bank[k % 2][:, :], ACT.Copy).then_inc(moved, 1)
                if c == DC - 1:
                    act.wait_ge(moved, 8 * h + (k + 1))
                    act.dma_start((query_dram, value_dram)[i][bass.ds(h * DC, DC), :, :].rearrange("c p n -> p c n"),
                                  made_out[i][:, :, :]).then_inc(stored[i], 16)

            def head(h, last):
                act.wait_ge(lin_raw_ready, h + 2)
                act.wait_ge(made, 12 * h + 1)
                act.activation(lin[0][:, :, :], lin_raw[:, :, :], ACT.Copy).then_inc(lin_hi, 1)
                for c in range(DC):
                    product(h, c)
                    turn_part(2, 2 * c, 16 * h + 8)
                    turn_part(2, 2 * c + 1, 16 * h + 8)
                for c in range(DC):
                    product(h, DC + c)
                    if not last:
                        turn_part(0, c, 16 * h + 16)
                if not last:
                    for c in range(DC):
                        turn_part(0, DC + c, 16 * h + 16)

            for i in range(2):
                act.sem_inc(stored[i], 16)
            for u in range(8):
                turn_part(0, u, 0)
            heads(act, head)
            act.wait_ge(summed, 4 * HEADS + 4)
            act.activation(turn[0][0][:, :, :], skip_sum[:, :, :], ACT.Copy).then_inc(skip_hi, 1)
            for i in range(2):
                act.wait_ge(stored[i], 16 * (HEADS + 1))

        @block.vector
        def _(dve):
            link = chain(dve, dve_step)
            dve.tensor_copy(head0[:, :], ident[:, :]).then_inc(lin_raw_ready, 1)
            dve.memset(skip_sum[:, :, :], 0.0).then_inc(summed, 4)
            dve.wait_ge(lin_raw_ready, 1)
            dve.wait_ge(summed, 4)
            dve.wait_ge(bias_turned, 1)
            link(dve.tensor_copy(bias_col[:, :, :], small[:, 0:4 * HC].rearrange("p (i k) -> p i k", i=4)))
            link(dve.tensor_copy(bias_pair[:, :, :, 0], bias_col[:, :, :]))
            dve.tensor_tensor(bias_pair[:, :, :, 1], bias_col[:, :, :], bias_pair[:, :, :, 0].bitcast(F32),
                              ALU.subtract).then_inc(pair_ready, 1)
            link(dve.tensor_tensor(bias_dot[:, :], bias_col[:, 0, :], bias_col[:, 1, :], ALU.mult))
            dve.tensor_reduce(bias_dots[:, :], bias_dot[:, :].rearrange("p (h c) -> p h c", c=DC), AX.X,
                              ALU.add).then_inc(dots_ready, 1)
            dve.sem_inc(small_read, 1)

            def turn_part(w0, u, first_unit):
                part, j = unit(w0, u)
                dve.wait_ge(turn_hi, first_unit + (u + 1))
                dve.tensor_tensor(part[1][:, j, :], turn_bank[u % 2][:, :], part[0][:, j, :].bitcast(F32),
                                  ALU.subtract).then_inc(turn_ready, 1)

            def head(h, last):
                dve.wait_ge(lin_loaded, 16 * h + 16)
                for c in range(DC):
                    ins = dve.tensor_tensor(lin_raw[:, c, P * c:P * (c + 1)], lin_raw[:, c, P * c:P * (c + 1)],
                                            head0[:, :], ALU.add)
                ins.then_inc(lin_raw_ready, 1)
                dve.wait_ge(lin_raw_ready, h + 2)
                dve.memset(head0[:, :], 0.0)
                dve.wait_ge(lin_hi, h + 1)
                dve.tensor_tensor(lin[1][:, :, :], lin_raw[:, :, :], lin[0][:, :, :].bitcast(F32), ALU.subtract
                                  ).then_inc(lin_ready, 1)
                for u in range(8):
                    turn_part(2, u, 16 * h + 8)
                dve.wait_ge(small_done, h + 1)
                pairs = small[:, 256:256 + 8 * DC].rearrange("p (i c k) -> p i c k", i=4, k=2)
                dve.tensor_reduce(fold_bias[:, bass.ds(h, 1), :].rearrange("p o c -> p (o c)"), pairs[:, 0, :, :], AX.X, ALU.add)
                dve.tensor_reduce(small_col[:, bass.ds(h, 1), :, :].rearrange("p o i c -> p (o i) c"), pairs[:, 1:4, :, :],
                                  AX.X, ALU.add).then_inc(small_read, 1)
                if not last:
                    for u in range(DC):
                        turn_part(0, u, 16 * h + 16)
                for c in range(DC):
                    dve.wait_ge(made, 12 * h + (8 + c + 2))
                    dve.wait_ge(summed, 4 * h + (c + 1))
                    dve.tensor_tensor(skip_sum[:, c, :], bank[c % 2][:, :], skip_sum[:, c, :], ALU.add).then_inc(summed, 1)
                    if not last:
                        turn_part(0, DC + c, 16 * h + 16)

            for u in range(8):
                turn_part(0, u, 0)
            heads(dve, head)
            dve.wait_ge(skip_hi, 1)
            dve.tensor_tensor(turn[0][1][:, :, :], skip_sum[:, :, :], turn[0][0][:, :, :].bitcast(F32),
                              ALU.subtract).then_inc(skip_ready, 1)
            dve.wait_ge(small_read, HEADS + 1)
            shift_col = small_col[:, :, 0, :].rearrange("p h c -> p c h")
            link(dve.tensor_copy(shift_pair[:, :, :, 0], shift_col))
            dve.tensor_tensor(shift_pair[:, :, :, 1], shift_col, shift_pair[:, :, :, 0].bitcast(F32),
                              ALU.subtract).then_inc(pair_ready, 1)
            dve.tensor_reduce(skip_col[:, :], small_col[:, :, 2, :].rearrange("p h c -> p c h"), AX.X,
                              ALU.add).then_inc(pair_ready, 1)
            dve.wait_ge(lin_bias_loaded, 16)
            for i in range(HEADS + 1):
                dve.wait_ge(rows_done, i + 1)
                if i < HEADS:
                    dve.tensor_copy(value_bias[:, i, :], row_bank[i % 2][0:TOK, :]).then_inc(row_read, 1)
                else:
                    dve.tensor_tensor(lin_bias[:, :], row_bank[i % 2][0:TOK, :], lin_bias[:, :], ALU.add).then_inc(row_read, 1)
                    dve.wait_ge(row_read, i + 1)
            for t in range(NT):
                i = HEADS + 1 + t
                dve.wait_ge(rows_done, i + 1)
                if t >= 2:
                    dve.wait_ge(row_stored[t % 2], 16 * (t // 2))
                dve.tensor_tensor(hidden_row[t % 2][:, :], row_bank[i % 2][0:TOK, :], lin_bias[:, :], ALU.add).then_inc(row_read, 1)
            dve.wait_ge(shift_done, 1)
            link(dve.tensor_reduce(shift_sum[:, :, :], shift_bank[0:TOK, 0:2 * NT * HEADS].rearrange(
                "p (t h k) -> p t h k", t=NT, k=2), AX.X, ALU.add))
            link(dve.tensor_tensor(row_shift[:, :, :], shift_sum[:, :, :],
                                   small[0:TOK, 320:320 + HEADS].unsqueeze(1).to_broadcast([TOK, NT, HEADS]), ALU.add))

        @block.tensor
        def _(pe):
            pe.wait_ge(bias_loaded, 64)
            pe.transpose(small[:, 0:4 * HC], bias_in[:, :], ident[0:4 * HC, 0:4 * HC]).then_inc(bias_turned, 1)

            def turn_part(w0, u, first_unit):
                w, j = w0 + u // DC, u % DC
                if not isinstance(first_unit, int) or u >= 2:
                    pe.wait_ge(turn_ready, first_unit + (u - 1))
                for c in range(DC):
                    ins = pe.transpose(turn_bank[u % 2][:, P * c:P * (c + 1)], raw[w][:, c, P * j:P * (j + 1)], ident[:, :])
                ins.then_inc(turned, 1)

            def product(h, k, left, right):
                c = k % DC
                if k < 2:
                    pe.wait_ge(summed, 4 * h + (k + 3))
                elif k < 10:
                    pe.wait_ge(moved, 8 * h + (k - 1))
                else:
                    pe.wait_ge(summed, 4 * h + (k - 5))
                for j in range(DC):
                    for n, (x, y) in enumerate(PARTS):
                        ins = pe.matmul(bank[k % 2][:, :], left[x][:, j, P * c:P * (c + 1)], right[y][:, j, :],
                                        start=(j == 0 and n == 0), stop=(j == DC - 1 and n == 2))
                ins.then_inc(made, 1)

            def head(h, last):
                pe.wait_ge(turn_ready, 16 * h + 8)
                pe.wait_ge(raw_loaded[2], 16 * h + 16)
                for c in range(DC):
                    product(h, c, turn[0], turn[1])
                    if c == 2:
                        pe.wait_ge(raw_loaded[3], 16 * h + 16)
                    turn_part(2, 2 * c, 16 * h + 8)
                    turn_part(2, 2 * c + 1, 16 * h + 8)
                pe.wait_ge(small_read, h + 1)
                pe.wait_ge(lin_ready, h + 1)
                for i, (mat, vec) in enumerate(((turn[1], 0), (turn[0], 1), (lin, 2), (lin, 3))):
                    for c in range(DC):
                        to = 256 + 2 * DC * i + 2 * c
                        for j in range(DC):
                            for n, part in enumerate(mat):
                                ins = pe.matmul(small[:, to:to + 2], part[:, j, P * c:P * (c + 1)],
                                                bias_pair[:, vec, bass.ds(h * DC + j, 1), :].rearrange("p o k -> p (o k)"),
                                                start=(j == 0 and n == 0), stop=(j == DC - 1 and n == 1))
                ins.then_inc(small_done, 1)
                pe.wait_ge(turn_ready, 16 * h + 16)
                if not last:
                    pe.wait_ge(raw_loaded[0], 16 * h + 32)
                    pe.wait_ge(raw_loaded[1], 16 * h + 32)
                for c in range(DC):
                    product(h, DC + c, turn[2], lin)
                    if not last:
                        turn_part(0, c, 16 * h + 16)
                for c in range(DC):
                    product(h, 2 * DC + c, turn[3], lin)
                    if not last:
                        turn_part(0, DC + c, 16 * h + 16)

            pe.wait_ge(pair_ready, 1)
            pe.sem_inc(made, 1)
            pe.wait_ge(raw_loaded[0], 16)
            for u in range(8):
                if u == DC:
                    pe.wait_ge(raw_loaded[1], 16)
                turn_part(0, u, 0)
            heads(pe, head)
            pe.wait_ge(pair_ready, 3)
            for i in range(HEADS + 1):
                if i >= 2:
                    pe.wait_ge(row_read, i - 1)
                for c in range(DC):
                    col = small_col[:, i, 1, c:c + 1] if i < HEADS else skip_col[:, c:c + 1]
                    ins = pe.matmul(row_bank[i % 2][0:TOK, P * c:P * (c + 1)], col.to_broadcast([P, TOK]), ident[:, :],
                                    start=True, stop=True)
                ins.then_inc(rows_done, 1)
            pe.wait_ge(skip_ready, 1)
            for t in range(NT):
                i = HEADS + 1 + t
                pe.wait_ge(row_read, i - 1)
                for c in range(DC):
                    for n, (x, y) in enumerate(PARTS):
                        ins = pe.matmul(row_bank[i % 2][0:TOK, :], xnT[x][:, c, TOK * t:TOK * (t + 1)], turn[0][y][:, c, :],
                                        start=(c == 0 and n == 0), stop=(c == DC - 1 and n == 2))
                ins.then_inc(rows_done, 1)
            for t in range(NT):
                for c in range(DC):
                    for n, part in enumerate(xnT):
                        pe.matmul(shift_bank[0:TOK, 8 * t:8 * t + 8], part[:, c, TOK * t:TOK * (t + 1)],
                                  shift_pair[:, c, :, :].rearrange("p h k -> p (h k)"),
                                  start=(c == 0 and n == 0), stop=(c == DC - 1 and n == 1))
            pe.wait_ge(dots_ready, 1)
            pe.wait_ge(ones_ready, 1)
            pe.matmul(small[0:TOK, 320:320 + HEADS], ones[:, :], bias_dots[:, :], start=True, stop=True).then_inc(shift_done, 1)


class Steps:

    def __init__(self, engine, sem, base, total):
        self.engine, self.sem, self.base, self.total, self.n = engine, sem, base, total, 0

    def __call__(self, ins):
        self.n += 1
        ins.then_inc(self.sem, 1)
        self.engine.wait_ge(self.sem, self.base + self.n)


def stage_attend(nc, xnT, counts, query_dram, value_dram, fold_bias, row_shift, value_bias, ident, hidden):
    SCALE = float(D) ** -0.5
    GROUP_STEPS = 6
    with ExitStack() as ctx:
        b = Buffers(nc, ctx)
        query_w = [b.sb(f"a_query_w_{k}", [P, DC, D], F32R) for k in ("hi", "lo")]
        value_w = [b.sb(f"a_value_w_{k}", [P, DC, D], F32R) for k in ("hi", "lo")]
        query_raw = b.sb("a_query_raw", [P, DC, D])
        value_raw = b.sb("a_value_raw", [P, DC, D])
        value = [b.sb(f"a_value_{k}", [TOK, NT, D], F32R) for k in ("hi", "lo")]
        value_sum = b.sb("a_value_sum", [TOK, 2, D])
        query_t = [b.sb(f"a_query_t_{k}", [P, DC, GRP], F32R) for k in ("hi", "lo")]
        prob_t = [b.sb(f"a_prob_t_{k}", [TOK, NT, GRP], F32R) for k in ("hi", "lo")]
        count = [b.sb(f"a_count{t}", [TOK, NS], U16) for t in range(2)]
        no_edge = b.sb("a_no_edge", [TOK, NS], BF16)
        score = [b.sb(f"a_score{t}", [TOK, NS]) for t in range(2)]
        fold_bias_now = b.sb("a_fold_bias_now", [P, DC])
        top = b.sb("a_top", [TOK, 2])
        shift = b.sb("a_shift", [TOK, 2])
        den = b.sb("a_den", [TOK, 2])
        inv_den = b.sb("a_inv_den", [TOK, 2])
        hold = b.sb("a_hold", [TOK, 2, D])
        bank_a = b.ps("a_bank_a", [P, NB, 512])
        bank_b = b.ps("a_bank_b", [P, NB, 512])
        bank_c = b.ps("a_bank_c", [P, 2, 512])

        query_loaded = b.sem("a_query_loaded")
        value_loaded = b.sem("a_value_loaded")
        count_loaded = [b.sem(f"a_count_loaded{t}") for t in range(2)]
        hold_loaded = b.sem("a_hold_loaded")
        hidden_stored = b.sem("a_hidden_stored")
        bias_ready = b.sem("a_bias_ready")
        query_w_hi = b.sem("a_query_w_hi")
        query_w_ready = b.sem("a_query_w_ready")
        value_w_hi = b.sem("a_value_w_hi")
        value_w_ready = b.sem("a_value_w_ready")
        value_done = b.sem("a_value_done")
        value_summed = b.sem("a_value_summed")
        value_hi = b.sem("a_value_hi")
        value_ready = b.sem("a_value_ready")
        query_done = b.sem("a_query_done")
        query_hi = b.sem("a_query_hi")
        query_ready = b.sem("a_query_ready")
        scored = b.sem("a_scored")
        masked = b.sem("a_masked")
        shift_ready = b.sem("a_shift_ready")
        exp_done = b.sem("a_exp_done")
        weighted = b.sem("a_weighted")
        turned = b.sem("a_turned")
        prob_t_hi = b.sem("a_prob_t_hi")
        prob_t_ready = b.sem("a_prob_t_ready")
        out_done = b.sem("a_out_done")
        added = b.sem("a_added")
        padded = b.sem("a_padded")
        dve_step = b.sem("a_dve_step")
        block = ctx.enter_context(nc.Block())

        def half(bank, c):
            return bank[:, c // 2, GRP * (c % 2):GRP * (c % 2 + 1)]

        def groups(engine, group, h):
            with engine.Fori(0, NG - 1) as g:
                group(h, g, False)
            group(h, NG - 1, True)

        def turned_parts(bank, t):
            cols = slice(TOK * t, TOK * (t + 1))
            yield (bank[0:TOK, 0:2, 0:500].rearrange("p b (i n) -> p b i n", n=TOK),
                   [part[:, 0:8, cols].rearrange("p (b i) n -> p b i n", b=2) for part in prob_t])
            yield (bank[0:TOK, 2, 0:250].rearrange("p (i n) -> p i n", n=TOK), [part[:, 8:10, cols] for part in prob_t])


        @block.sync
        def _(sp):
            def load(to, dram, h, sem):
                sp.dma_start(to[:, :, :], dram[bass.ds(h * DC, DC), :, :].rearrange("c p n -> p c n")).then_inc(sem, 16)

            def group(h, g, last):
                nth = h * NG + (g + 1)
                for t in range(2):
                    sp.wait_ge(weighted, 2 * nth - 1 + t)
                    sp.dma_start(count[t][:, 0:N], counts[bass.ds(g * GRP + t * TOK, TOK), 0:N]).then_inc(count_loaded[t], 16)

            load(value_raw, value_dram, 0, value_loaded)
            with sp.Fori(0, HEADS) as h:
                sp.wait_ge(query_w_ready, h + 1)
                load(query_raw, query_dram, h, query_loaded)
                sp.wait_ge(value_w_ready, h + 1)
                load(value_raw, value_dram, (h + 1) % HEADS, value_loaded)
                groups(sp, group, h)
            sp.wait_ge(value_loaded, 16 * (HEADS + 1))

        @block.gpsimd
        def _(pool):
            for t in range(2):
                pool.memset(count[t][:, N:NS].bitcast(BF16), 0.0).then_inc(padded, 1)

        @block.scalar
        def _(act):
            def rows(g):
                return hidden[bass.ds(g * GRP, GRP), :].rearrange("(t p) c -> p t c", p=TOK)

            def value_split(nth):
                act.wait_ge(value_loaded, 16 * nth)
                act.activation(value_w[0][:, :, :], value_raw[:, :, :], ACT.Copy).then_inc(value_w_hi, 1)

            def query(nth):
                act.wait_ge(query_done, nth + 1)
                for c in range(DC):
                    act.activation(query_t[0][:, c, :], half(bank_c, c), ACT.Identity,
                                   bias=fold_bias_now[:, c:c + 1]).then_inc(query_hi, 1)

            def group(h, g, last):
                nth = h * NG + (g + 1)
                act.wait_ge(hidden_stored, 16 * nth)
                act.dma_start(hold[:, :, :], rows(g)).then_inc(hold_loaded, 16)
                for t in range(2):
                    act.wait_ge(shift_ready, 2 * nth - 1 + t)
                    act.activation(score[t][:, :], score[t][:, :], ACT.Exp, bias=shift[:, t:t + 1],
                                   scale=SCALE).then_inc(exp_done, 1)
                if not last:
                    query(nth + 1)
                for t, bank in ((0, bank_a), (1, bank_b)):
                    act.wait_ge(turned, 2 * nth - 1 + t)
                    for part, to in turned_parts(bank, t):
                        ins = act.activation(to[0], part, ACT.Copy)
                    ins.then_inc(prob_t_hi, 1)
                if last:
                    value_split(h + 2)
                act.wait_ge(added, 2 * nth + 1)
                act.dma_start(rows(g), hold[:, :, :]).then_inc(hidden_stored, 16)

            act.sem_inc(hidden_stored, 16)
            value_split(1)
            with act.Fori(0, HEADS) as h:
                for s in range(NT):
                    act.wait_ge(value_summed, NT * h + s + 1)
                    act.activation(value[0][:, s, :], value_sum[:, s % 2, :], ACT.Copy).then_inc(value_hi, 1)
                    if s == 3:
                        act.wait_ge(query_loaded, 16 * h + 16)
                        act.wait_ge(query_done, h * NG + 1)
                        act.activation(query_w[0][:, :, :], query_raw[:, :, :], ACT.Copy).then_inc(query_w_hi, 1)
                act.wait_ge(bias_ready, h + 1)
                query(h * NG + 1)
                groups(act, group, h)
            act.wait_ge(hidden_stored, 16 * (HEADS * NG + 1))

        @block.vector
        def _(dve):
            def value_split(nth):
                dve.wait_ge(value_w_hi, nth)
                dve.tensor_tensor(value_w[1][:, :, :], value_raw[:, :, :], value_w[0][:, :, :].bitcast(F32),
                                  ALU.subtract).then_inc(value_w_ready, 1)

            def query(nth):
                for c in range(DC):
                    dve.wait_ge(query_hi, 4 * nth - 3 + (c | 1))
                    dve.scalar_tensor_tensor(query_t[1][:, c, :], half(bank_c, c), fold_bias_now[:, c:c + 1],
                                             query_t[0][:, c, :].bitcast(F32), ALU.add, ALU.subtract
                                             ).then_inc(query_ready, 1)

            def group(h, g, last):
                nth = h * NG + (g + 1)
                link = Steps(dve, dve_step, (nth - 1) * GROUP_STEPS, GROUP_STEPS)
                banks = (bank_a, bank_b)

                def mask(t):
                    dve.wait_ge(count_loaded[t], 16 * nth)
                    link(dve.tensor_scalar(no_edge[:, :], count[t][:, :], 0.0, -FAR, ALU.is_equal, ALU.mult))

                def largest(t):
                    dve.wait_ge(scored, 2 * nth - 1 + t)
                    dve.scalar_tensor_tensor(score[t][:, :].rearrange("p (b n) -> p b n", b=NB),
                                             no_edge[:, :].rearrange("p (b n) -> p b n", b=NB),
                                             row_shift[:, bass.ds(g * 2 + t, 1), bass.ds(h, 1)].rearrange("p a o -> p (a o)"),
                                             banks[t][0:TOK, :, 0:BW], ALU.add, ALU.add).then_inc(masked, 1)
                    dve.wait_ge(masked, 2 * nth - 1 + t)
                    link(dve.tensor_reduce(top[:, t:t + 1], score[t][:, :], AX.X, ALU.max))
                    dve.tensor_scalar(shift[:, t:t + 1], top[:, t:t + 1], -SCALE, None, ALU.mult).then_inc(shift_ready, 1)

                def weigh(t):
                    dve.wait_ge(exp_done, 2 * nth - 1 + t)
                    dve.scalar_tensor_tensor(score[t][:, :], count[t][:, :], 1.0, score[t][:, :], ALU.mult, ALU.mult,
                                             accum_out=den[:, t:t + 1]).then_inc(weighted, 1)
                    dve.wait_ge(weighted, 2 * nth + 1 + t)
                    link(dve.tensor_scalar(den[:, t:t + 1], den[:, t:t + 1], 0.5, None, ALU.max))
                    dve.reciprocal(inv_den[:, t:t + 1], den[:, t:t + 1])

                mask(0)
                largest(0)
                mask(1)
                weigh(0)
                largest(1)
                weigh(1)
                assert link.n == GROUP_STEPS
                if not last:
                    query(nth + 1)
                for t, bank in ((0, bank_a), (1, bank_b)):
                    dve.wait_ge(prob_t_hi, 2 * nth - 1 + t)
                    for part, to in turned_parts(bank, t):
                        ins = dve.tensor_tensor(to[1], part, to[0].bitcast(F32), ALU.subtract)
                    ins.then_inc(prob_t_ready, 1)
                if last:
                    value_split(h + 2)
                dve.wait_ge(hold_loaded, 16 * nth)
                for t in range(2):
                    dve.wait_ge(out_done, 2 * nth - 1 + t)
                    dve.scalar_tensor_tensor(hold[:, t, :], bank_c[0:TOK, t, :], inv_den[:, t:t + 1], hold[:, t, :],
                                             ALU.mult, ALU.add).then_inc(added, 1)

            dve.wait_ge(padded, 2)
            dve.sem_inc(query_w_ready, 1)
            dve.sem_inc(weighted, 2)
            dve.sem_inc(added, 1)
            value_split(1)
            with dve.Fori(0, HEADS) as h:
                dve.tensor_scalar(fold_bias_now[:, :], fold_bias[:, bass.ds(h, 1), :].rearrange("p o c -> p (o c)"), 1.0,
                                  None, ALU.mult).then_inc(bias_ready, 1)
                for s in range(NT):
                    bank = (bank_a, bank_b)[(s // 2) % 2]
                    dve.wait_ge(value_done, NT * h + s + 1)
                    dve.tensor_tensor(value_sum[:, s % 2, :], bank[0:TOK, s % 2, :],
                                      value_bias[:, bass.ds(h, 1), :].rearrange("p o n -> p (o n)"),
                                      ALU.add).then_inc(value_summed, 1)
                    dve.wait_ge(value_hi, NT * h + s + 1)
                    dve.tensor_tensor(value[1][:, s, :], value_sum[:, s % 2, :], value[0][:, s, :].bitcast(F32),
                                      ALU.subtract).then_inc(value_ready, 1)
                    if s == 3:
                        dve.wait_ge(query_w_hi, h + 1)
                        dve.tensor_tensor(query_w[1][:, :, :], query_raw[:, :, :], query_w[0][:, :, :].bitcast(F32),
                                          ALU.subtract).then_inc(query_w_ready, 1)
                dve.wait_ge(bias_ready, h + 1)
                query(h * NG + 1)
                groups(dve, group, h)

        @block.tensor
        def _(pe):
            def query(g):
                for m in range(DC):
                    for c in range(DC):
                        for n, (x, y) in enumerate(PARTS):
                            ins = pe.matmul(half(bank_c, m), query_w[x][:, c, P * m:P * (m + 1)],
                                            xnT[y][:, c, bass.ds(g * GRP, GRP)], start=(c == 0 and n == 0),
                                            stop=(c == DC - 1 and n == 2))
                ins.then_inc(query_done, 1)

            def group(h, g, last):
                nth = h * NG + (g + 1)
                banks = (bank_a, bank_b)
                pe.wait_ge(query_ready, 4 * nth)
                for t in range(2):
                    for c in range(DC):
                        for n, (x, y) in enumerate(PARTS):
                            for m in range(NB):
                                ins = pe.matmul(banks[t][0:TOK, m, 0:BW], query_t[x][:, c, TOK * t:TOK * (t + 1)],
                                                xnT[y][:, c, BW * m:BW * (m + 1)], start=(c == 0 and n == 0),
                                                stop=(c == DC - 1 and n == 2))
                    ins.then_inc(scored, 1)
                if not last:
                    pe.wait_ge(added, 2 * nth - 1)
                    query(g + 1)
                for t in range(2):
                    pe.wait_ge(weighted, 2 * nth + 1 + t)
                    for s in range(NT):
                        ins = pe.transpose(banks[t][0:TOK, s // 4, TOK * (s % 4):TOK * (s % 4 + 1)],
                                           score[t][:, TOK * s:TOK * (s + 1)], ident[0:TOK, 0:TOK])
                    ins.then_inc(turned, 1)
                if last:
                    pe.wait_ge(added, 2 * nth - 1)
                else:
                    pe.wait_ge(query_ready, 4 * nth + 4)
                pe.wait_ge(value_ready, NT * h + NT)
                for t in range(2):
                    pe.wait_ge(prob_t_ready, 2 * nth - 1 + t)
                    for s in range(NT):
                        for n, (x, y) in enumerate(PARTS):
                            ins = pe.matmul(bank_c[0:TOK, t, :], prob_t[x][:, s, TOK * t:TOK * (t + 1)], value[y][:, s, :],
                                            start=(s == 0 and n == 0), stop=(s == NT - 1 and n == 2))
                    ins.then_inc(out_done, 1)

            pe.sem_inc(query_done, 1)
            with pe.Fori(0, HEADS) as h:
                pe.wait_ge(value_w_ready, h + 1)
                for s in range(NT):
                    bank = (bank_a, bank_b)[(s // 2) % 2]
                    if s >= 4:
                        pe.wait_ge(value_summed, NT * h + s - 3)
                    for c in range(DC):
                        for n, (x, y) in enumerate(PARTS):
                            ins = pe.matmul(bank[0:TOK, s % 2, :], xnT[x][:, c, TOK * s:TOK * (s + 1)],
                                            value_w[y][:, c, :], start=(c == 0 and n == 0), stop=(c == DC - 1 and n == 2))
                    ins.then_inc(value_done, 1)
                pe.wait_ge(query_w_ready, h + 2)
                pe.wait_ge(added, 2 * NG * h + 1)
                query(0)
                groups(pe, group, h)


def wide(bank, rows, n=N):
    return ((bank[rows, 0:2, 0:500], slice(0, 1000)), (bank[rows, 2, 0:250], slice(1000, 1250)))


def stage_mix(nc, xrow, ident, w_qkv, w_out, norm_gamma, mixed):
    FEAT = MIX_HEADS * MIX_DIM
    with ExitStack() as outer:
        b = Buffers(nc, outer)
        xm_t = [b.sb(f"m_xm_t_{k}", [P, DC, N], F32R) for k in ("hi", "lo")]
        wt = [[b.sb(f"m_wt_{i}_{k}", [P, DC, FEAT], F32R) for k in ("hi", "lo")] for i in "qkv"]
        shared = b.sb("m_shared", [P, NT * D])
        raw = [shared[:, 2048 * i:2048 * (i + 1)].rearrange("p (c n) -> p c n", c=DC) for i in range(2)]
        key = shared[0:TOK, :].rearrange("p (t n) -> p t n", t=NT)
        w_out_raw = b.sb("m_w_out_raw", [P, DC, FEAT])
        w_out_loaded = b.sem("m_w_out_loaded")

        with ExitStack() as ctx:
            b = Buffers(nc, ctx)
            stats = b.sb("m_stats", [TOK, NT, 6])
            mean_var = b.sb("m_mean_var", [TOK, NT, 2])
            root_in = b.sb("m_root_in", [TOK, NT])
            root = b.sb("m_root", [TOK, NT])
            scratch = b.sb("m_scratch", [TOK, NT])
            rstd = b.sb("m_rstd", [TOK, NT])
            gamma_in = b.sb("m_gamma_in", [DC, P])
            gamma = b.sb("m_gamma", [P, DC])
            bank = [b.ps(f"m_bank{i}", [P, 512]) for i in range(4)]
            gamma_bank = b.ps("m_gamma_bank", [P, 512])
            gamma_loaded = b.sem("m_gamma_loaded")
            gamma_turned = b.sem("m_gamma_turned")
            gamma_ready = b.sem("m_gamma_ready")
            raw_loaded = [b.sem(f"m_raw_loaded{i}") for i in range(2)]
            dve_step = b.sem("m_dve_step")
            var_ready = b.sem("m_var_ready")
            root_ready = b.sem("m_root_ready")
            row_ready = b.sem("m_row_ready")
            turned = b.sem("m_turned")
            hi_ready = b.sem("m_hi_ready")
            lo_ready = b.sem("m_lo_ready")
            block = ctx.enter_context(nc.Block())
            units = [("w", i, c) for i in range(3) for c in range(DC)] + [("x", g, c) for g in range(3) for c in range(DC)]

            def place(kind, i, c):
                if kind == "w":
                    return [wt[i][k][:, c, :] for k in range(2)], FEAT
                n = TOK * len(tile_parts(i))
                return [xm_t[k][:, c, 500 * i:500 * i + n] for k in range(2)], n

            @block.sync
            def _(sp):
                sp.dma_start(gamma_in[:, :], norm_gamma.rearrange("(c p) -> c p", p=P)).then_inc(gamma_loaded, 16)
                for i in range(3):
                    if i == 2:
                        sp.wait_ge(turned, DC)
                    sp.dma_start(raw[i % 2][:, :, :], w_qkv[FEAT * i:FEAT * (i + 1), :].rearrange(
                        "(r p) n -> p r n", p=P)).then_inc(raw_loaded[i % 2], 16)
                sp.dma_start(w_out_raw[:, :, :], w_out.rearrange("(r p) n -> p r n", p=P)).then_inc(w_out_loaded, 16)

            @block.vector
            def _(dve):
                link = chain(dve, dve_step)
                node_stats(dve, link, xrow, stats, mean_var, root_in).then_inc(var_ready, 1)
                dve.wait_ge(root_ready, 1)
                inverse_root(dve, link, root_in[:, :], root[:, :], scratch[:, :], rstd[:, :])
                for t in range(NT):
                    dve.tensor_scalar(xrow[:, t, :], xrow[:, t, :], mean_var[:, t, 0:1], rstd[:, t:t + 1],
                                      ALU.subtract, ALU.mult).then_inc(row_ready, 1)
                dve.wait_ge(gamma_turned, 1)
                dve.tensor_copy(gamma[:, :], gamma_bank[:, 0:DC]).then_inc(gamma_ready, 1)
                dve.wait_ge(gamma_ready, 1)
                for u, (kind, i, c) in enumerate(units):
                    (hi, lo), n = place(kind, i, c)
                    dve.wait_ge(hi_ready, u + 1)
                    if kind == "w":
                        ins = dve.tensor_tensor(lo, bank[u % 4][:, 0:n], hi.bitcast(F32), ALU.subtract)
                    else:
                        ins = dve.scalar_tensor_tensor(lo, bank[u % 4][:, 0:n], gamma[:, c:c + 1], hi.bitcast(F32),
                                                       ALU.mult, ALU.subtract)
                    ins.then_inc(lo_ready, 1)

            @block.scalar
            def _(act):
                act.wait_ge(var_ready, 1)
                act.activation(root[:, :], root_in[:, :], ACT.Sqrt).then_inc(root_ready, 1)
                act.wait_ge(gamma_ready, 1)
                for u, (kind, i, c) in enumerate(units):
                    (hi, lo), n = place(kind, i, c)
                    act.wait_ge(turned, u + 1)
                    act.activation(hi, bank[u % 4][:, 0:n], ACT.Copy,
                                   scale=1.0 if kind == "w" else gamma[:, c:c + 1]).then_inc(hi_ready, 1)

            @block.tensor
            def _(pe):
                pe.wait_ge(gamma_loaded, 16)
                pe.transpose(gamma_bank[:, 0:DC], gamma_in[:, :], ident[0:DC, 0:DC]).then_inc(gamma_turned, 1)
                for u, (kind, i, c) in enumerate(units):
                    if u >= 4:
                        pe.wait_ge(lo_ready, u - 3)
                    if kind == "w":
                        pe.wait_ge(raw_loaded[i % 2], 16 * (i // 2 + 1))
                        for r in range(DC):
                            ins = pe.transpose(bank[u % 4][:, P * r:P * (r + 1)], raw[i % 2][:, r, P * c:P * (c + 1)],
                                               ident[:, :])
                    else:
                        pe.wait_ge(row_ready, tile_parts(i)[-1] + 1)
                        for j, t in enumerate(tile_parts(i)):
                            ins = pe.transpose(bank[u % 4][:, TOK * j:TOK * (j + 1)], xrow[:, t, P * c:P * (c + 1)],
                                               ident[0:TOK, 0:TOK])
                    ins.then_inc(turned, 1)

        with ExitStack() as ctx:
            b = Buffers(nc, ctx)
            value = xrow
            key_exp = [b.sb(f"m_key_exp{i}", [P, N]) for i in range(2)]
            key_top = b.sb("m_key_top", [P, DC])
            key_sum = b.sb("m_key_sum", [P, DC])
            key_scale = b.sb("m_key_scale", [P, DC])
            context = [b.sb(f"m_context_{k}", [P, DC, P], F32R) for k in ("hi", "lo")]
            key_bank = [b.ps(f"m_key_bank{i}", [P, 3, 512]) for i in range(2)]
            row_bank = [b.ps(f"m_row_bank{i}", [P, 512]) for i in range(2)]
            key_done = b.sem("m_key_done")
            key_copied = b.sem("m_key_copied")
            top_ready = b.sem("m_top_ready")
            exp_done = b.sem("m_exp_done")
            key_turned = b.sem("m_key_turned")
            key_ready = b.sem("m_key_ready")
            row_done = b.sem("m_row_done")
            row_hi = b.sem("m_row_hi")
            row_ready = b.sem("m_row2_ready")
            clear = b.sem("m_clear")
            scale_ready = b.sem("m_scale_ready")
            dve_step = b.sem("m_dve_step2")
            block = ctx.enter_context(nc.Block())
            VALUES, TURNS, CONTEXTS = 0, NT, NT + DC
            PRODUCTS = NT + 2 * DC
            USES = NT + 3 * DC

            @block.gpsimd
            def _(pool):
                for k in range(2):
                    pool.memset(context[k][:, :, :].bitcast(F32), 0.0).then_inc(clear, 1)

            @block.scalar
            def _(act):
                def key_part(f):
                    act.wait_ge(key_done, f + 1)
                    for part, cols in wide(key_bank[f % 2], slice(0, P)):
                        out = key_exp[f % 2][:, cols]
                        ins = act.activation(out.rearrange("p (b n) -> p b n", n=500) if cols.start == 0 else out,
                                             part, ACT.Copy)
                    ins.then_inc(key_copied, 1)
                    act.wait_ge(top_ready, f + 1)
                    act.activation(key_exp[f % 2][:, :], key_exp[f % 2][:, :], ACT.Exp, bias=key_top[:, f:f + 1],
                                   accum_out=key_sum[:, f:f + 1]).then_inc(exp_done, 1)

                def row(u):
                    act.wait_ge(row_done, u + 1)
                    src = row_bank[u % 2]
                    if u < TURNS:
                        act.activation(value[:, u, :], src[0:TOK, :], ACT.Copy).then_inc(row_hi, 1)
                    elif u < CONTEXTS:
                        act.activation(wt[2][0][:, u - TURNS, :], src[:, :], ACT.Copy).then_inc(row_hi, 1)
                    elif u < PRODUCTS:
                        f = u - CONTEXTS
                        act.activation(context[0][0:64, f, 0:64], src[0:64, 0:64], ACT.Copy)
                        act.activation(context[0][64:128, f, 64:128], src[64:128, 64:128], ACT.Copy).then_inc(row_hi, 1)
                    else:
                        f = u - PRODUCTS
                        act.activation(wt[1][0][:, f, :], src[:, :], ACT.Copy, scale=key_scale[:, f:f + 1]).then_inc(row_hi, 1)

                key_part(0)
                key_part(1)
                for u in range(5):
                    row(u)
                key_part(2)
                key_part(3)
                for u in range(5, CONTEXTS):
                    row(u)
                act.wait_ge(clear, 2)
                act.wait_ge(scale_ready, 1)
                for u in range(CONTEXTS, USES):
                    row(u)

            @block.vector
            def _(dve):
                link = chain(dve, dve_step)

                def top(f):
                    dve.wait_ge(key_copied, f + 1)
                    dve.tensor_reduce(key_top[:, f:f + 1], key_exp[f % 2][:, :], AX.X, ALU.max,
                                      negate=True).then_inc(top_ready, 1)

                def turn(f):
                    dve.wait_ge(key_turned, f + 1)
                    for part, tiles in ((key_bank[f % 2][0:TOK, 0:2, :], slice(0, 8)), (key_bank[f % 2][0:TOK, 2, 0:256], slice(8, 10))):
                        out = key[:, tiles, P * f:P * (f + 1)]
                        ins = dve.tensor_copy(out.rearrange("p (b i) n -> p b i n", i=4) if tiles.start == 0 else out,
                                              part.rearrange("p b (i n) -> p b i n", n=P) if tiles.start == 0
                                              else part.rearrange("p (i n) -> p i n", n=P))
                    ins.then_inc(key_ready, 1)

                def row(u):
                    dve.wait_ge(row_hi, u + 1)
                    src = row_bank[u % 2]
                    if u < CONTEXTS:
                        f = u - TURNS
                        dve.tensor_tensor(wt[2][1][:, f, :], src[:, :], wt[2][0][:, f, :].bitcast(F32),
                                          ALU.subtract).then_inc(row_ready, 1)
                    elif u < PRODUCTS:
                        f = u - CONTEXTS
                        for lo in (0, 64):
                            at = slice(lo, lo + 64)
                            ins = dve.tensor_tensor(context[1][at, f, at], src[at, at], context[0][at, f, at].bitcast(F32),
                                                    ALU.subtract)
                        ins.then_inc(row_ready, 1)
                    else:
                        f = u - PRODUCTS
                        dve.scalar_tensor_tensor(wt[1][1][:, f, :], src[:, :], key_scale[:, f:f + 1],
                                                 wt[1][0][:, f, :].bitcast(F32), ALU.mult, ALU.subtract
                                                 ).then_inc(row_ready, 1)

                top(0)
                top(1)
                turn(0)
                top(2)
                turn(1)
                top(3)
                turn(2)
                turn(3)
                for u in range(TURNS, CONTEXTS):
                    row(u)
                dve.wait_ge(exp_done, DC)
                link(dve.reciprocal(key_scale[:, :], key_sum[:, :]))
                dve.tensor_scalar(key_scale[:, :], key_scale[:, :], MIX_DIM ** -0.5, None, ALU.mult).then_inc(scale_ready, 1)
                dve.wait_ge(scale_ready, 1)
                dve.wait_ge(clear, 2)
                for u in range(CONTEXTS, USES):
                    row(u)

            @block.tensor
            def _(pe):
                def keys(f):
                    if f >= 2:
                        pe.wait_ge(key_ready, f - 1)
                    for c in range(DC):
                        for n, (x, y) in enumerate(PARTS):
                            for m, w in enumerate((500, 500, 250)):
                                ins = pe.matmul(key_bank[f % 2][:, m, 0:w], wt[1][x][:, c, P * f:P * (f + 1)],
                                                xm_t[y][:, c, 500 * m:500 * m + w], start=(c == 0 and n == 0),
                                                stop=(c == DC - 1 and n == 2))
                    ins.then_inc(key_done, 1)

                def turn(f):
                    pe.wait_ge(exp_done, f + 1)
                    for t in range(NT):
                        ins = pe.transpose(key_bank[f % 2][0:TOK, t // 4, P * (t % 4):P * (t % 4 + 1)],
                                           key_exp[f % 2][:, TOK * t:TOK * (t + 1)], ident[:, :])
                    ins.then_inc(key_turned, 1)

                def bank_free(u):
                    if u >= 2:
                        if u - 2 < TURNS:
                            pe.wait_ge(row_hi, u - 1)
                        else:
                            pe.wait_ge(row_ready, u - 1 - TURNS)

                def values(t):
                    bank_free(t)
                    for c in range(DC):
                        for n, (x, y) in enumerate(PARTS):
                            ins = pe.matmul(row_bank[t % 2][0:TOK, :], xm_t[x][:, c, TOK * t:TOK * (t + 1)],
                                            wt[2][y][:, c, :], start=(c == 0 and n == 0), stop=(c == DC - 1 and n == 2))
                    ins.then_inc(row_done, 1)

                keys(0)
                keys(1)
                for t in range(5):
                    values(t)
                turn(0)
                keys(2)
                turn(1)
                keys(3)
                for t in range(5, NT):
                    values(t)
                turn(2)
                turn(3)
                pe.wait_ge(w_out_loaded, 16)
                for f in range(DC):
                    u = TURNS + f
                    bank_free(u)
                    for r in range(DC):
                        ins = pe.transpose(row_bank[u % 2][:, P * r:P * (r + 1)], w_out_raw[:, r, P * f:P * (f + 1)], ident[:, :])
                    ins.then_inc(row_done, 1)
                for f in range(DC):
                    u = CONTEXTS + f
                    bank_free(u)
                    pe.wait_ge(key_ready, DC)
                    for t in range(NT):
                        ins = pe.matmul(row_bank[u % 2][:, 0:P], value[:, t, P * f:P * (f + 1)], key[:, t, P * f:P * (f + 1)],
                                        start=(t == 0), stop=(t == NT - 1))
                    ins.then_inc(row_done, 1)
                for f in range(DC):
                    u = PRODUCTS + f
                    pe.wait_ge(row_ready, DC + f + 1)
                    bank_free(u)
                    for n, (x, y) in enumerate(PARTS):
                        ins = pe.matmul(row_bank[u % 2][:, :], context[x][:, f, :], wt[2][y][:, f, :], start=(n == 0), stop=(n == 2))
                    ins.then_inc(row_done, 1)

            @block.sync
            def _(sp):
                sp.wait_ge(w_out_loaded, 16)

        with ExitStack() as ctx:
            b = Buffers(nc, ctx)
            query = [b.sb(f"m_query{i}", [TOK, FEAT]) for i in range(2)]
            top = b.sb("m_top", [TOK, 2, MIX_HEADS])
            total = b.sb("m_total", [TOK, 2, MIX_HEADS])
            query_t = [b.sb(f"m_query_t_{k}", [P, DC, TOK], F32R) for k in ("hi", "lo")]
            out_row = [b.sb(f"m_out_row{i}", [TOK, D]) for i in range(2)]
            query_bank = [b.ps(f"m_query_bank{i}", [P, 512]) for i in range(2)]
            turn_bank = b.ps("m_turn_bank", [P, 512])
            out_bank = [b.ps(f"m_out_bank{i}", [P, 512]) for i in range(2)]
            query_done = b.sem("m_query_done")
            centred = b.sem("m_centred")
            exp_done = b.sem("m_exp_done2")
            query_ready = b.sem("m_query_ready")
            turned = b.sem("m_turned2")
            turn_hi = b.sem("m_turn_hi")
            turn_ready = b.sem("m_turn_ready")
            out_done = b.sem("m_out_done")
            out_copied = b.sem("m_out_copied")
            stored = [b.sem(f"m_stored{i}") for i in range(2)]
            dve_step = b.sem("m_dve_step3")
            block = ctx.enter_context(nc.Block())

            def heads(ap):
                return ap.rearrange("p (h e) -> p h e", h=MIX_HEADS)

            def spread(ap):
                return ap.unsqueeze(2).to_broadcast([TOK, MIX_HEADS, MIX_DIM])

            @block.sync
            def _(sp):
                for t in range(NT):
                    sp.wait_ge(out_copied, t + 1)
                    sp.dma_start(mixed[TOK * t:TOK * (t + 1), :], out_row[t % 2][:, :]).then_inc(stored[t % 2], 16)
                for i in range(2):
                    sp.wait_ge(stored[i], 16 * NT // 2)

            @block.scalar
            def _(act):
                def out(t):
                    act.wait_ge(out_done, t + 1)
                    if t >= 2:
                        act.wait_ge(stored[t % 2], 16 * (t // 2))
                    act.activation(out_row[t % 2][:, :], out_bank[t % 2][0:TOK, :], ACT.Copy).then_inc(out_copied, 1)

                for t in range(NT):
                    act.wait_ge(centred, t + 1)
                    act.activation(query[t % 2][:, :], query[t % 2][:, :], ACT.Exp).then_inc(exp_done, 1)
                    act.wait_ge(turned, t + 1)
                    act.activation(query_t[0][:, :, :].rearrange("p c n -> p (c n)"), turn_bank[:, 0:4 * TOK],
                                   ACT.Copy).then_inc(turn_hi, 1)
                    if t:
                        out(t - 1)
                out(NT - 1)

            @block.vector
            def _(dve):
                link = chain(dve, dve_step)

                def centre(t):
                    dve.wait_ge(query_done, t + 1)
                    link(dve.tensor_reduce(top[:, t % 2, :], heads(query_bank[t % 2][0:TOK, :]), AX.X, ALU.max))
                    dve.tensor_tensor(heads(query[t % 2][:, :]), heads(query_bank[t % 2][0:TOK, :]), spread(top[:, t % 2, :]),
                                      ALU.subtract).then_inc(centred, 1)

                centre(0)
                for t in range(NT):
                    dve.wait_ge(exp_done, t + 1)
                    link(dve.tensor_reduce(total[:, t % 2, :], heads(query[t % 2][:, :]), AX.X, ALU.add))
                    link(dve.reciprocal(total[:, t % 2, :], total[:, t % 2, :]))
                    dve.tensor_tensor(heads(query[t % 2][:, :]), heads(query[t % 2][:, :]), spread(total[:, t % 2, :]),
                                      ALU.mult).then_inc(query_ready, 1)
                    if t + 1 < NT:
                        centre(t + 1)
                    dve.wait_ge(turn_hi, t + 1)
                    dve.tensor_tensor(query_t[1][:, :, :].rearrange("p c n -> p (c n)"), turn_bank[:, 0:4 * TOK],
                                      query_t[0][:, :, :].rearrange("p c n -> p (c n)").bitcast(F32),
                                      ALU.subtract).then_inc(turn_ready, 1)

            @block.tensor
            def _(pe):
                def queries(t):
                    if t >= 2:
                        pe.wait_ge(centred, t - 1)
                    for c in range(DC):
                        for n, (x, y) in enumerate(PARTS):
                            ins = pe.matmul(query_bank[t % 2][0:TOK, :], xm_t[x][:, c, TOK * t:TOK * (t + 1)],
                                            wt[0][y][:, c, :], start=(c == 0 and n == 0), stop=(c == DC - 1 and n == 2))
                    ins.then_inc(query_done, 1)

                def outs(t):
                    pe.wait_ge(turn_ready, t + 1)
                    if t >= 2:
                        pe.wait_ge(out_copied, t - 1)
                    for f in range(DC):
                        for n, (x, y) in enumerate(PARTS):
                            ins = pe.matmul(out_bank[t % 2][0:TOK, :], query_t[x][:, f, :], wt[1][y][:, f, :],
                                            start=(f == 0 and n == 0), stop=(f == DC - 1 and n == 2))
                    ins.then_inc(out_done, 1)

                queries(0)
                queries(1)
                for t in range(NT):
                    pe.wait_ge(query_ready, t + 1)
                    for f in range(DC):
                        ins = pe.transpose(turn_bank[:, TOK * f:TOK * (f + 1)], query[t % 2][:, P * f:P * (f + 1)],
                                           ident[0:TOK, 0:TOK])
                    ins.then_inc(turned, 1)
                    if t + 2 < NT:
                        queries(t + 2)
                    outs(t)


def stage_join(nc, x, hidden, mixed, gamma, beta, out_gamma, w_gate, ident, x1, xn2, route, slots_in):
    scatter_at, gather_at, weight, select_t, some, none = route
    E = EXPERTS
    with ExitStack() as ctx:
        b = Buffers(nc, ctx)
        rows = [b.sb(f"j_{k}", [TOK, NT, D]) for k in ("hidden", "mixed")]
        vec = [b.sb(f"j_vec{i}", [TOK, D]) for i in range(3)]
        stats = b.sb("j_stats", [TOK, 3, NT, 6])
        mean_var = b.sb("j_mean_var", [TOK, 3, NT, 2])
        root_in = b.sb("j_root_in", [TOK, 3, NT])
        root = b.sb("j_root", [TOK, 3, NT])
        scratch = b.sb("j_scratch", [TOK, 3, NT])
        rstd = b.sb("j_rstd", [TOK, 3, NT])
        zero = b.sb("j_zero", [CAP, D])
        xn2_t = b.sb("j_xn2_t", [P, DC, N])
        gate_w = b.sb("j_gate_w", [P, DC, E])
        before = b.sb("j_before", [TOK, TOK], BF16)
        ones = b.sb("j_ones", [TOK, TOK], BF16)
        expert_no = b.sb("j_expert_no", [TOK, E])
        dump = b.sb("j_dump", [TOK, TOPK, NT])
        prob = b.sb("j_prob", [TOK, NT, E])
        left = b.sb("j_left", [TOK, NT, E])
        same = b.sb("j_same", [TOK, NT, E])
        hot = b.sb("j_hot", [TOK, TOPK, NT, E])
        taken = b.sb("j_taken", [TOK, NT, E], BF16)
        best = b.sb("j_best", [TOK, TOPK, NT])
        expert = b.sb("j_expert", [TOK, TOPK, NT])
        rank = b.sb("j_rank", [TOK, TOPK, NT])
        keep = b.sb("j_keep", [TOK, TOPK, NT])
        dest = b.sb("j_dest", [TOK, TOPK, NT])
        place = b.sb("j_place", [TOK, TOPK, NT])
        norm = b.sb("j_norm", [TOK, NT])
        bank = [b.ps(f"j_bank{i}", [P, 512]) for i in range(4)]
        logit = b.ps("j_logit", [P, 512])
        rank_bank = b.ps("j_rank_bank", [P, 512])
        loaded = [b.sem(f"j_loaded{i}") for i in range(3)]
        vec_loaded = b.sem("j_vec_loaded")
        gate_loaded = b.sem("j_gate_loaded")
        consts = b.sem("j_consts")
        zero_ready = b.sem("j_zero_ready")
        cleared = b.sem("j_cleared")
        dve_step = b.sem("j_dve_step")
        var_ready = b.sem("j_var_ready")
        root_ready = b.sem("j_root_ready")
        normed = b.sem("j_normed")
        base_ready = b.sem("j_base_ready")
        pool_step = b.sem("j_pool_step")
        row_ready = b.sem("j_row_ready")
        turned = b.sem("j_turned")
        copied = b.sem("j_copied")
        gated = b.sem("j_gated")
        centred = b.sem("j_centred")
        exp_done = b.sem("j_exp_done")
        taken_ready = b.sem("j_taken_ready")
        ranked = b.sem("j_ranked")
        places_ready = b.sem("j_places_ready")
        select_ready = b.sem("j_select_ready")
        scattered = b.sem("j_scattered")
        block = ctx.enter_context(nc.Block())
        units = [(g, c) for g in range(3) for c in range(DC)]

        def tiles(dram):
            return dram.rearrange("(t p) c -> p t c", p=TOK)

        def over_experts(ap):
            return ap.unsqueeze(2).to_broadcast([TOK, NT, E])

        @block.sync
        def _(sp):
            sp.dma_start(rows[0][:, :, :], tiles(hidden)).then_inc(loaded[0], 16)
            sp.dma_start(rows[1][:, :, :], tiles(mixed)).then_inc(loaded[1], 16)
            sp.dma_start(x1[:, :, :], tiles(x)).then_inc(loaded[2], 16)
            for i, v in enumerate((gamma, beta, out_gamma)):
                sp.dma_start(vec[i][:, :], v.unsqueeze(0).to_broadcast([TOK, D])).then_inc(vec_loaded, 16)
            sp.dma_start(gate_w[:, :, :], w_gate.rearrange("(c p) e -> p c e", p=P)).then_inc(gate_loaded, 16)
            sp.wait_ge(zero_ready, 1)
            sp.dma_start(slots_in[0:SLOTS, :].rearrange("(e p) c -> p e c", p=CAP),
                         zero[:, :].unsqueeze(1).to_broadcast([CAP, E, D])).then_inc(cleared, 16)

        @block.gpsimd
        def _(pool):
            pool.memset(zero[:, :], 0.0).then_inc(zero_ready, 1)
            pool.memset(ones[:, :], 1.0).then_inc(consts, 1)
            pool.iota(expert_no[:, :], [[1, E]], base=-E, channel_multiplier=0,
                      allow_small_or_imprecise_dtypes=True).then_inc(consts, 1)
            pool.iota(dump[:, :, :], [[N, TOPK], [TOK, NT]], base=SLOTS, channel_multiplier=1,
                      allow_small_or_imprecise_dtypes=True).then_inc(consts, 1)
            pool.wait_ge(consts, 3)
            pool.affine_select(out=before[:, :], in_=ones[:, :], compare_op=ALU.is_gt, fill=0.0, base=0,
                               pattern=[[1, TOK]], channel_multiplier=-1).then_inc(consts, 1)
            pool.wait_ge(vec_loaded, 48)
            pool.wait_ge(loaded[2], 16)
            steps = 0
            for t in range(NT):
                pool.wait_ge(normed, t + 1)
                for out, other, op in ((rows[1], vec[2][:, :], ALU.mult), (x1, vec[1][:, :], ALU.add), (x1, rows[1][:, t, :], ALU.add)):
                    pool.tensor_tensor(out[:, t, :], out[:, t, :], other, op).then_inc(pool_step, 1)
                    steps += 1
                    pool.wait_ge(pool_step, steps)
                pool.sem_inc(base_ready, 1)
            pool.wait_ge(cleared, 16)
            pool.wait_ge(places_ready, 1)
            for k in range(TOPK):
                for t in range(NT):
                    pool.indirect_dma_start(
                        out=slots_in[:, :],
                        out_offset=bass.IndirectOffsetOnAxis(ap=scatter_at[:, k * NT + t:k * NT + t + 1], axis=0),
                        in_=xn2[:, t, :], in_offset=None).then_inc(scattered, 16)
            pool.wait_ge(scattered, 16 * TOPK * NT)

        @block.scalar
        def _(act):
            act.wait_ge(var_ready, 1)
            act.activation(root[:, 0:2, :], root_in[:, 0:2, :], ACT.Sqrt).then_inc(root_ready, 1)
            act.wait_ge(var_ready, 2)
            act.activation(root[:, 2, :], root_in[:, 2, :], ACT.Sqrt).then_inc(root_ready, 1)
            for u, (g, c) in enumerate(units):
                n = TOK * len(tile_parts(g))
                act.wait_ge(turned, u + 1)
                act.activation(xn2_t[:, c, 500 * g:500 * g + n], bank[u % 4][:, 0:n], ACT.Copy).then_inc(copied, 1)
            act.wait_ge(centred, 1)
            act.activation(prob[:, :, :], prob[:, :, :], ACT.Exp).then_inc(exp_done, 1)
            for t in range(NT):
                act.wait_ge(turned, len(units) + t + 1)
                act.activation(select_t[:, TOK * t:TOK * (t + 1)], bank[t % 4][0:E, 0:TOK], ACT.Copy).then_inc(copied, 1)

        @block.vector
        def _(dve):
            link = chain(dve, dve_step)

            def moments(i, source):
                for t in range(NT):
                    ins = dve.bn_stats(stats[:, i, t, :], source[:, t, :])
                link(ins)
                for t in range(NT):
                    ins = dve.bn_aggr(mean_var[:, i, t, :], stats[:, i, t, :])
                link(ins)
                return dve.tensor_scalar(root_in[:, i, :], mean_var[:, i, :, 1], EPS, None, ALU.add)

            for i in range(2):
                dve.wait_ge(loaded[i], 16)
                ins = moments(i, rows[i])
            ins.then_inc(var_ready, 1)
            dve.wait_ge(root_ready, 1)
            for i in (1, 0):
                inverse_root(dve, link, root_in[:, i, :], root[:, i, :], scratch[:, i, :], rstd[:, i, :])
                for t in range(NT):
                    ins = dve.tensor_scalar(rows[i][:, t, :], rows[i][:, t, :], mean_var[:, i, t, 0:1], rstd[:, i, t:t + 1],
                                            ALU.subtract, ALU.mult)
                    if i == 1:
                        ins.then_inc(normed, 1)
                if i == 0:
                    link(ins)
            dve.wait_ge(vec_loaded, 48)
            for t in range(NT):
                ins = dve.tensor_tensor(rows[0][:, t, :], rows[0][:, t, :], vec[0][:, :], ALU.mult)
            link(ins)
            for t in range(NT):
                dve.wait_ge(base_ready, t + 1)
                ins = dve.tensor_tensor(x1[:, t, :], x1[:, t, :], rows[0][:, t, :], ALU.add)
            link(ins)
            moments(2, x1).then_inc(var_ready, 1)
            dve.wait_ge(root_ready, 2)
            inverse_root(dve, link, root_in[:, 2, :], root[:, 2, :], scratch[:, 2, :], rstd[:, 2, :])
            for t in range(NT):
                dve.tensor_scalar(xn2[:, t, :], x1[:, t, :], mean_var[:, 2, t, 0:1], rstd[:, 2, t:t + 1],
                                  ALU.subtract, ALU.mult).then_inc(row_ready, 1)

            dve.wait_ge(gated, 1)
            dve.wait_ge(consts, 4)
            logits = logit[0:TOK, 0:NT * E].rearrange("p (t e) -> p t e", e=E)
            link(dve.tensor_reduce(norm[:, :], logits, AX.X, ALU.max))
            dve.tensor_tensor(prob[:, :, :], logits, over_experts(norm[:, :]), ALU.subtract).then_inc(centred, 1)
            dve.wait_ge(exp_done, 1)
            link(dve.tensor_reduce(norm[:, :], prob[:, :, :], AX.X, ALU.add))
            link(dve.reciprocal(norm[:, :], norm[:, :]))
            link(dve.tensor_tensor(prob[:, :, :], prob[:, :, :], over_experts(norm[:, :]), ALU.mult))
            number = expert_no[:, :].unsqueeze(1).to_broadcast([TOK, NT, E])
            for k in range(TOPK):
                source = (prob, left)[k]
                link(dve.tensor_reduce(best[:, k, :], source[:, :, :], AX.X, ALU.max))
                link(dve.tensor_tensor(same[:, :, :], source[:, :, :], over_experts(best[:, k, :]), ALU.is_equal))
                link(dve.tensor_tensor(same[:, :, :], same[:, :, :], number, ALU.mult))
                link(dve.tensor_reduce(expert[:, k, :], same[:, :, :], AX.X, ALU.min))
                link(dve.tensor_tensor(hot[:, k, :, :], over_experts(expert[:, k, :]), number, ALU.is_equal))
                if k == 0:
                    link(dve.scalar_tensor_tensor(left[:, :, :], hot[:, 0, :, :], -2.0, prob[:, :, :], ALU.mult, ALU.add))
            dve.tensor_tensor(taken[:, :, :], hot[:, 0, :, :], hot[:, 1, :, :], ALU.add).then_inc(taken_ready, 1)
            link(dve.tensor_tensor(norm[:, :], best[:, 0, :], best[:, 1, :], ALU.add))
            link(dve.tensor_scalar(norm[:, :], norm[:, :], 1e-9, None, ALU.max))
            link(dve.reciprocal(norm[:, :], norm[:, :]))
            dve.wait_ge(ranked, 1)
            ranks = rank_bank[0:TOK, 0:NT * E].rearrange("p (t e) -> p t e", e=E)
            for k in range(TOPK):
                link(dve.tensor_tensor(same[:, :, :], hot[:, k, :, :], ranks, ALU.mult))
                link(dve.tensor_reduce(rank[:, k, :], same[:, :, :], AX.X, ALU.add))
            dve.tensor_scalar(keep[:, :, :], rank[:, :, :], float(CAP), None, ALU.is_lt)
            link(dve.scalar_tensor_tensor(dest[:, :, :], expert[:, :, :], float(CAP), rank[:, :, :], ALU.mult, ALU.add))
            link(dve.tensor_scalar(dest[:, :, :], dest[:, :, :], float(E * CAP), None, ALU.add))
            link(dve.tensor_tensor(place[:, :, :], dest[:, :, :], dump[:, :, :], ALU.subtract))
            link(dve.tensor_tensor(place[:, :, :], place[:, :, :], keep[:, :, :], ALU.mult))
            link(dve.tensor_tensor(place[:, :, :], place[:, :, :], dump[:, :, :], ALU.add))
            dve.tensor_copy(scatter_at[:, :], place[:, :, :].rearrange("p k t -> p (k t)")).then_inc(places_ready, 1)
            dve.wait_ge(places_ready, 1)
            link(dve.scalar_tensor_tensor(place[:, :, :], dest[:, :, :], -float(SLOTS - 1), keep[:, :, :], ALU.add, ALU.mult))
            link(dve.tensor_scalar(place[:, :, :], place[:, :, :], float(SLOTS - 1), None, ALU.add))
            link(dve.tensor_copy(gather_at[:, :], place[:, :, :].rearrange("p k t -> p (k t)")))
            link(dve.tensor_tensor(weight[:, :, :], best[:, :, :], norm[:, :].unsqueeze(1).to_broadcast([TOK, TOPK, NT]), ALU.mult))
            link(dve.tensor_tensor(weight[:, :, :], weight[:, :, :], keep[:, :, :], ALU.mult))
            link(dve.tensor_tensor(norm[:, :], weight[:, 0, :], weight[:, 1, :], ALU.add))
            dve.tensor_scalar(none[:, :], norm[:, :], 1e-12, None, ALU.is_le)
            link(dve.tensor_scalar(some[:, :], norm[:, :], 1e-12, None, ALU.is_gt))
            for k in range(TOPK):
                link(dve.tensor_tensor(hot[:, k, :, :], hot[:, k, :, :], over_experts(weight[:, k, :]), ALU.mult))
            dve.tensor_tensor(same[:, :, :], hot[:, 0, :, :], hot[:, 1, :, :], ALU.add).then_inc(select_ready, 1)

        @block.tensor
        def _(pe):
            for u, (g, c) in enumerate(units):
                if u >= 4:
                    pe.wait_ge(copied, u - 3)
                pe.wait_ge(row_ready, tile_parts(g)[-1] + 1)
                for i, t in enumerate(tile_parts(g)):
                    ins = pe.transpose(bank[u % 4][:, TOK * i:TOK * (i + 1)], xn2[:, t, P * c:P * (c + 1)],
                                       ident[0:TOK, 0:TOK])
                ins.then_inc(turned, 1)
            pe.wait_ge(gate_loaded, 16)
            pe.wait_ge(copied, len(units))
            for t in range(NT):
                for c in range(DC):
                    ins = pe.matmul(logit[0:TOK, E * t:E * (t + 1)], xn2_t[:, c, TOK * t:TOK * (t + 1)], gate_w[:, c, :],
                                    start=(c == 0), stop=(c == DC - 1))
            ins.then_inc(gated, 1)
            pe.wait_ge(taken_ready, 1)
            for t in range(NT):
                for s in range(t + 1):
                    ins = pe.matmul(rank_bank[0:TOK, E * t:E * (t + 1)], (before if s == t else ones)[:, :], taken[:, s, :],
                                    start=(s == 0), stop=(s == t))
            ins.then_inc(ranked, 1)
            pe.wait_ge(select_ready, 1)
            for t in range(NT):
                if t >= 4:
                    pe.wait_ge(copied, len(units) + t - 3)
                pe.transpose(bank[t % 4][0:E, 0:TOK], same[:, t, :], ident[0:TOK, 0:TOK]).then_inc(turned, 1)


def stage_experts(nc, slots_in, slots_out, w1, b1, w2, ident):
    E = EXPERTS
    with ExitStack() as ctx:
        b = Buffers(nc, ctx)
        up = [b.sb(f"e_up{i}", [P, DC, D]) for i in range(2)]
        down = [b.sb(f"e_down{i}", [P, DC, D]) for i in range(2)]
        rows = [b.sb(f"e_rows{i}", [CAP, D]) for i in range(2)]
        rows_t = [b.sb(f"e_rows_t{i}", [P, DC, CAP]) for i in range(2)]
        mid_t = [b.sb(f"e_mid_t{i}", [P, DC, CAP]) for i in range(2)]
        out = [b.sb(f"e_out{i}", [CAP, D]) for i in range(2)]
        bias_in = b.sb("e_bias_in", [E, D])
        bias_t = b.sb("e_bias_t", [P, DC, E])
        turn_bank = [b.ps(f"e_turn_bank{i}", [P, 512]) for i in range(2)]
        mid_bank = [b.ps(f"e_mid_bank{i}", [P, 512]) for i in range(2)]
        out_bank = [b.ps(f"e_out_bank{i}", [P, 512]) for i in range(2)]
        bias_loaded = b.sem("e_bias_loaded")
        bias_turned = b.sem("e_bias_turned")
        bias_ready = b.sem("e_bias_ready")
        up_loaded = [b.sem(f"e_up_loaded{i}") for i in range(2)]
        down_loaded = [b.sem(f"e_down_loaded{i}") for i in range(2)]
        rows_loaded = [b.sem(f"e_rows_loaded{i}") for i in range(2)]
        stored = [b.sem(f"e_stored{i}") for i in range(2)]
        turned = b.sem("e_turned")
        rows_ready = b.sem("e_rows_ready")
        mid_done = b.sem("e_mid_done")
        mid_ready = b.sem("e_mid_ready")
        out_done = b.sem("e_out_done")
        out_ready = b.sem("e_out_ready")
        block = ctx.enter_context(nc.Block())


        @block.sync
        def _(sp):
            sp.dma_start(bias_in[:, :], b1).then_inc(bias_loaded, 16)
            with sp.Fori(0, E // 2) as i:
                for k in range(2):
                    e = 2 * i + k
                    sp.wait_ge(turned, e + 1)
                    sp.dma_start(rows[k][:, :], slots_in[bass.ds(e * CAP, CAP), :]).then_inc(rows_loaded[k], 16)
                    sp.wait_ge(mid_done, e + 1)
                    sp.dma_start(up[k][:, :, :], w1[bass.ds(e, 1), :, :].rearrange("o (c p) n -> p (o c) n", p=P)
                                 ).then_inc(up_loaded[k], 16)
                    sp.wait_ge(out_done, e + 1)
                    sp.dma_start(down[k][:, :, :], w2[bass.ds(e, 1), :, :].rearrange("o (c p) n -> p (o c) n", p=P)
                                 ).then_inc(down_loaded[k], 16)

        @block.scalar
        def _(act):
            def rows_out(i, k):
                act.wait_ge(turned, 2 * i + k + 3)
                act.activation(rows_t[k][:, :, :].rearrange("p c n -> p (c n)"), turn_bank[k][:, 0:DC * CAP],
                               ACT.Copy).then_inc(rows_ready, 1)

            rows_out(0, 0)
            act.sem_inc(stored[0], 16)
            act.sem_inc(stored[1], 16)

            def expert(i, k, last):
                if not last:
                    rows_out(i + (k == 1), 1 - k)
                act.wait_ge(out_done, 2 * i + k + 3)
                act.wait_ge(stored[k], 16 * i + 16)
                act.activation(out[k][:, :], out_bank[k][0:CAP, :], ACT.Copy).then_inc(out_ready, 1)
                act.wait_ge(out_ready, 2 * i + k + 3)
                act.dma_start(slots_out[bass.ds((2 * i + k) * CAP, CAP), :], out[k][:, :]).then_inc(stored[k], 16)

            with act.Fori(0, E // 2 - 1) as i:
                expert(i, 0, False)
                expert(i, 1, False)
            expert(E // 2 - 1, 0, False)
            expert(E // 2 - 1, 1, True)
            for k in range(2):
                act.wait_ge(stored[k], 16 * (E // 2 + 1))

        @block.vector
        def _(dve):
            dve.wait_ge(bias_turned, 1)
            dve.tensor_copy(bias_t[:, :, :].rearrange("p c e -> p (c e)"), turn_bank[1][:, 0:DC * E]).then_inc(bias_ready, 1)
            dve.wait_ge(bias_ready, 1)
            with dve.Fori(0, E // 2) as i:
                for k in range(2):
                    e = 2 * i + k
                    dve.wait_ge(mid_done, e + 3)
                    for c in range(DC):
                        ins = dve.tensor_scalar(mid_t[k][:, c, :], mid_bank[k][:, CAP * c:CAP * (c + 1)],
                                                bias_t[:, c, bass.ds(e, 1)], 0.0, ALU.add, ALU.max)
                    ins.then_inc(mid_ready, 1)

        @block.tensor
        def _(pe):
            pe.wait_ge(bias_loaded, 16)
            for c in range(DC):
                ins = pe.transpose(turn_bank[1][:, E * c:E * (c + 1)], bias_in[:, P * c:P * (c + 1)], ident[0:E, 0:E])
            ins.then_inc(bias_turned, 1)
            pe.sem_inc(turned, 2)
            pe.sem_inc(mid_done, 2)
            pe.sem_inc(out_done, 2)
            pe.sem_inc(out_ready, 2)

            def turn(i, k):
                pe.wait_ge(rows_loaded[k], 16 * i + 16)
                for c in range(DC):
                    ins = pe.transpose(turn_bank[k][:, CAP * c:CAP * (c + 1)], rows[k][:, P * c:P * (c + 1)], ident[0:CAP, 0:CAP])
                ins.then_inc(turned, 1)

            def expert(i, k, last):
                e = 2 * i + k
                pe.wait_ge(rows_ready, e + 1)
                pe.wait_ge(up_loaded[k], 16 * i + 16)
                for h in range(DC):
                    for c in range(DC):
                        ins = pe.matmul(mid_bank[k][:, CAP * h:CAP * (h + 1)], up[k][:, c, P * h:P * (h + 1)],
                                        rows_t[k][:, c, :], start=(c == 0), stop=(c == DC - 1))
                ins.then_inc(mid_done, 1)
                if not last:
                    turn(i + (k == 1), 1 - k)
                pe.wait_ge(mid_ready, e + 1)
                pe.wait_ge(down_loaded[k], 16 * i + 16)
                pe.wait_ge(out_ready, e + 1)
                for h in range(DC):
                    ins = pe.matmul(out_bank[k][0:CAP, :], mid_t[k][:, h, :], down[k][:, h, :], start=(h == 0), stop=(h == DC - 1))
                ins.then_inc(out_done, 1)

            pe.wait_ge(bias_ready, 1)
            turn(0, 0)
            with pe.Fori(0, E // 2 - 1) as i:
                expert(i, 0, False)
                expert(i, 1, False)
            expert(E // 2 - 1, 0, False)
            expert(E // 2 - 1, 1, True)


def stage_combine(nc, slots_out, b2, x1, xn2, route, out):
    _, gather_at, weight, select_t, some, none = route
    with ExitStack() as ctx:
        b = Buffers(nc, ctx)
        got = [b.sb(f"o_got{k}", [TOK, NT, D]) for k in range(TOPK)]
        bias = b.sb("o_bias", [EXPERTS, D])
        bank = [b.ps(f"o_bank{i}", [P, 512]) for i in range(4)]
        bias_loaded = b.sem("o_bias_loaded")
        gathered = [b.sem(f"o_gathered{t}") for t in range(NT)]
        biased = b.sem("o_biased")
        first = b.sem("o_first")
        both = b.sem("o_both")
        kept = b.sem("o_kept")
        row_ready = b.sem("o_row_ready")
        stored = b.sem("o_stored")
        block = ctx.enter_context(nc.Block())

        @block.sync
        def _(sp):
            sp.dma_start(bias[:, :], b2).then_inc(bias_loaded, 16)
            for t in range(NT):
                sp.wait_ge(row_ready, t + 1)
                sp.dma_start(out[TOK * t:TOK * (t + 1), :], x1[:, t, :]).then_inc(stored, 16)
            sp.wait_ge(stored, 16 * NT)

        @block.gpsimd
        def _(pool):
            for t in range(NT):
                for k in range(TOPK):
                    pool.indirect_dma_start(
                        out=got[k][:, t, :], out_offset=None, in_=slots_out[:, :],
                        in_offset=bass.IndirectOffsetOnAxis(ap=gather_at[:, k * NT + t:k * NT + t + 1], axis=0)
                    ).then_inc(gathered[t], 16)

        @block.tensor
        def _(pe):
            pe.wait_ge(bias_loaded, 16)
            for t in range(NT):
                if t >= 4:
                    pe.wait_ge(first, t - 3)
                pe.matmul(bank[t % 4][0:TOK, :], select_t[:, TOK * t:TOK * (t + 1)], bias[:, :], start=True,
                          stop=True).then_inc(biased, 1)

        @block.vector
        def _(dve):
            for t in range(NT):
                dve.scalar_tensor_tensor(x1[:, t, :], xn2[:, t, :], none[:, t:t + 1], x1[:, t, :], ALU.mult,
                                         ALU.add).then_inc(kept, 1)
            for t in range(NT):
                dve.wait_ge(gathered[t], 32)
                dve.wait_ge(biased, t + 1)
                dve.scalar_tensor_tensor(got[0][:, t, :], got[0][:, t, :], weight[:, 0, t:t + 1], bank[t % 4][0:TOK, :],
                                         ALU.mult, ALU.add).then_inc(first, 1)
                dve.wait_ge(first, t + 1)
                dve.scalar_tensor_tensor(got[1][:, t, :], got[1][:, t, :], weight[:, 1, t:t + 1], got[0][:, t, :],
                                         ALU.mult, ALU.add).then_inc(both, 1)
                dve.wait_ge(both, t + 1)
                dve.wait_ge(kept, t + 1)
                dve.scalar_tensor_tensor(x1[:, t, :], got[1][:, t, :], some[:, t:t + 1], x1[:, t, :], ALU.mult,
                                         ALU.add).then_inc(row_ready, 1)


def gps_layer(nc, x, src, dst, gnn, mix, ffn, out):
    counts = nc.dram_tensor("counts_dram", (N, NS), U16, kind="Internal").ap()
    query_dram, value_dram = (nc.dram_tensor(f"{k}_fold_dram", (HEADS * DC, P, D), F32, kind="Internal").ap()
                              for k in ("query", "value"))
    hidden = nc.dram_tensor("hidden_dram", (N, D), F32, kind="Internal").ap()
    mixed = nc.dram_tensor("mixed_dram", (N, D), F32, kind="Internal").ap()
    slots_in = nc.dram_tensor("slots_in_dram", (SLOTS + TOPK * N, D), F32, kind="Internal").ap()
    slots_out = nc.dram_tensor("slots_out_dram", (SLOTS, D), F32, kind="Internal").ap()
    Buffers.used.clear()
    with ExitStack() as ctx:
        b = Buffers(nc, ctx)
        ident = b.sb("ident", [P, P])
        with ExitStack() as nodes:
            b_nodes = Buffers(nc, nodes)
            xnT = [b_nodes.sb(f"xnT_{k}", [P, DC, NS], F32R) for k in ("hi", "lo")]
            with ExitStack() as rows:
                xrow = Buffers(nc, rows).sb("xrow", [TOK, NT, D])
                stage_norm(nc, x, ident, xnT[0], xnT[1], xrow)
                stage_mix(nc, xrow, ident, mix["w_qkv"], mix["w_out"], mix["norm_gamma"], mixed)
            stage_count(nc, src, dst, ident, counts)
            Buffers.reset(nc)
            fold_bias = b_nodes.sb("fold_bias", [P, HEADS, DC])
            row_shift = b_nodes.sb("row_shift", [TOK, NT, HEADS])
            value_bias = b_nodes.sb("value_bias", [TOK, HEADS, D])
            stage_fold(nc, gnn, ident, xnT, query_dram, value_dram, fold_bias, row_shift, value_bias, hidden)
            stage_attend(nc, xnT, counts, query_dram, value_dram, fold_bias, row_shift, value_bias, ident, hidden)
        x1 = b.sb("x1", [TOK, NT, D])
        xn2 = b.sb("xn2", [TOK, NT, D])
        route = (b.sb("scatter_at", [TOK, TOPK * NT], U32), b.sb("gather_at", [TOK, TOPK * NT], U32),
                 b.sb("weight", [TOK, TOPK, NT]), b.sb("select_t", [EXPERTS, N]),
                 b.sb("some", [TOK, NT]), b.sb("none", [TOK, NT]))
        stage_join(nc, x, hidden, mixed, gnn["gamma"], gnn["beta"], mix["out_gamma"], ffn["Wg"], ident, x1, xn2,
                   route, slots_in)
        stage_experts(nc, slots_in, slots_out, ffn["W1"], ffn["b1"], ffn["W2"], ident)
        stage_combine(nc, slots_out, ffn["b2"], x1, xn2, route, out)


def kernel(**inputs):
    import concourse.bacc as bacc
    from concourse.bass_utils import run_bass_kernel_spmd

    nc = bacc.Bacc("TRN2", target_bir_lowering=False, num_devices=1)
    arrays, aps = {}, {}
    for name, a in inputs.items():
        arrays[f"in_{name}"] = np.ascontiguousarray(a)
        aps[name] = nc.dram_tensor(f"in_{name}", a.shape, mybir.dt.from_np(a.dtype), kind="ExternalInput").ap()
    out = nc.dram_tensor("out", (N, D), F32, kind="ExternalOutput").ap()

    def part(prefix):
        return {name[len(prefix):]: ap for name, ap in aps.items() if name.startswith(prefix)}

    gps_layer(nc, aps["x"], aps["src"], aps["dst"], part("L0_gnn_"), part("L0_mix_"), part("L0_ffn_"), out)
    result = run_bass_kernel_spmd(nc, [arrays], core_ids=[0])
    return result.results[0]["out"]
```

```python
from contextlib import ExitStack

import numpy as np

import concourse.bass as bass
from concourse import mybir

F32 = mybir.dt.float32
F32R = mybir.dt.float32r
F16 = mybir.dt.float16
BF16 = mybir.dt.bfloat16
I32 = mybir.dt.int32
U32 = mybir.dt.uint32
U16 = mybir.dt.uint16
ALU = mybir.AluOpType
ACT = mybir.ActivationFunctionType
AX = mybir.AxisListType

P = 128
N = 1250
TOK = 125
NT = N // TOK
D = 512
DC = D // P
HEADS = 4
BW = 418
NB = 3
NS = BW * NB
GRP = 2 * TOK
NG = N // GRP
EDGES = 41250
EB = 375
NEB = EDGES // EB
SUB = EB // TOK
EPS = 1e-5
FAR = 1.0e30
MIX_HEADS, MIX_DIM = 8, 64
EXPERTS = 32
CAP = 98
SLOTS = EXPERTS * CAP
TOPK = 2


class Buffers:

    used = []

    def __init__(self, nc, ctx):
        self.nc, self.ctx = nc, ctx

    def sb(self, name, shape, dt=F32):
        return self.ctx.enter_context(self.nc.sbuf_tensor(name, shape, dt))

    def ps(self, name, shape, dt=F32):
        return self.ctx.enter_context(self.nc.psum_tensor(name, shape, dt))

    def sem(self, name):
        self.used.append(self.nc.alloc_semaphore(name))
        return self.used[-1]

    @classmethod
    def reset(cls, nc):
        nc.clear_and_free_semaphores(list(cls.used))
        cls.used.clear()
        nc.all_engine_barrier()


def chain(engine, sem):
    done = [0]

    def link(ins):
        done[0] += 1
        ins.then_inc(sem, 1)
        engine.wait_ge(sem, done[0])

    return link


class Steps:

    def __init__(self, engine, sem, base, total):
        self.engine, self.sem, self.base, self.total, self.n = engine, sem, base, total, 0

    def __call__(self, ins):
        self.n += 1
        ins.then_inc(self.sem, 1)
        self.engine.wait_ge(self.sem, self.base + self.n)


def tile_parts(g):
    return range(4 * g, min(4 * g + 4, NT))


def node_stats(dve, link, source, stats, mean_var, root_in, loaded=None):
    for t in range(NT):
        if loaded and t % 2 == 0:
            dve.wait_ge(loaded[t // 2], 16)
        ins = dve.bn_stats(stats[:, t, :], source[:, t, :])
    link(ins)
    for t in range(NT):
        ins = dve.bn_aggr(mean_var[:, t, :], stats[:, t, :])
    link(ins)
    return dve.tensor_scalar(root_in[:, :], mean_var[:, :, 1], EPS, None, ALU.add)


def inverse_root(dve, link, root_in, root, scratch, rstd):
    link(dve.reciprocal(rstd, root))
    link(dve.tensor_tensor(scratch, rstd, rstd, ALU.mult))
    link(dve.tensor_tensor(scratch, scratch, root_in, ALU.mult))
    link(dve.tensor_scalar(scratch, scratch, -0.5, 1.5, ALU.mult, ALU.add))
    link(dve.tensor_tensor(rstd, rstd, scratch, ALU.mult))


def stage_norm(nc, x, ident, xnT_hi, xnT_lo, xrow):
    with ExitStack() as ctx:
        b = Buffers(nc, ctx)
        stats = b.sb("n_stats", [TOK, NT, 6])
        mean_var = b.sb("n_mean_var", [TOK, NT, 2])
        root_in = b.sb("n_root_in", [TOK, NT])
        root = b.sb("n_root", [TOK, NT])
        scratch = b.sb("n_scratch", [TOK, NT])
        rstd = b.sb("n_rstd", [TOK, NT])
        bank = [b.ps(f"n_bank{i}", [P, 512]) for i in range(4)]
        x_loaded = [b.sem(f"n_x_loaded{g}") for g in range(NG)]
        dve_step = b.sem("n_dve_step")
        ident_ready = b.sem("n_ident_ready")
        var_ready = b.sem("n_var_ready")
        root_ready = b.sem("n_root_ready")
        row_ready = b.sem("n_row_ready")
        turned = b.sem("n_turned")
        hi_ready = b.sem("n_hi_ready")
        lo_ready = b.sem("n_lo_ready")
        block = ctx.enter_context(nc.Block())
        units = [(g, c) for g in range(3) for c in range(DC)]

        @block.sync
        def _(sp):
            view = x.rearrange("(t p) c -> p t c", p=TOK)
            for g in range(NG):
                sp.dma_start(xrow[:, 2 * g:2 * g + 2, :], view[:, 2 * g:2 * g + 2, :]).then_inc(x_loaded[g], 16)

        @block.gpsimd
        def _(pool):
            pool.memset(ident[:, :], 0.0).then_inc(ident_ready, 1)
            pool.wait_ge(ident_ready, 1)
            pool.affine_select(out=ident[:, :], in_=ident[:, :], compare_op=ALU.not_equal, fill=1.0,
                               base=0, pattern=[[-1, P]], channel_multiplier=1).then_inc(ident_ready, 1)
            pool.memset(xnT_hi[:, :, N:NS].bitcast(F32), 0.0)
            pool.memset(xnT_lo[:, :, N:NS].bitcast(F32), 0.0)

        @block.vector
        def _(dve):
            link = chain(dve, dve_step)
            node_stats(dve, link, xrow, stats, mean_var, root_in, x_loaded).then_inc(var_ready, 1)
            dve.wait_ge(root_ready, 1)
            inverse_root(dve, link, root_in[:, :], root[:, :], scratch[:, :], rstd[:, :])
            for t in range(NT):
                dve.tensor_scalar(xrow[:, t, :], xrow[:, t, :], mean_var[:, t, 0:1], rstd[:, t:t + 1],
                                  ALU.subtract, ALU.mult).then_inc(row_ready, 1)
            for u, (g, c) in enumerate(units):
                n = TOK * len(tile_parts(g))
                cols = slice(500 * g, 500 * g + n)
                dve.wait_ge(hi_ready, u + 1)
                dve.tensor_tensor(xnT_lo[:, c, cols], bank[u % 4][:, 0:n], xnT_hi[:, c, cols].bitcast(F32),
                                  ALU.subtract).then_inc(lo_ready, 1)

        @block.scalar
        def _(act):
            act.wait_ge(var_ready, 1)
            act.activation(root[:, :], root_in[:, :], ACT.Sqrt).then_inc(root_ready, 1)
            for u, (g, c) in enumerate(units):
                n = TOK * len(tile_parts(g))
                act.wait_ge(turned, u + 1)
                act.activation(xnT_hi[:, c, 500 * g:500 * g + n], bank[u % 4][:, 0:n],
                               ACT.Copy).then_inc(hi_ready, 1)

        @block.tensor
        def _(pe):
            pe.wait_ge(ident_ready, 2)
            for u, (g, c) in enumerate(units):
                if u >= 4:
                    pe.wait_ge(lo_ready, u - 3)
                pe.wait_ge(row_ready, tile_parts(g)[-1] + 1)
                for i, t in enumerate(tile_parts(g)):
                    ins = pe.transpose(bank[u % 4][:, TOK * i:TOK * (i + 1)], xrow[:, t, P * c:P * (c + 1)],
                                       ident[0:TOK, 0:TOK])
                ins.then_inc(turned, 1)


def stage_count(nc, src, dst, ident, counts, fold_inputs, x, mixed, mixed_norm, out_gamma, beta, base, slots_in):
    with ExitStack() as ctx:
        b = Buffers(nc, ctx)
        edge_in = b.sb("c_edge_in", [NEB, 2, EB], I32)
        edge_row = b.sb("c_edge_row", [NEB, 2, EB])
        edge_col = b.sb("c_edge_col", [TOK, 2, SUB, NEB])
        reach = b.sb("c_reach", [NEB, 2])
        block_no = b.sb("c_block_no", [NT, NEB])
        tile_lo = b.sb("c_tile_lo", [NT, 2])
        over = b.sb("c_over", [NT, 2, NEB])
        at = b.sb("c_at", [NT, 2, NEB])
        span = b.sb("c_span", [NT, 2])
        span_int = b.sb("c_span_int", [NT, 2], I32)
        span_row = b.sb("c_span_row", [1, 2 * NT], I32)
        node_no = b.sb("c_node_no", [TOK, NS], F16)
        src_hot = b.sb("c_src_hot", [TOK, SUB, NS], BF16)
        dst_hot = b.sb("c_dst_hot", [TOK, SUB, TOK], BF16)
        zeros = b.sb("c_zeros", [TOK, 512], BF16)
        count_out = b.sb("c_count_out", [TOK, NS], U16)
        base_row = b.sb("c_base_row", [TOK, NT, D])
        x_row = b.sb("c_x_row", [TOK, NT, D])
        vec = [b.sb(f"c_vec{i}", [TOK, D]) for i in range(2)]
        zero_rows = b.sb("c_zero_rows", [CAP, D])
        turn_bank = [b.ps(f"c_turn{i}", [P, 512]) for i in range(2)]
        reach_bank = b.ps("c_reach_bank", [P, 512])
        acc = b.ps("c_acc", [P, NB, 512])
        edges_loaded = b.sem("c_edges_loaded")
        iota_ready = b.sem("c_iota_ready")
        dve_step = b.sem("c_dve_step")
        rows_ready = b.sem("c_rows_ready")
        turned = b.sem("c_turned")
        cols_ready = b.sem("c_cols_ready")
        reach_spread = b.sem("c_reach_spread")
        span_ready = b.sem("c_span_ready")
        span_loaded = b.sem("c_span_loaded")
        hot_ready = b.sem("c_hot_ready")
        hot_used = b.sem("c_hot_used")
        tile_counted = b.sem("c_tile_counted")
        tile_copied = b.sem("c_tile_copied")
        tile_stored = b.sem("c_tile_stored")
        mixed_loaded = b.sem("c_mixed_loaded")
        terms_loaded = b.sem("c_terms_loaded")
        normed = b.sem("c_normed")
        pool_step = b.sem("c_pool_step")
        base_ready = b.sem("c_base_ready")
        base_stored = b.sem("c_base_stored")
        cleared = b.sem("c_cleared")
        block = ctx.enter_context(nc.Block())

        @block.sync
        def _(sp):
            sp.dma_start(edge_in[:, 0, :], src.rearrange("(r e) -> r e", e=EB)).then_inc(edges_loaded, 16)
            sp.dma_start(edge_in[:, 1, :], dst.rearrange("(r e) -> r e", e=EB)).then_inc(edges_loaded, 16)
            sp.wait_ge(span_ready, 1)
            sp.dma_start(span_row[0:1, :].rearrange("o (t k) -> o t k", k=2), span_int[:, :]).then_inc(span_loaded, 16)
            sp.dma_start(base_row[:, :, :], mixed.rearrange("(t p) c -> p t c", p=TOK)).then_inc(mixed_loaded, 16)
            sp.dma_start(x_row[:, :, :], x.rearrange("(t p) c -> p t c", p=TOK)).then_inc(terms_loaded, 16)
            for i, v in enumerate((out_gamma, beta)):
                sp.dma_start(vec[i][:, :], v.unsqueeze(0).to_broadcast([TOK, D])).then_inc(terms_loaded, 16)
            fold_inputs.load_first(sp)
            sp.wait_ge(pool_step, 1)
            sp.dma_start(slots_in[0:SLOTS, :].rearrange("(e p) c -> p e c", p=CAP),
                         zero_rows[:, :].unsqueeze(1).to_broadcast([CAP, EXPERTS, D])).then_inc(cleared, 16)

            def store_counts(tiles):
                with sp.Fori(tiles[0], tiles[-1] + 1) as t:
                    sp.wait_ge(tile_copied, t + 2)
                    sp.dma_start(counts[bass.ds(t * TOK, TOK), :], count_out[:, :]).then_inc(tile_stored, 16)

            store_counts(range(NT // 2))
            sp.wait_ge(base_ready, 1)
            sp.dma_start(base.rearrange("(t p) c -> p t c", p=TOK), base_row[:, :, :]).then_inc(base_stored, 16)
            store_counts(range(NT // 2, NT))
            sp.wait_ge(tile_stored, 16 * (NT + 1))
            sp.wait_ge(base_stored, 16)
            sp.wait_ge(cleared, 16)

        @block.gpsimd
        def _(pool):
            pool.iota(node_no[:, :], [[1, NS]], base=0, channel_multiplier=0,
                      allow_small_or_imprecise_dtypes=True).then_inc(iota_ready, 1)
            pool.iota(block_no[:, :], [[1, NEB]], base=0, channel_multiplier=0,
                      allow_small_or_imprecise_dtypes=True).then_inc(iota_ready, 1)
            pool.iota(tile_lo[:, :], [[TOK - 1, 2]], base=0, channel_multiplier=TOK,
                      allow_small_or_imprecise_dtypes=True).then_inc(iota_ready, 1)
            pool.memset(zeros[:, :], 0.0).then_inc(iota_ready, 1)
            pool.memset(zero_rows[:, :], 0.0).then_inc(pool_step, 1)
            pool.wait_ge(terms_loaded, 48)
            for t in range(NT):
                pool.wait_ge(normed, t + 1)
                for i, (other, op) in enumerate(((vec[0][:, :], ALU.mult), (vec[1][:, :], ALU.add), (x_row[:, t, :], ALU.add))):
                    pool.tensor_tensor(base_row[:, t, :], base_row[:, t, :], other, op).then_inc(pool_step, 1)
                    pool.wait_ge(pool_step, 3 * t + i + 2)
            pool.sem_inc(base_ready, 1)

        @block.vector
        def _(dve):
            link = chain(dve, dve_step)
            dve.wait_ge(edges_loaded, 32)
            link(dve.tensor_copy(edge_row[:, :, :], edge_in[:, :, :]))
            dve.tensor_reduce(reach[:, 0:1], edge_row[:, 1, :], AX.X, ALU.min)
            link(dve.tensor_reduce(reach[:, 1:2], edge_row[:, 1, :], AX.X, ALU.max))
            dve.sem_inc(rows_ready, 1)
            for w in range(2):
                dve.wait_ge(turned, w + 1)
                dve.tensor_copy(edge_col[:, w, :, :], turn_bank[w][0:TOK, 0:SUB * NEB].rearrange(
                    "p (k r) -> p k r", k=SUB)).then_inc(cols_ready, 1)
            dve.wait_ge(reach_spread, 1)
            dve.wait_ge(iota_ready, 4)
            dve.tensor_scalar(over[:, 0, :], reach_bank[0:NT, 0:NEB], tile_lo[:, 1:2], None, ALU.is_le)
            link(dve.tensor_scalar(over[:, 1, :], reach_bank[0:NT, NEB:2 * NEB], tile_lo[:, 0:1], None, ALU.is_ge))
            link(dve.tensor_tensor(over[:, 0, :], over[:, 0, :], over[:, 1, :], ALU.mult))
            dve.scalar_tensor_tensor(at[:, 0, :], block_no[:, :], -float(NEB - 1), over[:, 0, :], ALU.add, ALU.mult)
            link(dve.scalar_tensor_tensor(at[:, 1, :], block_no[:, :], 1.0, over[:, 0, :], ALU.add, ALU.mult))
            dve.tensor_reduce(span[:, 0:1], at[:, 0, :], AX.X, ALU.min)
            link(dve.tensor_reduce(span[:, 1:2], at[:, 1, :], AX.X, ALU.max))
            link(dve.tensor_scalar(span[:, 0:1], span[:, 0:1], float(NEB - 1), None, ALU.add))
            link(dve.scalar_tensor_tensor(span[:, 1:2], span[:, 0:1], 1.0, span[:, 1:2], ALU.add, ALU.max))
            dve.tensor_copy(span_int[:, :], span[:, :]).then_inc(span_ready, 1)
            dve.wait_ge(cols_ready, 2)
            dve.wait_ge(span_loaded, 16)
            serial = dve.alloc_register("c_dve_serial")
            dve.reg_mov(serial, 1)
            dve.sem_inc(hot_used, SUB)
            dve.sem_inc(hot_ready, 1)
            with dve.Fori(0, NT) as t:
                first = dve.value_load(span_row[0:1, bass.ds(2 * t, 1)], min_val=0, max_val=NEB - 1)
                stop = dve.value_load(span_row[0:1, bass.ds(2 * t + 1, 1)], min_val=1, max_val=NEB)
                with dve.Fori(first, stop) as r:
                    for k in range(SUB):
                        dve.wait_ge(hot_used, serial)
                        dve.tensor_scalar(src_hot[:, k, :], node_no[:, :], edge_col[:, 0, k, bass.ds(r, 1)],
                                          None, ALU.is_equal)
                        dve.tensor_scalar(dst_hot[:, k, :], node_no[:, 0:TOK], edge_col[:, 1, k, bass.ds(r, 1)],
                                          None, ALU.is_equal).then_inc(hot_ready, 1)
                        dve.reg_add(serial, serial, 1)
                dve.wait_ge(hot_ready, serial)
                dve.tensor_scalar(edge_col[:, 1, :, :], edge_col[:, 1, :, :], -float(TOK), None,
                                  ALU.add).then_inc(cols_ready, 1)
                dve.wait_ge(cols_ready, t + 3)

        @block.scalar
        def _(act):
            act.wait_ge(mixed_loaded, 16)
            for t in range(NT):
                act.activation(base_row[:, t, :], base_row[:, t, :], ACT.Identity, bias=mixed_norm[:, 1, t:t + 1],
                               scale=mixed_norm[:, 0, t:t + 1]).then_inc(normed, 1)
            act.sem_inc(tile_copied, 1)
            with act.Fori(0, NT) as t:
                act.wait_ge(tile_counted, t + 1)
                act.wait_ge(tile_stored, 16 * t + 16)
                act.activation(count_out[:, :].rearrange("p (b n) -> p b n", b=NB), acc[0:TOK, :, 0:BW],
                               ACT.Copy).then_inc(tile_copied, 1)

        @block.tensor
        def _(pe):
            pe.wait_ge(rows_ready, 1)
            for w in range(2):
                for k in range(SUB):
                    ins = pe.transpose(turn_bank[w][0:TOK, NEB * k:NEB * (k + 1)],
                                       edge_row[:, w, TOK * k:TOK * (k + 1)], ident[0:NEB, 0:NEB])
                ins.then_inc(turned, 1)
            for w in range(2):
                ins = pe.matmul(reach_bank[0:NT, NEB * w:NEB * (w + 1)],
                                reach[:, w:w + 1].to_broadcast([NEB, NT]), ident[0:NEB, 0:NEB],
                                start=True, stop=True)
            ins.then_inc(reach_spread, 1)
            pe.wait_ge(span_loaded, 16)
            pe.sem_inc(tile_stored, 16)
            serial = pe.alloc_register("c_pe_serial")
            pe.reg_mov(serial, 2)
            with pe.Fori(0, NT) as t:
                first = pe.value_load(span_row[0:1, bass.ds(2 * t, 1)], min_val=0, max_val=NEB - 1)
                stop = pe.value_load(span_row[0:1, bass.ds(2 * t + 1, 1)], min_val=1, max_val=NEB)
                pe.wait_ge(tile_copied, t + 1)
                for n in range(NB):
                    pe.matmul(acc[0:TOK, n, 0:BW], zeros[:, 0:TOK], zeros[:, 0:BW], start=True, stop=False)
                with pe.Fori(first, stop) as r:
                    for k in range(SUB):
                        pe.wait_ge(hot_ready, serial)
                        for n in range(NB):
                            ins = pe.matmul(acc[0:TOK, n, 0:BW], dst_hot[:, k, :], src_hot[:, k, BW * n:BW * (n + 1)],
                                            start=False, stop=False)
                        ins.then_inc(hot_used, 1)
                        pe.reg_add(serial, serial, 1)
                for n in range(NB):
                    ins = pe.matmul(acc[0:TOK, n, 0:BW], zeros[:, 0:TOK], zeros[:, 0:BW], start=False, stop=True)
                ins.then_inc(tile_counted, 1)


PARTS = ((0, 0), (0, 1), (1, 0))


class FoldedWeights:

    def __init__(self, nc, b):
        self.dram = [nc.dram_tensor(f"{k}_fold_dram", (HEADS * DC, P, D), F32, kind="Internal").ap()
                     for k in ("query", "value")]
        self.raw = [b.sb(f"{k}_fold", [P, DC, D]) for k in ("query", "value")]
        self.loaded = [b.sem(f"{k}_fold_loaded") for k in ("query", "value")]

    def load(self, sp, i, h):
        sp.dma_start(self.raw[i][:, :, :], self.dram[i][bass.ds(h * DC, DC), :, :].rearrange("c p n -> p c n")
                     ).then_inc(self.loaded[i], 16)


class FoldInputs:
    NAMES = ("Wq", "Wk", "Wv", "Wskip")

    def __init__(self, b, gnn, folded):
        self.gnn = gnn
        self.raw = [b.sb("f_query_raw", [P, DC, D]), b.sb("f_key_raw", [P, DC, D]), folded.raw[0], folded.raw[1]]
        self.lin_raw = b.sb("f_lin_raw", [P, DC, D])
        self.bias_row = b.sb("f_bias_row", [P, 2, D])
        self.bias_in = b.sb("f_bias_in", [2 * HEADS * DC, P])
        self.lin_bias = b.sb("f_lin_bias", [TOK, D])
        self.bias_loaded = b.sem("f_bias_loaded")
        self.lin_bias_loaded = b.sem("f_lin_bias_loaded")
        self.raw_loaded = [b.sem(f"f_raw_loaded{w}") for w in range(4)]
        self.lin_loaded = b.sem("f_lin_loaded")
        self.bias_row_loaded = b.sem("f_bias_row_loaded")

    def load(self, sp, w, h):
        dram = self.gnn[self.NAMES[w]].rearrange("(c p) n -> p c n", p=P)
        sp.dma_start(self.raw[w][:, :, :], dram[:, :, bass.ds(h * D, D)]).then_inc(self.raw_loaded[w], 16)

    def load_lin(self, sp, h):
        dram = self.gnn["Wlin"].rearrange("(c p) n -> p c n", p=P)
        sp.dma_start(self.lin_raw[:, :, :], dram[:, bass.ds(h * DC, DC), :]).then_inc(self.lin_loaded, 16)

    def load_bias_row(self, sp, h):
        for i, name in enumerate(("bq", "bk")):
            sp.dma_start(self.bias_row[:, i, :], self.gnn[name].unsqueeze(0)[:, bass.ds(h * D, D)].to_broadcast([P, D])
                         ).then_inc(self.bias_row_loaded, 16)

    def load_first(self, sp):
        for i, name in enumerate(("bv", "bskip")):
            rows = self.gnn[name].rearrange("(r p) -> r p", p=P)
            sp.dma_start(self.bias_in[HEADS * DC * i:HEADS * DC * (i + 1), :], rows).then_inc(self.bias_loaded, 16)
        sp.dma_start(self.lin_bias[:, :], self.gnn["blin"].unsqueeze(0).to_broadcast([TOK, D])
                     ).then_inc(self.lin_bias_loaded, 16)
        for w in range(4):
            self.load(sp, w, 0)
        self.load_lin(sp, 0)
        self.load_bias_row(sp, 0)


def stage_fold(nc, inputs, folded, ident, xnT, fold_bias, row_shift, value_bias, hidden):
    HC = HEADS * DC
    with ExitStack() as ctx:
        b = Buffers(nc, ctx)
        raw, lin_raw, bias_row = inputs.raw, inputs.lin_raw, inputs.bias_row
        bias_in, lin_bias = inputs.bias_in, inputs.lin_bias
        turn = [[b.sb(f"f_turn{w}_{k}", [P, DC, D], F32R) for k in ("hi", "lo")] for w in range(4)]
        lin = [b.sb(f"f_lin_{k}", [P, DC, D], F32R) for k in ("hi", "lo")]
        made_out = [b.sb(f"f_made_out{i}", [P, DC, D]) for i in range(2)]
        skip_sum = b.sb("f_skip_sum", [P, DC, D])
        head0 = b.sb("f_head0", [P, P])
        bias_col = b.sb("f_bias_col", [P, 2, HC])
        bias_pair = b.sb("f_bias_pair", [P, 2, 2, HC], F32R)
        bias_now = b.sb("f_bias_now", [P, 2, 2, DC], F32R)
        product_row = b.sb("f_product_row", [P, D])
        bias_dots = b.sb("f_bias_dots", [P, HEADS])
        shift_col = b.sb("f_shift_col", [P, DC, HEADS])
        shift_pair = b.sb("f_shift_pair", [P, DC, 2, HEADS], F32R)
        shift_row = b.sb("f_shift_row", [2 * HEADS, NB, BW])
        hidden_row = [raw[i][0:TOK, 0, :] for i in range(2)]
        shift_sum = b.sb("f_shift_sum", [TOK, NT, HEADS])
        turn_bank = [b.ps(f"f_turn_bank{i}", [P, 512]) for i in range(2)]
        bank = [b.ps(f"f_bank{i}", [P, 512]) for i in range(2)]
        bias_bank = b.ps("f_bias_bank", [P, 512])
        shift_bank = b.ps("f_shift", [P, 512])
        row_bank = [b.ps(f"f_row_bank{i}", [P, 512]) for i in range(2)]
        bias_loaded, lin_bias_loaded = inputs.bias_loaded, inputs.lin_bias_loaded
        raw_loaded, lin_loaded, bias_row_loaded = inputs.raw_loaded, inputs.lin_loaded, inputs.bias_row_loaded
        bias_turned = b.sem("f_bias_turned")
        pair_ready = b.sem("f_pair_ready")
        dve_step = b.sem("f_dve_step")
        dot_step = b.sem("f_dot_step")
        lin_raw_ready = b.sem("f_lin_raw_ready")
        lin_hi = b.sem("f_lin_hi")
        lin_ready = b.sem("f_lin_ready")
        turned = b.sem("f_turned")
        turn_hi = b.sem("f_turn_hi")
        turn_ready = b.sem("f_turn_ready")
        made = b.sem("f_made")
        moved = b.sem("f_moved")
        summed = b.sem("f_summed")
        stored = [b.sem(f"f_stored{i}") for i in range(2)]
        dots_done = b.sem("f_dots_done")
        now_ready = b.sem("f_now_ready")
        head_rows = b.sem("f_head_rows")
        head_rows_read = b.sem("f_head_rows_read")
        shift_pair_ready = b.sem("f_shift_pair_ready")
        shift_rows = b.sem("f_shift_rows")
        shift_row_ready = b.sem("f_shift_row_ready")
        skip_hi = b.sem("f_skip_hi")
        skip_ready = b.sem("f_skip_ready")
        rows_done = b.sem("f_rows_done")
        row_read = b.sem("f_row_read")
        shift_done = b.sem("f_shift_done")
        row_stored = [b.sem(f"f_row_stored{i}") for i in range(2)]
        block = ctx.enter_context(nc.Block())


        def unit(w0, u):
            return turn[w0 + u // DC], u % DC

        def heads(engine, head):
            with engine.Fori(0, HEADS - 1) as h:
                head(h, False)
            head(HEADS - 1, True)

        @block.sync
        def _(sp):
            with sp.Fori(0, HEADS - 1) as h:
                sp.wait_ge(dots_done, h + 1)
                inputs.load(sp, 0, h + 1)
                inputs.load(sp, 1, h + 1)
                inputs.load_bias_row(sp, h + 1)
                sp.wait_ge(lin_ready, h + 1)
                inputs.load_lin(sp, h + 1)
                sp.wait_ge(turned, 16 * h + 16)
                inputs.load(sp, 2, h + 1)
                inputs.load(sp, 3, h + 1)
            sp.wait_ge(turned, 16 * HEADS)
            for i in range(2):
                sp.wait_ge(stored[i], 32)
                folded.load(sp, i, 0)
            for t in range(NT):
                sp.wait_ge(row_read, t + 1)
                sp.dma_start(hidden[TOK * t:TOK * (t + 1), :], hidden_row[t % 2]).then_inc(row_stored[t % 2], 16)
            for i in range(2):
                sp.wait_ge(row_stored[i], 16 * NT // 2)

        @block.scalar
        def _(act):
            def turn_part(w0, u, first_unit):
                part, j = unit(w0, u)
                act.wait_ge(turned, first_unit + (u + 1))
                act.activation(part[0][:, j, :], turn_bank[u % 2][:, :], ACT.Copy).then_inc(turn_hi, 1)

            def product(h, k):
                i, c = divmod(k, DC)
                if c == 0:
                    act.wait_ge(stored[i], 16 * h + 16)
                act.wait_ge(made, 12 * h + (k + 2))
                act.activation(made_out[i][:, c, :], bank[k % 2][:, :], ACT.Copy).then_inc(moved, 1)
                if c == DC - 1:
                    act.wait_ge(moved, 8 * h + (k + 1))
                    act.dma_start(folded.dram[i][bass.ds(h * DC, DC), :, :].rearrange("c p n -> p c n"),
                                  made_out[i][:, :, :]).then_inc(stored[i], 16)

            def head(h, last):
                for c in range(DC):
                    turn_part(2, 2 * c, 16 * h + 8)
                    turn_part(2, 2 * c + 1, 16 * h + 8)
                    if c == 0:
                        act.wait_ge(lin_raw_ready, h + 2)
                        act.wait_ge(made, 12 * h + 1)
                    act.activation(lin[0][:, c, :], lin_raw[:, c, :], ACT.Copy).then_inc(lin_hi, 1)
                    product(h, c)
                for c in range(DC):
                    if not last:
                        turn_part(0, c, 16 * h + 16)
                    product(h, DC + c)
                for c in range(DC):
                    if last:
                        act.wait_ge(summed, 4 * h + c + 5)
                        act.activation(turn[0][0][:, c, :], skip_sum[:, c, :], ACT.Copy).then_inc(skip_hi, 1)
                    else:
                        turn_part(0, DC + c, 16 * h + 16)

            for i in range(2):
                act.sem_inc(stored[i], 16)
            for u in range(8):
                turn_part(0, u, 0)
            heads(act, head)
            for m, shift_rows_bank in enumerate((*row_bank, bias_bank)):
                act.wait_ge(shift_rows, m + 1)
                act.activation(shift_row[:, m, :], shift_rows_bank[0:2 * HEADS, 0:BW], ACT.Copy).then_inc(shift_row_ready, 1)
            for i in range(2):
                act.wait_ge(stored[i], 16 * (HEADS + 1))

        @block.vector
        def _(dve):
            link = chain(dve, dve_step)
            dve.tensor_copy(head0[:, :], ident[:, :]).then_inc(lin_raw_ready, 1)
            dve.memset(skip_sum[:, :, :], 0.0).then_inc(summed, 4)
            dve.wait_ge(lin_raw_ready, 1)
            dve.wait_ge(summed, 4)
            dve.wait_ge(bias_turned, 1)
            link(dve.tensor_copy(bias_col[:, :, :], bias_bank[:, 0:2 * HC].rearrange("p (i k) -> p i k", i=2)))
            link(dve.tensor_copy(bias_pair[:, :, 0, :], bias_col[:, :, :]))
            dve.tensor_tensor(bias_pair[:, :, 1, :], bias_col[:, :, :], bias_pair[:, :, 0, :].bitcast(F32),
                              ALU.subtract).then_inc(pair_ready, 1)
            dve.wait_ge(pair_ready, 1)
            dve.wait_ge(lin_bias_loaded, 16)
            dve.sem_inc(head_rows_read, 1)

            def bias_products(h, u):
                step = Steps(dve, dot_step, 9 * h + u, 1)

                def dot(a, b, out):
                    return dve.scalar_tensor_tensor(product_row[:, :], a, 1.0, b, ALU.mult, ALU.mult, accum_out=out)

                if u == 0:
                    dve.wait_ge(bias_row_loaded, 32 * h + 32)
                if u < DC:
                    dve.wait_ge(raw_loaded[0], 16 * h + 16)
                    step(dot(raw[0][:, u, :], bias_row[:, 1, :], shift_col[:, u, bass.ds(h, 1)]))
                else:
                    dve.wait_ge(raw_loaded[1], 16 * h + 16)
                    step(dot(raw[1][:, u - DC, :], bias_row[:, 0, :], fold_bias[:, bass.ds(h, 1), u - DC]))
                if u == 7:
                    step(dot(bias_row[:, 0, :], bias_row[:, 1, :], bias_dots[:, bass.ds(h, 1)]))
                    dve.sem_inc(dots_done, 1)

            def turn_part(w0, u, first_unit):
                part, j = unit(w0, u)
                dve.wait_ge(turn_hi, first_unit + (u + 1))
                dve.tensor_tensor(part[1][:, j, :], turn_bank[u % 2][:, :], part[0][:, j, :].bitcast(F32),
                                  ALU.subtract).then_inc(turn_ready, 1)

            def head_inputs(h):
                dve.wait_ge(head_rows_read, 2 * h + 1)
                dve.tensor_copy(bias_now[:, :, :, :], bias_pair[:, :, :, bass.ds(h * DC, DC)].bitcast(F32)
                                ).then_inc(now_ready, 1)
                dve.wait_ge(lin_loaded, 16 * h + 16)
                for c in range(DC):
                    ins = dve.tensor_tensor(lin_raw[:, c, P * c:P * (c + 1)], lin_raw[:, c, P * c:P * (c + 1)],
                                            head0[:, :], ALU.add)
                ins.then_inc(lin_raw_ready, 1)
                dve.wait_ge(lin_raw_ready, h + 2)
                dve.memset(head0[:, :], 0.0)

            def head(h, last):
                for c in range(DC):
                    turn_part(2, 2 * c, 16 * h + 8)
                    turn_part(2, 2 * c + 1, 16 * h + 8)
                    if c == 0:
                        head_inputs(h)
                    dve.wait_ge(lin_hi, 4 * h + (c + 1))
                    ins = dve.tensor_tensor(lin[1][:, c, :], lin_raw[:, c, :], lin[0][:, c, :].bitcast(F32), ALU.subtract)
                ins.then_inc(lin_ready, 1)
                dve.wait_ge(head_rows, 2 * h + 1)
                dve.tensor_copy(value_bias[:, bass.ds(h, 1), :].rearrange("p o n -> p (o n)"), row_bank[0][0:TOK, :]
                                ).then_inc(head_rows_read, 1)
                dve.wait_ge(head_rows, 2 * h + 2)
                dve.tensor_tensor(lin_bias[:, :], row_bank[1][0:TOK, :], lin_bias[:, :], ALU.add).then_inc(head_rows_read, 1)
                if not last:
                    for u in range(DC):
                        turn_part(0, u, 16 * h + 16)
                        bias_products(h + 1, u)
                for c in range(DC):
                    if not last:
                        turn_part(0, DC + c, 16 * h + 16)
                    dve.wait_ge(made, 12 * h + (8 + c + 2))
                    dve.wait_ge(summed, 4 * h + (c + 1))
                    dve.tensor_tensor(skip_sum[:, c, :], bank[c % 2][:, :], skip_sum[:, c, :], ALU.add).then_inc(summed, 1)
                    if not last:
                        bias_products(h + 1, DC + c)
                    elif c > 0:
                        skip_low(c - 1)
                if last:
                    skip_low(DC - 1)

            def skip_low(c):
                dve.wait_ge(skip_hi, c + 1)
                dve.tensor_tensor(turn[0][1][:, c, :], skip_sum[:, c, :], turn[0][0][:, c, :].bitcast(F32),
                                  ALU.subtract).then_inc(skip_ready, 1)

            for u in range(8):
                turn_part(0, u, 0)
                bias_products(0, u)
            heads(dve, head)
            link(dve.tensor_copy(shift_pair[:, :, 0, :], shift_col[:, :, :]))
            dve.tensor_tensor(shift_pair[:, :, 1, :], shift_col[:, :, :], shift_pair[:, :, 0, :].bitcast(F32),
                              ALU.subtract).then_inc(shift_pair_ready, 1)
            dve.wait_ge(head_rows_read, 2 * HEADS + 1)
            for t in range(NT):
                dve.wait_ge(rows_done, t + 1)
                if t >= 2:
                    dve.wait_ge(row_stored[t % 2], 16 * (t // 2))
                dve.tensor_tensor(hidden_row[t % 2], row_bank[t % 2][0:TOK, :], lin_bias[:, :], ALU.add).then_inc(row_read, 1)
            dve.wait_ge(shift_done, 1)
            link(dve.tensor_reduce(shift_sum[:, :, :], shift_bank[0:TOK, 0:2 * NT * HEADS].rearrange(
                "p (t k h) -> p t h k", t=NT, k=2), AX.X, ALU.add))
            link(dve.tensor_tensor(row_shift[:, :, :], shift_sum[:, :, :],
                                   bias_dots[0:TOK, :].unsqueeze(1).to_broadcast([TOK, NT, HEADS]), ALU.add))

        @block.tensor
        def _(pe):
            pe.wait_ge(bias_loaded, 32)
            pe.transpose(bias_bank[:, 0:2 * HC], bias_in[:, :], ident[0:2 * HC, 0:2 * HC]).then_inc(bias_turned, 1)

            def turn_part(w0, u, first_unit):
                w, j = w0 + u // DC, u % DC
                if not isinstance(first_unit, int) or first_unit + u >= 2:
                    pe.wait_ge(turn_ready, first_unit + (u - 1))
                for c in range(DC):
                    ins = pe.transpose(turn_bank[u % 2][:, P * c:P * (c + 1)], raw[w][:, c, P * j:P * (j + 1)], ident[:, :])
                ins.then_inc(turned, 1)

            def product(h, k, left, right):
                c = k % DC
                if k < 2:
                    pe.wait_ge(summed, 4 * h + (k + 3))
                elif k < 10:
                    pe.wait_ge(moved, 8 * h + (k - 1))
                else:
                    pe.wait_ge(summed, 4 * h + (k - 5))
                for j in range(DC):
                    for n, (x, y) in enumerate(PARTS):
                        ins = pe.matmul(bank[k % 2][:, :], left[x][:, j, P * c:P * (c + 1)], right[y][:, j, :],
                                        start=(j == 0 and n == 0), stop=(j == DC - 1 and n == 2))
                ins.then_inc(made, 1)

            def head(h, last):
                pe.wait_ge(raw_loaded[2], 16 * h + 16)
                for c in range(DC):
                    if c == 2:
                        pe.wait_ge(raw_loaded[3], 16 * h + 16)
                    turn_part(2, 2 * c, 16 * h + 8)
                    turn_part(2, 2 * c + 1, 16 * h + 8)
                    if c == 0:
                        pe.wait_ge(turn_ready, 16 * h + 8)
                    product(h, c, turn[0], turn[1])
                pe.wait_ge(lin_ready, h + 1)
                pe.wait_ge(now_ready, h + 1)
                for i in range(2):
                    pe.wait_ge(head_rows_read, 2 * h + i)
                    for j in range(DC):
                        for n, (x, y) in enumerate(PARTS):
                            ins = pe.matmul(row_bank[i][0:TOK, :], bias_now[:, i, x, j:j + 1].to_broadcast([P, TOK]),
                                            lin[y][:, j, :], start=(j == 0 and n == 0), stop=(j == DC - 1 and n == 2))
                    ins.then_inc(head_rows, 1)
                pe.wait_ge(turn_ready, 16 * h + 16)
                if not last:
                    pe.wait_ge(raw_loaded[0], 16 * h + 32)
                    pe.wait_ge(raw_loaded[1], 16 * h + 32)
                for c in range(DC):
                    if not last:
                        turn_part(0, c, 16 * h + 16)
                    product(h, DC + c, turn[2], lin)
                for c in range(DC):
                    if not last:
                        turn_part(0, DC + c, 16 * h + 16)
                    product(h, 2 * DC + c, turn[3], lin)

            pe.wait_ge(pair_ready, 1)
            pe.sem_inc(made, 1)
            pe.wait_ge(raw_loaded[0], 16)
            for u in range(8):
                if u == DC:
                    pe.wait_ge(raw_loaded[1], 16)
                turn_part(0, u, 0)
            heads(pe, head)
            pe.wait_ge(shift_pair_ready, 1)
            pe.wait_ge(head_rows_read, 2 * HEADS + 1)
            for m, shift_rows_bank in enumerate((*row_bank, bias_bank)):
                for c in range(DC):
                    for n, part in enumerate(xnT):
                        ins = pe.matmul(shift_rows_bank[0:2 * HEADS, 0:BW], shift_pair[:, c, :, :].rearrange("p k h -> p (k h)"),
                                        part[:, c, BW * m:BW * (m + 1)], start=(c == 0 and n == 0),
                                        stop=(c == DC - 1 and n == 1))
                ins.then_inc(shift_rows, 1)
            pe.wait_ge(skip_ready, DC)
            pe.wait_ge(shift_row_ready, NB)
            shift_flat = shift_row[:, :, :].rearrange("q b n -> q (b n)")
            for t in range(NT):
                ins = pe.transpose(shift_bank[0:TOK, 2 * HEADS * t:2 * HEADS * (t + 1)],
                                   shift_flat[:, TOK * t:TOK * (t + 1)], ident[0:2 * HEADS, 0:2 * HEADS])
            ins.then_inc(shift_done, 1)
            for t in range(NT):
                if t >= 2:
                    pe.wait_ge(row_read, t - 1)
                for c in range(DC):
                    for n, (x, y) in enumerate(PARTS):
                        ins = pe.matmul(row_bank[t % 2][0:TOK, :], xnT[x][:, c, TOK * t:TOK * (t + 1)], turn[0][y][:, c, :],
                                        start=(c == 0 and n == 0), stop=(c == DC - 1 and n == 2))
                ins.then_inc(rows_done, 1)


def stage_attend(nc, xnT, counts, folded, fold_bias, row_shift, value_bias, ident, hidden, hidden_stats):
    SCALE = float(D) ** -0.5
    GROUP_STEPS = 6
    with ExitStack() as ctx:
        b = Buffers(nc, ctx)
        query_w = [b.sb(f"a_query_w_{k}", [P, DC, D], F32R) for k in ("hi", "lo")]
        value_w = [b.sb(f"a_value_w_{k}", [P, DC, D], F32R) for k in ("hi", "lo")]
        query_raw, value_raw = folded.raw
        value = [b.sb(f"a_value_{k}", [TOK, NT, D], F32R) for k in ("hi", "lo")]
        value_sum = b.sb("a_value_sum", [TOK, 2, D])
        query_t = [b.sb(f"a_query_t_{k}", [P, DC, GRP], F32R) for k in ("hi", "lo")]
        prob_t = [b.sb(f"a_prob_t_{k}", [TOK, NT, GRP], F32R) for k in ("hi", "lo")]
        count = [b.sb(f"a_count{t}", [TOK, NS], U16) for t in range(2)]
        no_edge = b.sb("a_no_edge", [TOK, NS], BF16)
        score = [b.sb(f"a_score{t}", [TOK, NS]) for t in range(2)]
        fold_bias_now = b.sb("a_fold_bias_now", [P, DC])
        top = b.sb("a_top", [TOK, 2])
        shift = b.sb("a_shift", [TOK, 2])
        den = b.sb("a_den", [TOK, 2])
        inv_den = b.sb("a_inv_den", [TOK, 2])
        hold = b.sb("a_hold", [TOK, 2, D])
        bank_a = b.ps("a_bank_a", [P, NB, 512])
        bank_b = b.ps("a_bank_b", [P, NB, 512])
        bank_c = b.ps("a_bank_c", [P, 2, 512])

        query_loaded, value_loaded = folded.loaded
        count_loaded = [b.sem(f"a_count_loaded{t}") for t in range(2)]
        hold_loaded = b.sem("a_hold_loaded")
        hidden_stored = b.sem("a_hidden_stored")
        bias_ready = b.sem("a_bias_ready")
        query_w_hi = b.sem("a_query_w_hi")
        query_w_ready = b.sem("a_query_w_ready")
        value_w_hi = b.sem("a_value_w_hi")
        value_w_ready = b.sem("a_value_w_ready")
        value_done = b.sem("a_value_done")
        value_summed = b.sem("a_value_summed")
        value_hi = b.sem("a_value_hi")
        value_ready = b.sem("a_value_ready")
        query_done = b.sem("a_query_done")
        query_hi = b.sem("a_query_hi")
        query_ready = b.sem("a_query_ready")
        scored = b.sem("a_scored")
        masked = b.sem("a_masked")
        shift_ready = b.sem("a_shift_ready")
        exp_done = b.sem("a_exp_done")
        weighted = b.sem("a_weighted")
        turned = b.sem("a_turned")
        prob_t_hi = b.sem("a_prob_t_hi")
        prob_t_ready = b.sem("a_prob_t_ready")
        out_done = b.sem("a_out_done")
        added = b.sem("a_added")
        stats_done = b.sem("a_stats_done")
        padded = b.sem("a_padded")
        dve_step = b.sem("a_dve_step")
        block = ctx.enter_context(nc.Block())

        def half(bank, c):
            return bank[:, c // 2, GRP * (c % 2):GRP * (c % 2 + 1)]

        def groups(engine, group, h):
            with engine.Fori(0, NG - 1) as g:
                group(h, g, False)
            group(h, NG - 1, True)

        def turned_parts(bank, t):
            cols = slice(TOK * t, TOK * (t + 1))
            yield (bank[0:TOK, 0:2, 0:500].rearrange("p b (i n) -> p b i n", n=TOK),
                   [part[:, 0:8, cols].rearrange("p (b i) n -> p b i n", b=2) for part in prob_t])
            yield (bank[0:TOK, 2, 0:250].rearrange("p (i n) -> p i n", n=TOK), [part[:, 8:10, cols] for part in prob_t])


        @block.sync
        def _(sp):
            def group(h, g, last):
                nth = h * NG + (g + 1)
                for t in range(2):
                    sp.wait_ge(weighted, 2 * nth - 1 + t)
                    sp.dma_start(count[t][:, 0:N], counts[bass.ds(g * GRP + t * TOK, TOK), 0:N]).then_inc(count_loaded[t], 16)

            with sp.Fori(0, HEADS) as h:
                sp.wait_ge(query_w_ready, h + 1)
                folded.load(sp, 0, (h + 1) % HEADS)
                sp.wait_ge(value_w_ready, h + 1)
                folded.load(sp, 1, (h + 1) % HEADS)
                groups(sp, group, h)
            sp.wait_ge(query_loaded, 16 * (HEADS + 1))
            sp.wait_ge(value_loaded, 16 * (HEADS + 1))

        @block.gpsimd
        def _(pool):
            for t in range(2):
                pool.memset(count[t][:, N:NS].bitcast(BF16), 0.0).then_inc(padded, 1)

        @block.scalar
        def _(act):
            def rows(g):
                return hidden[bass.ds(g * GRP, GRP), :].rearrange("(t p) c -> p t c", p=TOK)

            def value_split(nth):
                act.wait_ge(value_loaded, 16 * nth)
                for c in range(DC):
                    act.activation(value_w[0][:, c, :], value_raw[:, c, :], ACT.Copy).then_inc(value_w_hi, 1)

            def query_split(nth):
                act.wait_ge(query_loaded, 16 * nth)
                act.wait_ge(query_done, (nth - 1) * NG + 1)
                for c in range(DC):
                    act.activation(query_w[0][:, c, :], query_raw[:, c, :], ACT.Copy).then_inc(query_w_hi, 1)

            def query(nth):
                act.wait_ge(query_done, nth + 1)
                for c in range(DC):
                    act.activation(query_t[0][:, c, :], half(bank_c, c), ACT.Identity,
                                   bias=fold_bias_now[:, c:c + 1]).then_inc(query_hi, 1)

            def group(h, g, last):
                nth = h * NG + (g + 1)
                act.wait_ge(hidden_stored, 16 * nth)
                act.wait_ge(stats_done, 2 * nth)
                act.dma_start(hold[:, :, :], rows(g)).then_inc(hold_loaded, 16)
                if last:
                    query_split(h + 2)

                def exp(t):
                    act.wait_ge(shift_ready, 2 * nth - 1 + t)
                    act.activation(score[t][:, :], score[t][:, :], ACT.Exp, bias=shift[:, t:t + 1],
                                   scale=SCALE).then_inc(exp_done, 1)

                def high(t, bank):
                    act.wait_ge(turned, 2 * nth - 1 + t)
                    for part, to in turned_parts(bank, t):
                        ins = act.activation(to[0], part, ACT.Copy)
                    ins.then_inc(prob_t_hi, 1)

                exp(0)
                high(0, bank_a)
                exp(1)
                if last:
                    act.wait_ge(bias_ready, h + 2)
                query(nth + 1)
                high(1, bank_b)
                if last:
                    value_split(h + 2)
                act.wait_ge(added, 2 * nth + 2)
                act.dma_start(rows(g), hold[:, :, :]).then_inc(hidden_stored, 16)

            act.sem_inc(hidden_stored, 16)
            query_split(1)
            value_split(1)
            act.wait_ge(bias_ready, 1)
            query(1)
            with act.Fori(0, HEADS) as h:
                for s in range(NT):
                    act.wait_ge(value_summed, NT * h + s + 1)
                    act.activation(value[0][:, s, :], value_sum[:, s % 2, :], ACT.Copy).then_inc(value_hi, 1)
                groups(act, group, h)
            act.wait_ge(hidden_stored, 16 * (HEADS * NG + 1))

        @block.vector
        def _(dve):
            def value_split(nth):
                for c in range(DC):
                    dve.wait_ge(value_w_hi, DC * (nth - 1) + (c + 1))
                    ins = dve.tensor_tensor(value_w[1][:, c, :], value_raw[:, c, :], value_w[0][:, c, :].bitcast(F32), ALU.subtract)
                ins.then_inc(value_w_ready, 1)

            def query_split(nth):
                for c in range(DC):
                    dve.wait_ge(query_w_hi, DC * (nth - 1) + (c + 1))
                    ins = dve.tensor_tensor(query_w[1][:, c, :], query_raw[:, c, :], query_w[0][:, c, :].bitcast(F32), ALU.subtract)
                ins.then_inc(query_w_ready, 1)

            def bias(h):
                dve.tensor_scalar(fold_bias_now[:, :], fold_bias[:, bass.ds(h, 1), :].rearrange("p o c -> p (o c)"), 1.0,
                                  None, ALU.mult).then_inc(bias_ready, 1)

            def query(nth):
                for c in range(DC):
                    dve.wait_ge(query_hi, 4 * nth - 3 + (c | 1))
                    dve.scalar_tensor_tensor(query_t[1][:, c, :], half(bank_c, c), fold_bias_now[:, c:c + 1],
                                             query_t[0][:, c, :].bitcast(F32), ALU.add, ALU.subtract
                                             ).then_inc(query_ready, 1)

            def group(h, g, last):
                nth = h * NG + (g + 1)
                link = Steps(dve, dve_step, (nth - 1) * GROUP_STEPS, GROUP_STEPS)
                banks = (bank_a, bank_b)

                def mask(t):
                    dve.wait_ge(count_loaded[t], 16 * nth)
                    link(dve.tensor_scalar(no_edge[:, :], count[t][:, :], 0.0, -FAR, ALU.is_equal, ALU.mult))

                def largest(t):
                    dve.wait_ge(scored, 2 * nth - 1 + t)
                    dve.scalar_tensor_tensor(score[t][:, :].rearrange("p (b n) -> p b n", b=NB),
                                             no_edge[:, :].rearrange("p (b n) -> p b n", b=NB),
                                             row_shift[:, bass.ds(g * 2 + t, 1), bass.ds(h, 1)].rearrange("p a o -> p (a o)"),
                                             banks[t][0:TOK, :, 0:BW], ALU.add, ALU.add).then_inc(masked, 1)
                    dve.wait_ge(masked, 2 * nth - 1 + t)
                    link(dve.tensor_reduce(top[:, t:t + 1], score[t][:, :], AX.X, ALU.max))
                    dve.tensor_scalar(shift[:, t:t + 1], top[:, t:t + 1], -SCALE, None, ALU.mult).then_inc(shift_ready, 1)

                def weigh(t):
                    dve.wait_ge(exp_done, 2 * nth - 1 + t)
                    dve.scalar_tensor_tensor(score[t][:, :], count[t][:, :], 1.0, score[t][:, :], ALU.mult, ALU.mult,
                                             accum_out=den[:, t:t + 1]).then_inc(weighted, 1)
                    dve.wait_ge(weighted, 2 * nth + 1 + t)
                    link(dve.tensor_scalar(den[:, t:t + 1], den[:, t:t + 1], 0.5, None, ALU.max))
                    dve.reciprocal(inv_den[:, t:t + 1], den[:, t:t + 1])

                def low(t, bank):
                    dve.wait_ge(prob_t_hi, 2 * nth - 1 + t)
                    for part, to in turned_parts(bank, t):
                        ins = dve.tensor_tensor(to[1], part, to[0].bitcast(F32), ALU.subtract)
                    ins.then_inc(prob_t_ready, 1)

                mask(0)
                if last:
                    query_split(h + 2)
                    bias((h + 1) % HEADS)
                largest(0)
                mask(1)
                weigh(0)
                largest(1)
                low(0, bank_a)
                weigh(1)
                assert link.n == GROUP_STEPS
                if last:
                    dve.wait_ge(bias_ready, h + 2)
                query(nth + 1)
                low(1, bank_b)
                if last:
                    value_split(h + 2)
                dve.wait_ge(hold_loaded, 16 * nth)
                for t, bank in ((0, bank_a), (1, bank_b)):
                    dve.wait_ge(out_done, 2 * nth - 1 + t)
                    dve.scalar_tensor_tensor(hold[:, t, :], bank[0:TOK, 0, :], inv_den[:, t:t + 1], hold[:, t, :],
                                             ALU.mult, ALU.add).then_inc(added, 1)
                for t in range(2):
                    dve.wait_ge(added, 2 * nth + 1 + t)
                    dve.wait_ge(stats_done, 2 * nth)
                    dve.bn_stats(hidden_stats[:, bass.ds(g * 2 + t, 1), :].rearrange("p o k -> p (o k)"), hold[:, t, :]
                                 ).then_inc(stats_done, 1)

            dve.wait_ge(padded, 2)
            dve.sem_inc(weighted, 2)
            dve.sem_inc(added, 2)
            dve.sem_inc(stats_done, 2)
            bias(0)
            query_split(1)
            value_split(1)
            dve.wait_ge(bias_ready, 1)
            query(1)
            with dve.Fori(0, HEADS) as h:
                for s in range(NT):
                    bank = (bank_a, bank_b)[(s // 2) % 2]
                    dve.wait_ge(value_done, NT * h + s + 1)
                    dve.tensor_tensor(value_sum[:, s % 2, :], bank[0:TOK, s % 2, :],
                                      value_bias[:, bass.ds(h, 1), :].rearrange("p o n -> p (o n)"),
                                      ALU.add).then_inc(value_summed, 1)
                    dve.wait_ge(value_hi, NT * h + s + 1)
                    dve.tensor_tensor(value[1][:, s, :], value_sum[:, s % 2, :], value[0][:, s, :].bitcast(F32),
                                      ALU.subtract).then_inc(value_ready, 1)
                groups(dve, group, h)

        @block.tensor
        def _(pe):
            def query(g):
                for m in range(DC):
                    for c in range(DC):
                        for n, (x, y) in enumerate(PARTS):
                            ins = pe.matmul(half(bank_c, m), query_w[x][:, c, P * m:P * (m + 1)],
                                            xnT[y][:, c, bass.ds(g * GRP, GRP)], start=(c == 0 and n == 0),
                                            stop=(c == DC - 1 and n == 2))
                ins.then_inc(query_done, 1)

            def group(h, g, last):
                nth = h * NG + (g + 1)
                banks = (bank_a, bank_b)

                def turn(t):
                    pe.wait_ge(weighted, 2 * nth + 1 + t)
                    for s in range(NT):
                        ins = pe.transpose(banks[t][0:TOK, s // 4, TOK * (s % 4):TOK * (s % 4 + 1)],
                                           score[t][:, TOK * s:TOK * (s + 1)], ident[0:TOK, 0:TOK])
                    ins.then_inc(turned, 1)

                pe.wait_ge(query_ready, 4 * nth)
                for t in range(2):
                    pe.wait_ge(value_summed, NT * h + NT)
                    pe.wait_ge(added, 2 * nth - 1 + t)
                    for c in range(DC):
                        for n, (x, y) in enumerate(PARTS):
                            for m in range(NB):
                                ins = pe.matmul(banks[t][0:TOK, m, 0:BW], query_t[x][:, c, TOK * t:TOK * (t + 1)],
                                                xnT[y][:, c, BW * m:BW * (m + 1)], start=(c == 0 and n == 0),
                                                stop=(c == DC - 1 and n == 2))
                    ins.then_inc(scored, 1)
                turn(0)
                if last:
                    pe.wait_ge(query_w_ready, h + 2)
                query(0 if last else g + 1)
                turn(1)
                pe.wait_ge(value_ready, NT * h + NT)
                for t in range(2):
                    pe.wait_ge(prob_t_ready, 2 * nth - 1 + t)
                    for s in range(NT):
                        for n, (x, y) in enumerate(PARTS):
                            ins = pe.matmul(banks[t][0:TOK, 0, :], prob_t[x][:, s, TOK * t:TOK * (t + 1)], value[y][:, s, :],
                                            start=(s == 0 and n == 0), stop=(s == NT - 1 and n == 2))
                    ins.then_inc(out_done, 1)

            pe.sem_inc(query_done, 1)
            pe.wait_ge(query_w_ready, 1)
            query(0)
            with pe.Fori(0, HEADS) as h:
                pe.wait_ge(value_w_ready, h + 1)
                for s in range(NT):
                    bank = (bank_a, bank_b)[(s // 2) % 2]
                    if s == 0 or s == 2:
                        pe.wait_ge(added, 2 * NG * h + 1 + s // 2)
                    if s >= 4:
                        pe.wait_ge(value_summed, NT * h + s - 3)
                    for c in range(DC):
                        for n, (x, y) in enumerate(PARTS):
                            ins = pe.matmul(bank[0:TOK, s % 2, :], xnT[x][:, c, TOK * s:TOK * (s + 1)],
                                            value_w[y][:, c, :], start=(c == 0 and n == 0), stop=(c == DC - 1 and n == 2))
                    ins.then_inc(value_done, 1)
                groups(pe, group, h)


def wide(bank, rows, n=N):
    return ((bank[rows, 0:2, 0:500], slice(0, 1000)), (bank[rows, 2, 0:250], slice(1000, 1250)))


def stage_mix(nc, xrow, ident, w_qkv, w_out, norm_gamma, mixed, mixed_norm):
    FEAT = MIX_HEADS * MIX_DIM
    with ExitStack() as outer:
        b = Buffers(nc, outer)
        xm_t = [b.sb(f"m_xm_t_{k}", [P, DC, N], F32R) for k in ("hi", "lo")]
        wt = [[b.sb(f"m_wt_{i}_{k}", [P, DC, FEAT], F32R) for k in ("hi", "lo")] for i in "qkv"]
        shared = b.sb("m_shared", [P, NT * D])
        raw = [shared[:, 2048 * i:2048 * (i + 1)].rearrange("p (c n) -> p c n", c=DC) for i in range(2)]
        key = shared[0:TOK, :].rearrange("p (t n) -> p t n", t=NT)
        w_out_raw = b.sb("m_w_out_raw", [P, DC, FEAT])
        w_out_loaded = b.sem("m_w_out_loaded")

        with ExitStack() as ctx:
            b = Buffers(nc, ctx)
            stats = b.sb("m_stats", [TOK, NT, 6])
            mean_var = b.sb("m_mean_var", [TOK, NT, 2])
            root_in = b.sb("m_root_in", [TOK, NT])
            root = b.sb("m_root", [TOK, NT])
            scratch = b.sb("m_scratch", [TOK, NT])
            rstd = b.sb("m_rstd", [TOK, NT])
            gamma_in = b.sb("m_gamma_in", [DC, P])
            gamma = b.sb("m_gamma", [P, DC])
            bank = [b.ps(f"m_bank{i}", [P, 512]) for i in range(4)]
            gamma_bank = b.ps("m_gamma_bank", [P, 512])
            gamma_loaded = b.sem("m_gamma_loaded")
            gamma_turned = b.sem("m_gamma_turned")
            gamma_ready = b.sem("m_gamma_ready")
            raw_loaded = [b.sem(f"m_raw_loaded{i}") for i in range(2)]
            dve_step = b.sem("m_dve_step")
            var_ready = b.sem("m_var_ready")
            root_ready = b.sem("m_root_ready")
            row_ready = b.sem("m_row_ready")
            turned = b.sem("m_turned")
            hi_ready = b.sem("m_hi_ready")
            lo_ready = b.sem("m_lo_ready")
            block = ctx.enter_context(nc.Block())
            units = [("w", i, c) for i in range(3) for c in range(DC)] + [("x", g, c) for g in range(3) for c in range(DC)]

            def place(kind, i, c):
                if kind == "w":
                    return [wt[i][k][:, c, :] for k in range(2)], FEAT
                n = TOK * len(tile_parts(i))
                return [xm_t[k][:, c, 500 * i:500 * i + n] for k in range(2)], n

            @block.sync
            def _(sp):
                sp.dma_start(gamma_in[:, :], norm_gamma.rearrange("(c p) -> c p", p=P)).then_inc(gamma_loaded, 16)
                for i in range(3):
                    if i == 2:
                        sp.wait_ge(turned, DC)
                    sp.dma_start(raw[i % 2][:, :, :], w_qkv[FEAT * i:FEAT * (i + 1), :].rearrange(
                        "(r p) n -> p r n", p=P)).then_inc(raw_loaded[i % 2], 16)
                sp.dma_start(w_out_raw[:, :, :], w_out.rearrange("(r p) n -> p r n", p=P)).then_inc(w_out_loaded, 16)

            @block.vector
            def _(dve):
                link = chain(dve, dve_step)
                node_stats(dve, link, xrow, stats, mean_var, root_in).then_inc(var_ready, 1)
                dve.wait_ge(root_ready, 1)
                inverse_root(dve, link, root_in[:, :], root[:, :], scratch[:, :], rstd[:, :])
                for t in range(NT):
                    dve.tensor_scalar(xrow[:, t, :], xrow[:, t, :], mean_var[:, t, 0:1], rstd[:, t:t + 1],
                                      ALU.subtract, ALU.mult).then_inc(row_ready, 1)
                dve.wait_ge(gamma_turned, 1)
                dve.tensor_copy(gamma[:, :], gamma_bank[:, 0:DC]).then_inc(gamma_ready, 1)
                dve.wait_ge(gamma_ready, 1)
                for u, (kind, i, c) in enumerate(units):
                    (hi, lo), n = place(kind, i, c)
                    dve.wait_ge(hi_ready, u + 1)
                    if kind == "w":
                        ins = dve.tensor_tensor(lo, bank[u % 4][:, 0:n], hi.bitcast(F32), ALU.subtract)
                    else:
                        ins = dve.scalar_tensor_tensor(lo, bank[u % 4][:, 0:n], gamma[:, c:c + 1], hi.bitcast(F32),
                                                       ALU.mult, ALU.subtract)
                    ins.then_inc(lo_ready, 1)

            @block.scalar
            def _(act):
                act.wait_ge(var_ready, 1)
                act.activation(root[:, :], root_in[:, :], ACT.Sqrt).then_inc(root_ready, 1)
                act.wait_ge(gamma_ready, 1)
                for u, (kind, i, c) in enumerate(units):
                    (hi, lo), n = place(kind, i, c)
                    act.wait_ge(turned, u + 1)
                    act.activation(hi, bank[u % 4][:, 0:n], ACT.Copy,
                                   scale=1.0 if kind == "w" else gamma[:, c:c + 1]).then_inc(hi_ready, 1)

            @block.tensor
            def _(pe):
                pe.wait_ge(gamma_loaded, 16)
                pe.transpose(gamma_bank[:, 0:DC], gamma_in[:, :], ident[0:DC, 0:DC]).then_inc(gamma_turned, 1)
                for u, (kind, i, c) in enumerate(units):
                    if u >= 4:
                        pe.wait_ge(lo_ready, u - 3)
                    if kind == "w":
                        pe.wait_ge(raw_loaded[i % 2], 16 * (i // 2 + 1))
                        for r in range(DC):
                            ins = pe.transpose(bank[u % 4][:, P * r:P * (r + 1)], raw[i % 2][:, r, P * c:P * (c + 1)],
                                               ident[:, :])
                    else:
                        pe.wait_ge(row_ready, tile_parts(i)[-1] + 1)
                        for j, t in enumerate(tile_parts(i)):
                            ins = pe.transpose(bank[u % 4][:, TOK * j:TOK * (j + 1)], xrow[:, t, P * c:P * (c + 1)],
                                               ident[0:TOK, 0:TOK])
                    ins.then_inc(turned, 1)

        with ExitStack() as ctx:
            b = Buffers(nc, ctx)
            value = xrow
            key_exp = [b.sb(f"m_key_exp{i}", [P, N]) for i in range(2)]
            key_top = b.sb("m_key_top", [P, DC])
            key_sum = b.sb("m_key_sum", [P, DC])
            key_scale = b.sb("m_key_scale", [P, DC])
            context = [b.sb(f"m_context_{k}", [P, DC, P], F32R) for k in ("hi", "lo")]
            key_bank = [b.ps(f"m_key_bank{i}", [P, 3, 512]) for i in range(2)]
            row_bank = [b.ps(f"m_row_bank{i}", [P, 512]) for i in range(2)]
            key_done = b.sem("m_key_done")
            key_copied = b.sem("m_key_copied")
            top_ready = b.sem("m_top_ready")
            exp_done = b.sem("m_exp_done")
            key_turned = b.sem("m_key_turned")
            key_ready = b.sem("m_key_ready")
            row_done = b.sem("m_row_done")
            row_hi = b.sem("m_row_hi")
            row_ready = b.sem("m_row2_ready")
            clear = b.sem("m_clear")
            scale_ready = b.sem("m_scale_ready")
            dve_step = b.sem("m_dve_step2")
            block = ctx.enter_context(nc.Block())
            TURNS, CONTEXTS = NT, NT + DC
            PRODUCTS = NT + 2 * DC
            USES = NT + 3 * DC

            @block.gpsimd
            def _(pool):
                for k in range(2):
                    pool.memset(context[k][:, :, :].bitcast(F32), 0.0).then_inc(clear, 1)

            @block.scalar
            def _(act):
                def key_part(f):
                    act.wait_ge(key_done, f + 1)
                    for part, cols in wide(key_bank[f % 2], slice(0, P)):
                        out = key_exp[f % 2][:, cols]
                        ins = act.activation(out.rearrange("p (b n) -> p b n", n=500) if cols.start == 0 else out,
                                             part, ACT.Copy)
                    ins.then_inc(key_copied, 1)
                    act.wait_ge(top_ready, f + 1)
                    act.activation(key_exp[f % 2][:, :], key_exp[f % 2][:, :], ACT.Exp, bias=key_top[:, f:f + 1],
                                   accum_out=key_sum[:, f:f + 1]).then_inc(exp_done, 1)

                def row(u):
                    act.wait_ge(row_done, u + 1)
                    src = row_bank[u % 2]
                    if u < TURNS:
                        act.activation(value[:, u, :], src[0:TOK, :], ACT.Copy).then_inc(row_hi, 1)
                    elif u < CONTEXTS:
                        act.activation(wt[2][0][:, u - TURNS, :], src[:, :], ACT.Copy).then_inc(row_hi, 1)
                    elif u < PRODUCTS:
                        f = u - CONTEXTS
                        act.activation(context[0][0:64, f, 0:64], src[0:64, 0:64], ACT.Copy)
                        act.activation(context[0][64:128, f, 64:128], src[64:128, 64:128], ACT.Copy).then_inc(row_hi, 1)
                    else:
                        f = u - PRODUCTS
                        act.activation(wt[1][0][:, f, :], src[:, :], ACT.Copy, scale=key_scale[:, f:f + 1]).then_inc(row_hi, 1)

                key_part(0)
                key_part(1)
                for u in range(5):
                    row(u)
                key_part(2)
                key_part(3)
                for u in range(5, CONTEXTS):
                    row(u)
                act.wait_ge(clear, 2)
                act.wait_ge(scale_ready, 1)
                for u in range(CONTEXTS, USES):
                    row(u)

            @block.vector
            def _(dve):
                link = chain(dve, dve_step)

                def top(f):
                    dve.wait_ge(key_copied, f + 1)
                    dve.tensor_reduce(key_top[:, f:f + 1], key_exp[f % 2][:, :], AX.X, ALU.max,
                                      negate=True).then_inc(top_ready, 1)

                def turn(f):
                    dve.wait_ge(key_turned, f + 1)
                    for part, tiles in ((key_bank[f % 2][0:TOK, 0:2, :], slice(0, 8)), (key_bank[f % 2][0:TOK, 2, 0:256], slice(8, 10))):
                        out = key[:, tiles, P * f:P * (f + 1)]
                        ins = dve.tensor_copy(out.rearrange("p (b i) n -> p b i n", i=4) if tiles.start == 0 else out,
                                              part.rearrange("p b (i n) -> p b i n", n=P) if tiles.start == 0
                                              else part.rearrange("p (i n) -> p i n", n=P))
                    ins.then_inc(key_ready, 1)

                def row(u):
                    dve.wait_ge(row_hi, u + 1)
                    src = row_bank[u % 2]
                    if u < CONTEXTS:
                        f = u - TURNS
                        dve.tensor_tensor(wt[2][1][:, f, :], src[:, :], wt[2][0][:, f, :].bitcast(F32),
                                          ALU.subtract).then_inc(row_ready, 1)
                    elif u < PRODUCTS:
                        f = u - CONTEXTS
                        for lo in (0, 64):
                            at = slice(lo, lo + 64)
                            ins = dve.tensor_tensor(context[1][at, f, at], src[at, at], context[0][at, f, at].bitcast(F32),
                                                    ALU.subtract)
                        ins.then_inc(row_ready, 1)
                    else:
                        f = u - PRODUCTS
                        dve.scalar_tensor_tensor(wt[1][1][:, f, :], src[:, :], key_scale[:, f:f + 1],
                                                 wt[1][0][:, f, :].bitcast(F32), ALU.mult, ALU.subtract
                                                 ).then_inc(row_ready, 1)

                top(0)
                top(1)
                turn(0)
                top(2)
                turn(1)
                top(3)
                turn(2)
                turn(3)
                for u in range(TURNS, CONTEXTS):
                    row(u)
                dve.wait_ge(exp_done, DC)
                link(dve.reciprocal(key_scale[:, :], key_sum[:, :]))
                dve.tensor_scalar(key_scale[:, :], key_scale[:, :], MIX_DIM ** -0.5, None, ALU.mult).then_inc(scale_ready, 1)
                dve.wait_ge(scale_ready, 1)
                dve.wait_ge(clear, 2)
                for u in range(CONTEXTS, USES):
                    row(u)

            @block.tensor
            def _(pe):
                def keys(f):
                    if f >= 2:
                        pe.wait_ge(key_ready, f - 1)
                    for c in range(DC):
                        for n, (x, y) in enumerate(PARTS):
                            for m, w in enumerate((500, 500, 250)):
                                ins = pe.matmul(key_bank[f % 2][:, m, 0:w], wt[1][x][:, c, P * f:P * (f + 1)],
                                                xm_t[y][:, c, 500 * m:500 * m + w], start=(c == 0 and n == 0),
                                                stop=(c == DC - 1 and n == 2))
                    ins.then_inc(key_done, 1)

                def turn(f):
                    pe.wait_ge(exp_done, f + 1)
                    for t in range(NT):
                        ins = pe.transpose(key_bank[f % 2][0:TOK, t // 4, P * (t % 4):P * (t % 4 + 1)],
                                           key_exp[f % 2][:, TOK * t:TOK * (t + 1)], ident[:, :])
                    ins.then_inc(key_turned, 1)

                def bank_free(u):
                    if u >= 2:
                        if u - 2 < TURNS:
                            pe.wait_ge(row_hi, u - 1)
                        else:
                            pe.wait_ge(row_ready, u - 1 - TURNS)

                def values(t):
                    bank_free(t)
                    for c in range(DC):
                        for n, (x, y) in enumerate(PARTS):
                            ins = pe.matmul(row_bank[t % 2][0:TOK, :], xm_t[x][:, c, TOK * t:TOK * (t + 1)],
                                            wt[2][y][:, c, :], start=(c == 0 and n == 0), stop=(c == DC - 1 and n == 2))
                    ins.then_inc(row_done, 1)

                keys(0)
                keys(1)
                for t in range(5):
                    values(t)
                turn(0)
                keys(2)
                turn(1)
                keys(3)
                for t in range(5, NT):
                    values(t)
                turn(2)
                turn(3)
                pe.wait_ge(w_out_loaded, 16)
                for f in range(DC):
                    u = TURNS + f
                    bank_free(u)
                    for r in range(DC):
                        ins = pe.transpose(row_bank[u % 2][:, P * r:P * (r + 1)], w_out_raw[:, r, P * f:P * (f + 1)], ident[:, :])
                    ins.then_inc(row_done, 1)
                for f in range(DC):
                    u = CONTEXTS + f
                    bank_free(u)
                    pe.wait_ge(key_ready, DC)
                    for t in range(NT):
                        ins = pe.matmul(row_bank[u % 2][:, 0:P], value[:, t, P * f:P * (f + 1)], key[:, t, P * f:P * (f + 1)],
                                        start=(t == 0), stop=(t == NT - 1))
                    ins.then_inc(row_done, 1)
                for f in range(DC):
                    u = PRODUCTS + f
                    pe.wait_ge(row_ready, DC + f + 1)
                    bank_free(u)
                    for n, (x, y) in enumerate(PARTS):
                        ins = pe.matmul(row_bank[u % 2][:, :], context[x][:, f, :], wt[2][y][:, f, :], start=(n == 0), stop=(n == 2))
                    ins.then_inc(row_done, 1)

            @block.sync
            def _(sp):
                sp.wait_ge(w_out_loaded, 16)

        with ExitStack() as ctx:
            b = Buffers(nc, ctx)
            query = [b.sb(f"m_query{i}", [TOK, FEAT]) for i in range(2)]
            top = b.sb("m_top", [TOK, 2, MIX_HEADS])
            total = b.sb("m_total", [TOK, 2, MIX_HEADS])
            query_t = [b.sb(f"m_query_t_{k}", [P, DC, TOK], F32R) for k in ("hi", "lo")]
            out_row = [b.sb(f"m_out_row{i}", [TOK, D]) for i in range(2)]
            query_bank = [b.ps(f"m_query_bank{i}", [P, 512]) for i in range(2)]
            turn_bank = b.ps("m_turn_bank", [P, 512])
            out_bank = [b.ps(f"m_out_bank{i}", [P, 512]) for i in range(2)]
            query_done = b.sem("m_query_done")
            centred = b.sem("m_centred")
            exp_done = b.sem("m_exp_done2")
            query_ready = b.sem("m_query_ready")
            turned = b.sem("m_turned2")
            turn_hi = b.sem("m_turn_hi")
            turn_ready = b.sem("m_turn_ready")
            out_done = b.sem("m_out_done")
            out_copied = b.sem("m_out_copied")
            stored = [b.sem(f"m_stored{i}") for i in range(2)]
            counted = b.sem("m_counted")
            var_ready = b.sem("m_out_var_ready")
            root_ready = b.sem("m_out_root_ready")
            stats = b.sb("m_out_stats", [TOK, NT, 6])
            mean_var = b.sb("m_out_mean_var", [TOK, NT, 2])
            root_in = b.sb("m_out_root_in", [TOK, NT])
            root = b.sb("m_out_root", [TOK, NT])
            scratch = b.sb("m_out_scratch", [TOK, NT])
            dve_step = b.sem("m_dve_step3")
            block = ctx.enter_context(nc.Block())

            def heads(ap):
                return ap.rearrange("p (h e) -> p h e", h=MIX_HEADS)

            def spread(ap):
                return ap.unsqueeze(2).to_broadcast([TOK, MIX_HEADS, MIX_DIM])

            @block.sync
            def _(sp):
                for t in range(NT):
                    sp.wait_ge(out_copied, t + 1)
                    sp.dma_start(mixed[TOK * t:TOK * (t + 1), :], out_row[t % 2][:, :]).then_inc(stored[t % 2], 16)
                for i in range(2):
                    sp.wait_ge(stored[i], 16 * NT // 2)

            @block.scalar
            def _(act):
                def out(t):
                    act.wait_ge(out_done, t + 1)
                    if t >= 2:
                        act.wait_ge(stored[t % 2], 16 * (t // 2))
                        act.wait_ge(counted, t - 1)
                    act.activation(out_row[t % 2][:, :], out_bank[t % 2][0:TOK, :], ACT.Copy).then_inc(out_copied, 1)

                for t in range(NT):
                    act.wait_ge(centred, t + 1)
                    act.activation(query[t % 2][:, :], query[t % 2][:, :], ACT.Exp).then_inc(exp_done, 1)
                    act.wait_ge(turned, t + 1)
                    act.activation(query_t[0][:, :, :].rearrange("p c n -> p (c n)"), turn_bank[:, 0:4 * TOK],
                                   ACT.Copy).then_inc(turn_hi, 1)
                    if t:
                        out(t - 1)
                out(NT - 1)
                act.wait_ge(var_ready, 1)
                act.activation(root[:, :], root_in[:, :], ACT.Sqrt).then_inc(root_ready, 1)

            @block.vector
            def _(dve):
                link = chain(dve, dve_step)

                def centre(t):
                    dve.wait_ge(query_done, t + 1)
                    link(dve.tensor_reduce(top[:, t % 2, :], heads(query_bank[t % 2][0:TOK, :]), AX.X, ALU.max))
                    dve.tensor_tensor(heads(query[t % 2][:, :]), heads(query_bank[t % 2][0:TOK, :]), spread(top[:, t % 2, :]),
                                      ALU.subtract).then_inc(centred, 1)

                def count(t):
                    dve.wait_ge(out_copied, t + 1)
                    dve.bn_stats(stats[:, t, :], out_row[t % 2][:, :]).then_inc(counted, 1)

                centre(0)
                for t in range(NT):
                    dve.wait_ge(exp_done, t + 1)
                    link(dve.tensor_reduce(total[:, t % 2, :], heads(query[t % 2][:, :]), AX.X, ALU.add))
                    link(dve.reciprocal(total[:, t % 2, :], total[:, t % 2, :]))
                    dve.tensor_tensor(heads(query[t % 2][:, :]), heads(query[t % 2][:, :]), spread(total[:, t % 2, :]),
                                      ALU.mult).then_inc(query_ready, 1)
                    if t + 1 < NT:
                        centre(t + 1)
                    dve.wait_ge(turn_hi, t + 1)
                    dve.tensor_tensor(query_t[1][:, :, :].rearrange("p c n -> p (c n)"), turn_bank[:, 0:4 * TOK],
                                      query_t[0][:, :, :].rearrange("p c n -> p (c n)").bitcast(F32),
                                      ALU.subtract).then_inc(turn_ready, 1)
                    if t >= 2:
                        count(t - 2)
                count(NT - 2)
                count(NT - 1)
                dve.wait_ge(counted, NT)
                for t in range(NT):
                    ins = dve.bn_aggr(mean_var[:, t, :], stats[:, t, :])
                link(ins)
                dve.tensor_scalar(root_in[:, :], mean_var[:, :, 1], EPS, None, ALU.add).then_inc(var_ready, 1)
                dve.wait_ge(root_ready, 1)
                inverse_root(dve, link, root_in[:, :], root[:, :], scratch[:, :], mixed_norm[:, 0, :])
                link(dve.scalar_tensor_tensor(mixed_norm[:, 1, :], mean_var[:, :, 0], -1.0, mixed_norm[:, 0, :],
                                              ALU.mult, ALU.mult))

            @block.tensor
            def _(pe):
                def queries(t):
                    if t >= 2:
                        pe.wait_ge(centred, t - 1)
                    for c in range(DC):
                        for n, (x, y) in enumerate(PARTS):
                            ins = pe.matmul(query_bank[t % 2][0:TOK, :], xm_t[x][:, c, TOK * t:TOK * (t + 1)],
                                            wt[0][y][:, c, :], start=(c == 0 and n == 0), stop=(c == DC - 1 and n == 2))
                    ins.then_inc(query_done, 1)

                def outs(t):
                    pe.wait_ge(turn_ready, t + 1)
                    if t >= 2:
                        pe.wait_ge(out_copied, t - 1)
                    for f in range(DC):
                        for n, (x, y) in enumerate(PARTS):
                            ins = pe.matmul(out_bank[t % 2][0:TOK, :], query_t[x][:, f, :], wt[1][y][:, f, :],
                                            start=(f == 0 and n == 0), stop=(f == DC - 1 and n == 2))
                    ins.then_inc(out_done, 1)

                queries(0)
                queries(1)
                for t in range(NT):
                    pe.wait_ge(query_ready, t + 1)
                    for f in range(DC):
                        ins = pe.transpose(turn_bank[:, TOK * f:TOK * (f + 1)], query[t % 2][:, P * f:P * (f + 1)],
                                           ident[0:TOK, 0:TOK])
                    ins.then_inc(turned, 1)
                    if t + 2 < NT:
                        queries(t + 2)
                    outs(t)


class ExpertInputs:
    RING = 4

    def __init__(self, b, w1, b1, w2):
        self.dram = (w1, w2)
        self.weights = [[b.sb(f"e_weights{w}_{k}", [P, DC, D]) for k in range(self.RING)] for w in range(2)]
        self.loaded = [[b.sem(f"e_loaded{w}_{k}") for k in range(self.RING)] for w in range(2)]
        self.b1 = b1
        self.bias_in = b.sb("e_bias_in", [EXPERTS, D])
        self.bias_loaded = b.sem("e_bias_loaded")

    def load(self, sp, w, e, k):
        sp.dma_start(self.weights[w][k][:, :, :], self.dram[w][bass.ds(e, 1), :, :].rearrange("o (c p) n -> p (o c) n", p=P)
                     ).then_inc(self.loaded[w][k], 16)

    def load_first(self, sp):
        sp.dma_start(self.bias_in[:, :], self.b1).then_inc(self.bias_loaded, 16)
        for k in range(self.RING):
            for w in range(2):
                self.load(sp, w, k, k)


def stage_join(nc, hidden, hidden_stats, base, gamma, w_gate, ident, x1, xn2, route, slots_in, expert_inputs):
    scatter_at, gather_at, weight, select_t, some, none = route
    E = EXPERTS
    with ExitStack() as ctx:
        b = Buffers(nc, ctx)
        row = b.sb("j_row", [TOK, NT, D])
        gamma_row = b.sb("j_gamma_row", [TOK, D])
        x1_stats = b.sb("j_x1_stats", [TOK, NT, 6])
        mean_var = b.sb("j_mean_var", [TOK, 2, NT, 2])
        root_in = b.sb("j_root_in", [TOK, 2, NT])
        root = b.sb("j_root", [TOK, 2, NT])
        scratch = b.sb("j_scratch", [TOK, 2, NT])
        rstd = b.sb("j_rstd", [TOK, 2, NT])
        xn2_t = b.sb("j_xn2_t", [P, DC, N])
        gate_w = b.sb("j_gate_w", [P, DC, E])
        before = b.sb("j_before", [TOK, TOK], BF16)
        ones = b.sb("j_ones", [TOK, TOK], BF16)
        expert_no = b.sb("j_expert_no", [TOK, E])
        dump = b.sb("j_dump", [TOK, TOPK, NT])
        prob = b.sb("j_prob", [TOK, NT, E])
        left = b.sb("j_left", [TOK, NT, E])
        same = b.sb("j_same", [TOK, NT, E])
        hot = b.sb("j_hot", [TOK, TOPK, NT, E])
        taken = b.sb("j_taken", [TOK, NT, E], BF16)
        best = b.sb("j_best", [TOK, TOPK, NT])
        expert = b.sb("j_expert", [TOK, TOPK, NT])
        rank = b.sb("j_rank", [TOK, TOPK, NT])
        keep = b.sb("j_keep", [TOK, TOPK, NT])
        dest = b.sb("j_dest", [TOK, TOPK, NT])
        place = b.sb("j_place", [TOK, TOPK, NT])
        norm = b.sb("j_norm", [TOK, NT])
        bank = [b.ps(f"j_bank{i}", [P, 512]) for i in range(4)]
        logit = b.ps("j_logit", [P, 512])
        rank_bank = b.ps("j_rank_bank", [P, 512])
        loaded = [b.sem(f"j_loaded{g}") for g in range(NG)]
        base_loaded = b.sem("j_base_loaded")
        gamma_loaded = b.sem("j_gamma_loaded")
        gate_loaded = b.sem("j_gate_loaded")
        consts = b.sem("j_consts")
        dve_step = b.sem("j_dve_step")
        var_ready = b.sem("j_var_ready")
        root_ready = b.sem("j_root_ready")
        row_ready = b.sem("j_row_ready")
        turned = b.sem("j_turned")
        copied = b.sem("j_copied")
        gated = b.sem("j_gated")
        centred = b.sem("j_centred")
        exp_done = b.sem("j_exp_done")
        taken_ready = b.sem("j_taken_ready")
        ranked = b.sem("j_ranked")
        places_ready = b.sem("j_places_ready")
        select_ready = b.sem("j_select_ready")
        scattered = b.sem("j_scattered")
        block = ctx.enter_context(nc.Block())
        units = [(g, c) for g in range(3) for c in range(DC)]

        def tiles(dram):
            return dram.rearrange("(t p) c -> p t c", p=TOK)

        def over_experts(ap):
            return ap.unsqueeze(2).to_broadcast([TOK, NT, E])

        @block.sync
        def _(sp):
            sp.dma_start(gamma_row[:, :], gamma.unsqueeze(0).to_broadcast([TOK, D])).then_inc(gamma_loaded, 16)
            for g in range(NG):
                sp.dma_start(row[:, 2 * g:2 * g + 2, :], tiles(hidden)[:, 2 * g:2 * g + 2, :]).then_inc(loaded[g], 16)
            sp.dma_start(x1[:, :, :], tiles(base)).then_inc(base_loaded, 16)
            sp.dma_start(gate_w[:, :, :], w_gate.rearrange("(c p) e -> p c e", p=P)).then_inc(gate_loaded, 16)
            expert_inputs.load_first(sp)

        @block.gpsimd
        def _(pool):
            pool.memset(ones[:, :], 1.0).then_inc(consts, 1)
            pool.iota(expert_no[:, :], [[1, E]], base=-E, channel_multiplier=0,
                      allow_small_or_imprecise_dtypes=True).then_inc(consts, 1)
            pool.iota(dump[:, :, :], [[N, TOPK], [TOK, NT]], base=SLOTS, channel_multiplier=1,
                      allow_small_or_imprecise_dtypes=True).then_inc(consts, 1)
            pool.wait_ge(consts, 3)
            pool.affine_select(out=before[:, :], in_=ones[:, :], compare_op=ALU.is_gt, fill=0.0, base=0,
                               pattern=[[1, TOK]], channel_multiplier=-1).then_inc(consts, 1)
            pool.wait_ge(places_ready, 1)
            for k in range(TOPK):
                for t in range(NT):
                    pool.indirect_dma_start(
                        out=slots_in[:, :],
                        out_offset=bass.IndirectOffsetOnAxis(ap=scatter_at[:, k * NT + t:k * NT + t + 1], axis=0),
                        in_=xn2[:, t, :], in_offset=None).then_inc(scattered, 16)
            pool.wait_ge(scattered, 16 * TOPK * NT)

        @block.scalar
        def _(act):
            for i in range(2):
                act.wait_ge(var_ready, i + 1)
                act.activation(root[:, i, :], root_in[:, i, :], ACT.Sqrt).then_inc(root_ready, 1)
            for u, (g, c) in enumerate(units):
                n = TOK * len(tile_parts(g))
                act.wait_ge(turned, u + 1)
                act.activation(xn2_t[:, c, 500 * g:500 * g + n], bank[u % 4][:, 0:n], ACT.Copy).then_inc(copied, 1)
            act.wait_ge(centred, 1)
            act.activation(prob[:, :, :], prob[:, :, :], ACT.Exp).then_inc(exp_done, 1)
            for t in range(NT):
                act.wait_ge(turned, len(units) + t + 1)
                act.activation(select_t[:, TOK * t:TOK * (t + 1)], bank[t % 4][0:E, 0:TOK], ACT.Copy).then_inc(copied, 1)

        @block.vector
        def _(dve):
            link = chain(dve, dve_step)

            def rows_rstd(i):
                for t in range(NT):
                    ins = dve.bn_aggr(mean_var[:, i, t, :], (hidden_stats, x1_stats)[i][:, t, :])
                link(ins)
                dve.tensor_scalar(root_in[:, i, :], mean_var[:, i, :, 1], EPS, None, ALU.add).then_inc(var_ready, 1)
                dve.wait_ge(root_ready, i + 1)
                inverse_root(dve, link, root_in[:, i, :], root[:, i, :], scratch[:, i, :], rstd[:, i, :])

            rows_rstd(0)
            dve.wait_ge(gamma_loaded, 16)
            for t in range(NT):
                if t % 2 == 0:
                    dve.wait_ge(loaded[t // 2], 16)
                ins = dve.scalar_tensor_tensor(row[:, t, :], row[:, t, :], mean_var[:, 0, t, 0:1], gamma_row[:, :],
                                               ALU.subtract, ALU.mult)
            link(ins)
            dve.wait_ge(base_loaded, 16)
            for t in range(NT):
                ins = dve.scalar_tensor_tensor(x1[:, t, :], row[:, t, :], rstd[:, 0, t:t + 1], x1[:, t, :], ALU.mult, ALU.add)
            link(ins)
            for t in range(NT):
                ins = dve.bn_stats(x1_stats[:, t, :], x1[:, t, :])
            link(ins)
            rows_rstd(1)
            for t in range(NT):
                dve.tensor_scalar(xn2[:, t, :], x1[:, t, :], mean_var[:, 1, t, 0:1], rstd[:, 1, t:t + 1],
                                  ALU.subtract, ALU.mult).then_inc(row_ready, 1)

            dve.wait_ge(gated, 1)
            dve.wait_ge(consts, 4)
            logits = logit[0:TOK, 0:NT * E].rearrange("p (t e) -> p t e", e=E)
            link(dve.tensor_reduce(norm[:, :], logits, AX.X, ALU.max))
            dve.tensor_tensor(prob[:, :, :], logits, over_experts(norm[:, :]), ALU.subtract).then_inc(centred, 1)
            dve.wait_ge(exp_done, 1)
            link(dve.tensor_reduce(norm[:, :], prob[:, :, :], AX.X, ALU.add))
            link(dve.reciprocal(norm[:, :], norm[:, :]))
            link(dve.tensor_tensor(prob[:, :, :], prob[:, :, :], over_experts(norm[:, :]), ALU.mult))
            number = expert_no[:, :].unsqueeze(1).to_broadcast([TOK, NT, E])
            for k in range(TOPK):
                source = (prob, left)[k]
                link(dve.tensor_reduce(best[:, k, :], source[:, :, :], AX.X, ALU.max))
                link(dve.tensor_tensor(same[:, :, :], source[:, :, :], over_experts(best[:, k, :]), ALU.is_equal))
                link(dve.tensor_tensor(same[:, :, :], same[:, :, :], number, ALU.mult))
                link(dve.tensor_reduce(expert[:, k, :], same[:, :, :], AX.X, ALU.min))
                link(dve.tensor_tensor(hot[:, k, :, :], over_experts(expert[:, k, :]), number, ALU.is_equal))
                if k == 0:
                    link(dve.scalar_tensor_tensor(left[:, :, :], hot[:, 0, :, :], -2.0, prob[:, :, :], ALU.mult, ALU.add))
            dve.tensor_tensor(taken[:, :, :], hot[:, 0, :, :], hot[:, 1, :, :], ALU.add).then_inc(taken_ready, 1)
            link(dve.tensor_tensor(norm[:, :], best[:, 0, :], best[:, 1, :], ALU.add))
            link(dve.tensor_scalar(norm[:, :], norm[:, :], 1e-9, None, ALU.max))
            link(dve.reciprocal(norm[:, :], norm[:, :]))
            dve.wait_ge(ranked, 1)
            ranks = rank_bank[0:TOK, 0:NT * E].rearrange("p (t e) -> p t e", e=E)
            for k in range(TOPK):
                link(dve.tensor_tensor(same[:, :, :], hot[:, k, :, :], ranks, ALU.mult))
                link(dve.tensor_reduce(rank[:, k, :], same[:, :, :], AX.X, ALU.add))
            dve.tensor_scalar(keep[:, :, :], rank[:, :, :], float(CAP), None, ALU.is_lt)
            link(dve.scalar_tensor_tensor(dest[:, :, :], expert[:, :, :], float(CAP), rank[:, :, :], ALU.mult, ALU.add))
            link(dve.tensor_scalar(dest[:, :, :], dest[:, :, :], float(E * CAP), None, ALU.add))
            link(dve.tensor_tensor(place[:, :, :], dest[:, :, :], dump[:, :, :], ALU.subtract))
            link(dve.tensor_tensor(place[:, :, :], place[:, :, :], keep[:, :, :], ALU.mult))
            link(dve.tensor_tensor(place[:, :, :], place[:, :, :], dump[:, :, :], ALU.add))
            dve.tensor_copy(scatter_at[:, :], place[:, :, :].rearrange("p k t -> p (k t)")).then_inc(places_ready, 1)
            dve.wait_ge(places_ready, 1)
            link(dve.scalar_tensor_tensor(place[:, :, :], dest[:, :, :], -float(SLOTS - 1), keep[:, :, :], ALU.add, ALU.mult))
            link(dve.tensor_scalar(place[:, :, :], place[:, :, :], float(SLOTS - 1), None, ALU.add))
            link(dve.tensor_copy(gather_at[:, :], place[:, :, :].rearrange("p k t -> p (k t)")))
            link(dve.tensor_tensor(weight[:, :, :], best[:, :, :], norm[:, :].unsqueeze(1).to_broadcast([TOK, TOPK, NT]), ALU.mult))
            link(dve.tensor_tensor(weight[:, :, :], weight[:, :, :], keep[:, :, :], ALU.mult))
            link(dve.tensor_tensor(norm[:, :], weight[:, 0, :], weight[:, 1, :], ALU.add))
            dve.tensor_scalar(none[:, :], norm[:, :], 1e-12, None, ALU.is_le)
            link(dve.tensor_scalar(some[:, :], norm[:, :], 1e-12, None, ALU.is_gt))
            for k in range(TOPK):
                link(dve.tensor_tensor(hot[:, k, :, :], hot[:, k, :, :], over_experts(weight[:, k, :]), ALU.mult))
            dve.tensor_tensor(same[:, :, :], hot[:, 0, :, :], hot[:, 1, :, :], ALU.add).then_inc(select_ready, 1)

        @block.tensor
        def _(pe):
            pe.wait_ge(gate_loaded, 16)

            def logits(g):
                pe.wait_ge(copied, DC * (g + 1))
                for t in tile_parts(g):
                    for c in range(DC):
                        ins = pe.matmul(logit[0:TOK, E * t:E * (t + 1)], xn2_t[:, c, TOK * t:TOK * (t + 1)], gate_w[:, c, :],
                                        start=(c == 0), stop=(c == DC - 1))
                return ins

            for u, (g, c) in enumerate(units):
                if u >= 4:
                    pe.wait_ge(copied, u - 3)
                pe.wait_ge(row_ready, tile_parts(g)[-1] + 1)
                for i, t in enumerate(tile_parts(g)):
                    ins = pe.transpose(bank[u % 4][:, TOK * i:TOK * (i + 1)], xn2[:, t, P * c:P * (c + 1)],
                                       ident[0:TOK, 0:TOK])
                ins.then_inc(turned, 1)
                if c == DC - 1 and g > 0:
                    logits(g - 1)
            logits(2).then_inc(gated, 1)
            pe.wait_ge(taken_ready, 1)
            for t in range(NT):
                for s in range(t + 1):
                    ins = pe.matmul(rank_bank[0:TOK, E * t:E * (t + 1)], (before if s == t else ones)[:, :], taken[:, s, :],
                                    start=(s == 0), stop=(s == t))
            ins.then_inc(ranked, 1)
            pe.wait_ge(select_ready, 1)
            for t in range(NT):
                if t >= 4:
                    pe.wait_ge(copied, len(units) + t - 3)
                pe.transpose(bank[t % 4][0:E, 0:TOK], same[:, t, :], ident[0:TOK, 0:TOK]).then_inc(turned, 1)


def stage_experts(nc, slots_in, slots_out, inputs, ident):
    E, RING = EXPERTS, inputs.RING
    with ExitStack() as ctx:
        b = Buffers(nc, ctx)
        up, down = inputs.weights
        up_loaded, down_loaded = inputs.loaded
        rows = [b.sb(f"e_rows{k}", [CAP, D]) for k in range(RING)]
        rows_t = [b.sb(f"e_rows_t{i}", [P, DC, CAP]) for i in range(2)]
        mid = [b.sb(f"e_mid{i}", [P, DC, CAP]) for i in range(2)]
        mid_t = [[b.sb(f"e_mid_t{i}_{k}", [P, DC, CAP], F32R) for k in ("hi", "lo")] for i in range(2)]
        down_t = [[b.sb(f"e_down{i}_{k}", [P, DC, D], F32R) for k in ("hi", "lo")] for i in range(2)]
        out = [b.sb(f"e_out{i}", [CAP, D]) for i in range(2)]
        bias_t = b.sb("e_bias_t", [P, DC, E])
        turn_bank = [b.ps(f"e_turn_bank{i}", [P, 512]) for i in range(2)]
        mid_bank = [b.ps(f"e_mid_bank{i}", [P, 512]) for i in range(2)]
        out_bank = [b.ps(f"e_out_bank{i}", [P, 512]) for i in range(2)]
        bias_turned = b.sem("e_bias_turned")
        bias_ready = b.sem("e_bias_ready")
        rows_loaded = [b.sem(f"e_rows_loaded{k}") for k in range(RING)]
        stored = [b.sem(f"e_stored{i}") for i in range(2)]
        turned = b.sem("e_turned")
        rows_ready = b.sem("e_rows_ready")
        mid_done = b.sem("e_mid_done")
        relu_done = b.sem("e_relu_done")
        mid_hi = b.sem("e_mid_hi")
        mid_ready = b.sem("e_mid_ready")
        down_hi = b.sem("e_down_hi")
        down_ready = b.sem("e_down_ready")
        out_done = b.sem("e_out_done")
        out_ready = b.sem("e_out_ready")
        block = ctx.enter_context(nc.Block())


        @block.sync
        def _(sp):
            def load_rows(e, k):
                sp.dma_start(rows[k][:, :], slots_in[bass.ds(e * CAP, CAP), :]).then_inc(rows_loaded[k], 16)

            for k in range(RING):
                load_rows(k, k)
            with sp.Fori(0, E // RING - 1) as i:
                for k in range(RING):
                    e = RING * i + k
                    sp.wait_ge(turned, e + 1)
                    load_rows(e + RING, k)
                    sp.wait_ge(mid_done, e + 1)
                    inputs.load(sp, 0, e + RING, k)
                    sp.wait_ge(down_ready, e + 1)
                    inputs.load(sp, 1, e + RING, k)

        @block.scalar
        def _(act):
            def rows_out(e, k):
                act.wait_ge(turned, e + 1)
                act.activation(rows_t[k % 2][:, :, :].rearrange("p c n -> p (c n)"), turn_bank[k % 2][:, 0:DC * CAP],
                               ACT.Copy).then_inc(rows_ready, 1)

            def mid_high(i, k):
                act.wait_ge(relu_done, RING * i + (k + 1))
                act.activation(mid_t[k % 2][0][:, :, :], mid[k % 2][:, :, :], ACT.Copy).then_inc(mid_hi, 1)

            def down_high(i, k):
                i, k = i + k // RING, k % RING
                act.wait_ge(down_loaded[k], 16 * i + 16)
                act.wait_ge(out_done, RING * i + k + 1)
                for c in range(DC):
                    act.activation(down_t[k % 2][0][:, c, :], down[k][:, c, :], ACT.Copy).then_inc(down_hi, 1)

            act.sem_inc(stored[0], 16)
            act.sem_inc(stored[1], 16)
            down_high(0, 0)
            rows_out(0, 0)
            rows_out(1, 1)
            down_high(0, 1)
            mid_high(0, 0)

            def expert(i, k, last):
                e = RING * i + k
                if not (last and k >= RING - 2):
                    rows_out(e + 2, k)
                if not (last and k == RING - 1):
                    mid_high(i, k + 1)
                act.wait_ge(out_done, e + 3)
                act.wait_ge(stored[k % 2], 16 * (RING // 2) * i + 16 * (k // 2 + 1))
                act.activation(out[k % 2][:, :], out_bank[k % 2][0:CAP, :], ACT.Copy).then_inc(out_ready, 1)
                act.wait_ge(out_ready, e + 3)
                act.dma_start(slots_out[bass.ds(e * CAP, CAP), :], out[k % 2][:, :]).then_inc(stored[k % 2], 16)
                if not (last and k >= RING - 2):
                    down_high(i, k + 2)

            with act.Fori(0, E // RING - 1) as i:
                for k in range(RING):
                    expert(i, k, False)
            for k in range(RING):
                expert(E // RING - 1, k, True)
            for k in range(2):
                act.wait_ge(stored[k], 16 * (E // 2 + 1))

        @block.vector
        def _(dve):
            dve.wait_ge(bias_turned, 1)
            dve.tensor_copy(bias_t[:, :, :].rearrange("p c e -> p (c e)"), out_bank[1][:, 0:DC * E]).then_inc(bias_ready, 1)
            dve.wait_ge(bias_ready, 1)

            def down_low(i, k):
                i, k = i + k // RING, k % RING
                for c in range(DC):
                    dve.wait_ge(down_hi, DC * RING * i + (DC * k + c + 1))
                    ins = dve.tensor_tensor(down_t[k % 2][1][:, c, :], down[k][:, c, :], down_t[k % 2][0][:, c, :].bitcast(F32),
                                            ALU.subtract)
                ins.then_inc(down_ready, 1)

            def mid_parts(i, k):
                i, k = i + k // RING, k % RING
                e = RING * i + k
                dve.wait_ge(mid_done, e + 1)
                for c in range(DC):
                    ins = dve.tensor_scalar(mid[k % 2][:, c, :], mid_bank[k % 2][:, CAP * c:CAP * (c + 1)],
                                            bias_t[:, c, bass.ds(e, 1)], 0.0, ALU.add, ALU.max)
                ins.then_inc(relu_done, 1)
                dve.wait_ge(mid_hi, e + 1)
                dve.tensor_tensor(mid_t[k % 2][1][:, :, :], mid[k % 2][:, :, :], mid_t[k % 2][0][:, :, :].bitcast(F32),
                                  ALU.subtract).then_inc(mid_ready, 1)

            def expert(i, k, last):
                if not (last and k == RING - 1):
                    mid_parts(i, k + 1)
                if not (last and k >= RING - 2):
                    down_low(i, k + 2)

            down_low(0, 0)
            down_low(0, 1)
            mid_parts(0, 0)
            with dve.Fori(0, E // RING - 1) as i:
                for k in range(RING):
                    expert(i, k, False)
            for k in range(RING):
                expert(E // RING - 1, k, True)

        @block.tensor
        def _(pe):
            pe.wait_ge(inputs.bias_loaded, 16)
            for c in range(DC):
                ins = pe.transpose(out_bank[1][:, E * c:E * (c + 1)], inputs.bias_in[:, P * c:P * (c + 1)], ident[0:E, 0:E])
            ins.then_inc(bias_turned, 1)

            def turn(i, k):
                i, k = i + k // RING, k % RING
                pe.wait_ge(rows_loaded[k], 16 * i + 16)
                for c in range(DC):
                    ins = pe.transpose(turn_bank[k % 2][:, CAP * c:CAP * (c + 1)], rows[k][:, P * c:P * (c + 1)],
                                       ident[0:CAP, 0:CAP])
                ins.then_inc(turned, 1)

            def product_up(i, k):
                i, k = i + k // RING, k % RING
                pe.wait_ge(rows_ready, RING * i + (k + 1))
                pe.wait_ge(up_loaded[k], 16 * i + 16)
                for h in range(DC):
                    for c in range(DC):
                        ins = pe.matmul(mid_bank[k % 2][:, CAP * h:CAP * (h + 1)], up[k][:, c, P * h:P * (h + 1)],
                                        rows_t[k % 2][:, c, :], start=(c == 0), stop=(c == DC - 1))
                ins.then_inc(mid_done, 1)

            def product_down(i, k):
                e = RING * i + k
                pe.wait_ge(mid_ready, e + 1)
                pe.wait_ge(down_ready, e + 1)
                pe.wait_ge(out_ready, e + 1)
                for h in range(DC):
                    for n, (x, y) in enumerate(PARTS):
                        ins = pe.matmul(out_bank[k % 2][0:CAP, :], mid_t[k % 2][x][:, h, :], down_t[k % 2][y][:, h, :],
                                        start=(h == 0 and n == 0), stop=(h == DC - 1 and n == 2))
                ins.then_inc(out_done, 1)

            pe.sem_inc(out_ready, 2)
            pe.sem_inc(out_done, 2)
            turn(0, 0)
            turn(0, 1)
            product_up(0, 0)
            pe.wait_ge(bias_ready, 1)
            with pe.Fori(0, E // RING - 1) as i:
                for k in range(RING):
                    product_up(i, k + 1)
                    turn(i, k + 2)
                    product_down(i, k)
            for k in range(RING):
                if k < RING - 1:
                    product_up(E // RING - 1, k + 1)
                if k < RING - 2:
                    turn(E // RING - 1, k + 2)
                product_down(E // RING - 1, k)


def stage_combine(nc, slots_out, b2, x1, xn2, route, out):
    _, gather_at, weight, select_t, some, none = route
    with ExitStack() as ctx:
        b = Buffers(nc, ctx)
        got = [b.sb(f"o_got{k}", [TOK, NT, D]) for k in range(TOPK)]
        bias = b.sb("o_bias", [EXPERTS, D])
        bank = [b.ps(f"o_bank{i}", [P, 512]) for i in range(4)]
        bias_loaded = b.sem("o_bias_loaded")
        gathered = [b.sem(f"o_gathered{t}") for t in range(NT)]
        biased = b.sem("o_biased")
        first = b.sem("o_first")
        both = b.sem("o_both")
        kept = b.sem("o_kept")
        row_ready = b.sem("o_row_ready")
        stored = b.sem("o_stored")
        block = ctx.enter_context(nc.Block())

        @block.sync
        def _(sp):
            sp.dma_start(bias[:, :], b2).then_inc(bias_loaded, 16)
            for t in range(NT):
                sp.wait_ge(row_ready, t + 1)
                sp.dma_start(out[TOK * t:TOK * (t + 1), :], x1[:, t, :]).then_inc(stored, 16)
            sp.wait_ge(stored, 16 * NT)

        @block.gpsimd
        def _(pool):
            for t in range(NT):
                for k in range(TOPK):
                    pool.indirect_dma_start(
                        out=got[k][:, t, :], out_offset=None, in_=slots_out[:, :],
                        in_offset=bass.IndirectOffsetOnAxis(ap=gather_at[:, k * NT + t:k * NT + t + 1], axis=0)
                    ).then_inc(gathered[t], 16)

        @block.tensor
        def _(pe):
            pe.wait_ge(bias_loaded, 16)
            for t in range(NT):
                if t >= 4:
                    pe.wait_ge(first, t - 3)
                pe.matmul(bank[t % 4][0:TOK, :], select_t[:, TOK * t:TOK * (t + 1)], bias[:, :], start=True,
                          stop=True).then_inc(biased, 1)

        @block.vector
        def _(dve):
            for t in range(NT):
                dve.scalar_tensor_tensor(x1[:, t, :], xn2[:, t, :], none[:, t:t + 1], x1[:, t, :], ALU.mult,
                                         ALU.add).then_inc(kept, 1)
            for t in range(NT):
                dve.wait_ge(gathered[t], 32)
                dve.wait_ge(biased, t + 1)
                dve.scalar_tensor_tensor(got[0][:, t, :], got[0][:, t, :], weight[:, 0, t:t + 1], bank[t % 4][0:TOK, :],
                                         ALU.mult, ALU.add).then_inc(first, 1)
                dve.wait_ge(first, t + 1)
                dve.scalar_tensor_tensor(got[1][:, t, :], got[1][:, t, :], weight[:, 1, t:t + 1], got[0][:, t, :],
                                         ALU.mult, ALU.add).then_inc(both, 1)
                dve.wait_ge(both, t + 1)
                dve.wait_ge(kept, t + 1)
                dve.scalar_tensor_tensor(x1[:, t, :], got[1][:, t, :], some[:, t:t + 1], x1[:, t, :], ALU.mult,
                                         ALU.add).then_inc(row_ready, 1)


def gps_layer(nc, x, src, dst, gnn, mix, ffn, out):
    counts = nc.dram_tensor("counts_dram", (N, NS), U16, kind="Internal").ap()
    hidden = nc.dram_tensor("hidden_dram", (N, D), F32, kind="Internal").ap()
    base = nc.dram_tensor("base_dram", (N, D), F32, kind="Internal").ap()
    mixed = nc.dram_tensor("mixed_dram", (N, D), F32, kind="Internal").ap()
    slots_in = nc.dram_tensor("slots_in_dram", (SLOTS + TOPK * N, D), F32, kind="Internal").ap()
    slots_out = nc.dram_tensor("slots_out_dram", (SLOTS, D), F32, kind="Internal").ap()
    Buffers.used.clear()
    with ExitStack() as ctx:
        b = Buffers(nc, ctx)
        ident = b.sb("ident", [P, P])
        hidden_stats = b.sb("hidden_stats", [TOK, NT, 6])
        with ExitStack() as nodes:
            b_nodes = Buffers(nc, nodes)
            xnT = [b_nodes.sb(f"xnT_{k}", [P, DC, NS], F32R) for k in ("hi", "lo")]
            mixed_norm = b_nodes.sb("mixed_norm", [TOK, 2, NT])
            with ExitStack() as rows:
                xrow = Buffers(nc, rows).sb("xrow", [TOK, NT, D])
                stage_norm(nc, x, ident, xnT[0], xnT[1], xrow)
                stage_mix(nc, xrow, ident, mix["w_qkv"], mix["w_out"], mix["norm_gamma"], mixed, mixed_norm)
            fold_bias = b_nodes.sb("fold_bias", [P, HEADS, DC])
            row_shift = b_nodes.sb("row_shift", [TOK, NT, HEADS])
            value_bias = b_nodes.sb("value_bias", [TOK, HEADS, D])
            Buffers.reset(nc)
            folded = FoldedWeights(nc, b_nodes)
            with ExitStack() as weights:
                fold_inputs = FoldInputs(Buffers(nc, weights), gnn, folded)
                stage_count(nc, src, dst, ident, counts, fold_inputs, x, mixed, mixed_norm, mix["out_gamma"], gnn["beta"],
                            base, slots_in)
                stage_fold(nc, fold_inputs, folded, ident, xnT, fold_bias, row_shift, value_bias, hidden)
            stage_attend(nc, xnT, counts, folded, fold_bias, row_shift, value_bias, ident, hidden, hidden_stats)
        x1 = b.sb("x1", [TOK, NT, D])
        xn2 = b.sb("xn2", [TOK, NT, D])
        route = (b.sb("scatter_at", [TOK, TOPK * NT], U32), b.sb("gather_at", [TOK, TOPK * NT], U32),
                 b.sb("weight", [TOK, TOPK, NT]), b.sb("select_t", [EXPERTS, N]),
                 b.sb("some", [TOK, NT]), b.sb("none", [TOK, NT]))
        with ExitStack() as weights:
            expert_inputs = ExpertInputs(Buffers(nc, weights), ffn["W1"], ffn["b1"], ffn["W2"])
            stage_join(nc, hidden, hidden_stats, base, gnn["gamma"], ffn["Wg"], ident, x1, xn2, route, slots_in,
                       expert_inputs)
            stage_experts(nc, slots_in, slots_out, expert_inputs, ident)
        stage_combine(nc, slots_out, ffn["b2"], x1, xn2, route, out)


def kernel(**inputs):
    import concourse.bacc as bacc
    from concourse.bass_utils import run_bass_kernel_spmd

    nc = bacc.Bacc("TRN2", target_bir_lowering=False, num_devices=1)
    arrays, aps = {}, {}
    for name, a in inputs.items():
        arrays[f"in_{name}"] = np.ascontiguousarray(a)
        aps[name] = nc.dram_tensor(f"in_{name}", a.shape, mybir.dt.from_np(a.dtype), kind="ExternalInput").ap()
    out = nc.dram_tensor("out", (N, D), F32, kind="ExternalOutput").ap()

    def part(prefix):
        return {name[len(prefix):]: ap for name, ap in aps.items() if name.startswith(prefix)}

    gps_layer(nc, aps["x"], aps["src"], aps["dst"], part("L0_gnn_"), part("L0_mix_"), part("L0_ffn_"), out)
    result = run_bass_kernel_spmd(nc, [arrays], core_ids=[0])
    return result.results[0]["out"]
```
